# Optimizing a Trainium2 kernel written in Bass

```python
import numpy as np
import jax
import jax.numpy as jnp

def _softmax(x, axis=-1):
    return jax.nn.softmax(x, axis=axis)

def _gelu(x):
    return jax.nn.gelu(x, approximate=True)

def _silu(x):
    return jax.nn.silu(x)

def _sigmoid(x):
    return jax.nn.sigmoid(x)

def _layernorm(x, axis=-1, eps=1e-05):
    m = jnp.mean(x, axis=axis, keepdims=True)
    v = jnp.var(x, axis=axis, keepdims=True)
    return (x - m) / jnp.sqrt(v + eps)

def _scatter_add(tgt, idx, src, axis=0):
    return tgt.at[idx].add(src)

def _segment_sum(src, seg, n):
    return jax.ops.segment_sum(src, seg, n)
kernel_name = 'mk_gps_d2_gnn_r16_2b2e33'

def setup_inputs(seed: int=0):
    np.random.seed(seed)
    _w = jnp.asarray

    def _rec_inputs():
        import jax
        import jax.numpy as jnp
        _gk = jax.random.key(seed)
        x = -0.0003713 + 1 * jax.random.normal(jax.random.fold_in(_gk, 1), (3125, 256), jnp.float32)
        src = jax.random.randint(jax.random.fold_in(_gk, 2), (100000,), 0, 3125, jnp.int32)
        dst = jax.random.randint(jax.random.fold_in(_gk, 3), (100000,), 0, 3125, jnp.int32)
        _o = jnp.argsort(dst, stable=True)
        src = src[_o]
        dst = dst[_o]
        edge_attr_64 = -9.77346e-05 + 0.999888 * jax.random.normal(jax.random.fold_in(_gk, 12), (100000, 64), jnp.float32)
        return (x, src, dst, edge_attr_64)
    x, src, dst, edge_attr_64 = _rec_inputs()

    def _L0_gnn_setup():
        import jax, jax.numpy as jnp
        import numpy as np
        N, E, D, H, FE = (3125, 50000, 256, 8, 64)
        HD = D // H
        key = jax.random.key(seed)
        ks = jax.random.split(key, 14)
        sD = 1.0 / np.sqrt(D)
        sF = 1.0 / np.sqrt(FE)
        return {'h': jax.random.normal(ks[0], (N, D), jnp.float32), 'efeat': jax.random.normal(ks[1], (E, FE), jnp.float32), 'src': jax.random.randint(ks[2], (E,), 0, N), 'dst': jax.random.randint(ks[3], (E,), 0, N), 'Wq': jax.random.normal(ks[4], (D, D), jnp.float32) * sD, 'Wk': jax.random.normal(ks[5], (D, D), jnp.float32) * sD, 'Wv': jax.random.normal(ks[6], (D, D), jnp.float32) * sD, 'W1': jax.random.normal(ks[7], (FE, D), jnp.float32) * sF, 'b1': jnp.zeros((D,), jnp.float32), 'W2': jax.random.normal(ks[8], (D, H), jnp.float32) * sD, 'b2': jnp.zeros((H,), jnp.float32), 'Wo': jax.random.normal(ks[9], (D, D), jnp.float32) * sD, 'bo': jnp.zeros((D,), jnp.float32)}
    _L0_gnn_all = _L0_gnn_setup()
    _L0_gnn_in = {k: v for k, v in _L0_gnn_all.items() if k in ('Wq', 'Wk', 'Wv', 'W1', 'b1', 'W2', 'b2', 'Wo', 'bo')}
    del _L0_gnn_all

    def _L0_mix_setup():
        import jax, jax.numpy as jnp
        import numpy as np
        MIDC = 256
        HEADS = 8
        HEADC = MIDC // HEADS
        EPS = 1e-05

        def _ln(x, gamma, beta):
            mu = jnp.mean(x, axis=-1, keepdims=True)
            var = jnp.var(x, axis=-1, keepdims=True)
            return (x - mu) * jax.lax.rsqrt(var + EPS) * gamma + beta
        key = jax.random.key(seed)
        ks = jax.random.split(key, 8)
        B, HW, C = (8, 256, MIDC)
        s = 1.0 / np.sqrt(C)
        return {'x': jax.random.normal(ks[0], (B, HW, C), jnp.float32), 'w_qkv': jax.random.normal(ks[1], (C, 3 * C), jnp.float32) * s, 'b_qkv': jnp.zeros((3 * C,), jnp.float32), 'kln_g': jnp.ones((HEADC,), jnp.float32), 'kln_b': jnp.zeros((HEADC,), jnp.float32), 'vln_g': jnp.ones((HEADC,), jnp.float32), 'vln_b': jnp.zeros((HEADC,), jnp.float32), 'w1': jax.random.normal(ks[2], (C, C), jnp.float32) * s, 'b1': jnp.zeros((C,), jnp.float32), 'w2': jax.random.normal(ks[3], (C, C), jnp.float32) * s, 'b2': jnp.zeros((C,), jnp.float32)}
    _L0_mix_all = _L0_mix_setup()
    _L0_mix_in = {k: v for k, v in _L0_mix_all.items() if k in ('w_qkv', 'b_qkv', 'kln_g', 'kln_b', 'vln_g', 'vln_b', 'w1', 'b1', 'w2', 'b2')}
    del _L0_mix_all

    def _L0_ffn_setup():
        import math
        import jax, jax.numpy as jnp
        import numpy as np
        CAPACITY_FACTOR = 1.25
        key = jax.random.key(seed)
        ks = jax.random.split(key, 5)
        B, L, D, F, E = (8, 512, 256, 1024, 8)
        h = jax.random.normal(ks[0], (B, L, D), dtype=jnp.float32)
        gate_w = jax.random.normal(ks[1], (D, E), dtype=jnp.float32) * 0.02
        gate_b = jnp.zeros((E,), dtype=jnp.float32)
        w1 = jax.random.normal(ks[2], (E, D, F), dtype=jnp.float32) * (1.0 / math.sqrt(D))
        b1 = jnp.zeros((E, F), dtype=jnp.float32)
        w2 = jax.random.normal(ks[3], (E, F, D), dtype=jnp.float32) * (1.0 / math.sqrt(F))
        b2 = jnp.zeros((E, D), dtype=jnp.float32)
        return {'h': h, 'gate_w': gate_w, 'gate_b': gate_b, 'w1': w1, 'b1': b1, 'w2': w2, 'b2': b2}
    _L0_ffn_all = _L0_ffn_setup()
    _L0_ffn_in = {k: v for k, v in _L0_ffn_all.items() if k in ('gate_w', 'gate_b', 'w1', 'b1', 'w2', 'b2')}
    del _L0_ffn_all

    def _L1_gnn_setup():
        import jax, jax.numpy as jnp
        import numpy as np
        N_NODES = 25000
        N_EDGES = 25000
        D = 256
        key = jax.random.key(seed)
        k1, k2, k3, k4, k5 = jax.random.split(key, 5)
        feat = jax.random.normal(k1, (N_NODES, D), dtype=jnp.float32)
        src = jax.random.randint(k2, (N_EDGES,), 0, N_NODES, dtype=jnp.int32)
        dst = jax.random.randint(k3, (N_EDGES,), 0, N_NODES, dtype=jnp.int32)
        a = float(np.sqrt(6.0 / (D + D)))
        W1 = jax.random.uniform(k4, (D, D), minval=-a, maxval=a, dtype=jnp.float32)
        W2 = jax.random.uniform(k5, (D, D), minval=-a, maxval=a, dtype=jnp.float32)
        b = jnp.zeros((D,), dtype=jnp.float32)
        return {'feat': feat, 'W1': W1, 'W2': W2, 'b': b, 'src': src, 'dst': dst}
    _L1_gnn_all = _L1_gnn_setup()
    _L1_gnn_in = {k: v for k, v in _L1_gnn_all.items() if k in ('W1', 'W2', 'b')}
    del _L1_gnn_all

    def _L1_mix_setup():
        import jax, jax.numpy as jnp
        import numpy as np
        N, F, C, H = (32, 256, 256, 8)
        D = C // H
        EPS_ATTN = 1e-06
        EPS_LN = 1e-05

        def layer_norm(x, g, b):
            mu = jnp.mean(x, axis=-1, keepdims=True)
            var = jnp.var(x, axis=-1, keepdims=True)
            return (x - mu) * jax.lax.rsqrt(var + EPS_LN) * g + b
        key = jax.random.key(seed)
        ks = jax.random.split(key, 8)
        s = 1.0 / np.sqrt(C)
        return {'x': jax.random.normal(ks[0], (N, F, C), jnp.float32), 'Wqkv': jax.random.uniform(ks[1], (3 * C, C), jnp.float32, -s, s), 'ln1_g': jnp.ones((C,), jnp.float32), 'ln1_b': jnp.zeros((C,), jnp.float32), 'W1': jax.random.uniform(ks[2], (C, C), jnp.float32, -s, s), 'b1': jax.random.uniform(ks[3], (C,), jnp.float32, -s, s), 'W2': jax.random.uniform(ks[4], (C, C), jnp.float32, -s, s), 'b2': jax.random.uniform(ks[5], (C,), jnp.float32, -s, s), 'ln2_g': jnp.ones((C,), jnp.float32), 'ln2_b': jnp.zeros((C,), jnp.float32)}
    _L1_mix_all = _L1_mix_setup()
    _L1_mix_in = {k: v for k, v in _L1_mix_all.items() if k in ('Wqkv', 'ln1_g', 'ln1_b', 'W1', 'b1', 'W2', 'b2', 'ln2_g', 'ln2_b')}
    del _L1_mix_all

    def _L1_ffn_setup():
        import jax, jax.numpy as jnp
        import numpy as np
        B, S, D = (8, 256, 256)
        H = 4 * D
        CAPACITY = 0.5
        key = jax.random.key(seed)
        ks = jax.random.split(key, 6)
        x = jax.random.normal(ks[0], (B, S, D), dtype=jnp.float32)
        attention_mask = jnp.zeros((B, 1, 1, S), dtype=jnp.float32)
        wr = jax.random.normal(ks[1], (D, 1), dtype=jnp.float32) * 0.02
        br = jnp.zeros((1,), dtype=jnp.float32)
        w1 = jax.random.normal(ks[2], (D, H), dtype=jnp.float32) * 0.02
        b1 = jnp.zeros((H,), dtype=jnp.float32)
        w2 = jax.random.normal(ks[3], (H, D), dtype=jnp.float32) * 0.02
        b2 = jnp.zeros((D,), dtype=jnp.float32)
        return {'x': x, 'attention_mask': attention_mask, 'wr': wr, 'br': br, 'w1': w1, 'b1': b1, 'w2': w2, 'b2': b2}
    _L1_ffn_all = _L1_ffn_setup()
    _L1_ffn_in = {k: v for k, v in _L1_ffn_all.items() if k in ('attention_mask', 'wr', 'br', 'w1', 'b1', 'w2', 'b2')}
    del _L1_ffn_all
    return {'x': x, 'src': src, 'dst': dst, 'edge_attr_64': edge_attr_64, 'L0_gnn_Wq': _L0_gnn_in['Wq'], 'L0_gnn_Wk': _L0_gnn_in['Wk'], 'L0_gnn_Wv': _L0_gnn_in['Wv'], 'L0_gnn_W1': _L0_gnn_in['W1'], 'L0_gnn_b1': _L0_gnn_in['b1'], 'L0_gnn_W2': _L0_gnn_in['W2'], 'L0_gnn_b2': _L0_gnn_in['b2'], 'L0_gnn_Wo': _L0_gnn_in['Wo'], 'L0_gnn_bo': _L0_gnn_in['bo'], 'L0_mix_w_qkv': _L0_mix_in['w_qkv'], 'L0_mix_b_qkv': _L0_mix_in['b_qkv'], 'L0_mix_kln_g': _L0_mix_in['kln_g'], 'L0_mix_kln_b': _L0_mix_in['kln_b'], 'L0_mix_vln_g': _L0_mix_in['vln_g'], 'L0_mix_vln_b': _L0_mix_in['vln_b'], 'L0_mix_w1': _L0_mix_in['w1'], 'L0_mix_b1': _L0_mix_in['b1'], 'L0_mix_w2': _L0_mix_in['w2'], 'L0_mix_b2': _L0_mix_in['b2'], 'L0_ffn_gate_w': _L0_ffn_in['gate_w'], 'L0_ffn_gate_b': _L0_ffn_in['gate_b'], 'L0_ffn_w1': _L0_ffn_in['w1'], 'L0_ffn_b1': _L0_ffn_in['b1'], 'L0_ffn_w2': _L0_ffn_in['w2'], 'L0_ffn_b2': _L0_ffn_in['b2'], 'L1_gnn_W1': _L1_gnn_in['W1'], 'L1_gnn_W2': _L1_gnn_in['W2'], 'L1_gnn_b': _L1_gnn_in['b'], 'L1_mix_Wqkv': _L1_mix_in['Wqkv'], 'L1_mix_ln1_g': _L1_mix_in['ln1_g'], 'L1_mix_ln1_b': _L1_mix_in['ln1_b'], 'L1_mix_W1': _L1_mix_in['W1'], 'L1_mix_b1': _L1_mix_in['b1'], 'L1_mix_W2': _L1_mix_in['W2'], 'L1_mix_b2': _L1_mix_in['b2'], 'L1_mix_ln2_g': _L1_mix_in['ln2_g'], 'L1_mix_ln2_b': _L1_mix_in['ln2_b'], 'L1_ffn_attention_mask': _L1_ffn_in['attention_mask'], 'L1_ffn_wr': _L1_ffn_in['wr'], 'L1_ffn_br': _L1_ffn_in['br'], 'L1_ffn_w1': _L1_ffn_in['w1'], 'L1_ffn_b1': _L1_ffn_in['b1'], 'L1_ffn_w2': _L1_ffn_in['w2'], 'L1_ffn_b2': _L1_ffn_in['b2']}

def reference(x, src, dst, edge_attr_64, L0_gnn_Wq, L0_gnn_Wk, L0_gnn_Wv, L0_gnn_W1, L0_gnn_b1, L0_gnn_W2, L0_gnn_b2, L0_gnn_Wo, L0_gnn_bo, L0_mix_w_qkv, L0_mix_b_qkv, L0_mix_kln_g, L0_mix_kln_b, L0_mix_vln_g, L0_mix_vln_b, L0_mix_w1, L0_mix_b1, L0_mix_w2, L0_mix_b2, L0_ffn_gate_w, L0_ffn_gate_b, L0_ffn_w1, L0_ffn_b1, L0_ffn_w2, L0_ffn_b2, L1_gnn_W1, L1_gnn_W2, L1_gnn_b, L1_mix_Wqkv, L1_mix_ln1_g, L1_mix_ln1_b, L1_mix_W1, L1_mix_b1, L1_mix_W2, L1_mix_b2, L1_mix_ln2_g, L1_mix_ln2_b, L1_ffn_attention_mask, L1_ffn_wr, L1_ffn_br, L1_ffn_w1, L1_ffn_b1, L1_ffn_w2, L1_ffn_b2):
    import jax
    import jax.numpy as jnp

    def _L0_gnn_ref(h, efeat, src, dst, Wq, Wk, Wv, W1, b1, W2, b2, Wo, bo):
        import jax, jax.numpy as jnp
        import numpy as np
        N, E, D, H, FE = (3125, 50000, 256, 8, 64)
        HD = D // H
        n = h.shape[0]
        Q = (h @ Wq).reshape(n, H, HD)
        K = (h @ Wk).reshape(n, H, HD)
        V = (h @ Wv).reshape(n, H, HD)
        score = jnp.einsum('ehd,ehd->eh', Q[dst], K[src]) / np.sqrt(HD)
        score = score + jax.nn.relu(efeat @ W1 + b1) @ W2 + b2
        m = jax.ops.segment_max(score, dst, num_segments=n)
        ex = jnp.exp(score - m[dst])
        denom = jax.ops.segment_sum(ex, dst, num_segments=n)
        alpha = ex / denom[dst]
        out = jax.ops.segment_sum(alpha[:, :, None] * V[src], dst, num_segments=n)
        out = out.reshape(n, D)
        return out @ Wo + bo

    def _L0_mix_ref(x, w_qkv, b_qkv, kln_g, kln_b, vln_g, vln_b, w1, b1, w2, b2):
        import jax, jax.numpy as jnp
        import numpy as np
        MIDC = 256
        HEADS = 8
        HEADC = MIDC // HEADS
        EPS = 1e-05

        def _ln(x, gamma, beta):
            mu = jnp.mean(x, axis=-1, keepdims=True)
            var = jnp.var(x, axis=-1, keepdims=True)
            return (x - mu) * jax.lax.rsqrt(var + EPS) * gamma + beta
        B, HW, C = x.shape
        bias = x
        qkv = (x @ w_qkv + b_qkv).reshape(B, HW, HEADS, 3 * HEADC)
        qkv = qkv.transpose(0, 2, 1, 3)
        q, k, v = jnp.split(qkv, 3, axis=-1)
        k = _ln(k, kln_g, kln_b)
        v = _ln(v, vln_g, vln_b)
        kv = jnp.einsum('bhnd,bhne->bhde', k, v) / HW
        out = jnp.einsum('bhnd,bhde->bhne', q, kv)
        out = out.transpose(0, 2, 1, 3).reshape(B, HW, C)
        ret = out + bias
        h = jax.nn.gelu(ret @ w1 + b1, approximate=False)
        return h @ w2 + b2 + bias

    def _L0_ffn_ref(h, gate_w, gate_b, w1, b1, w2, b2):
        import math
        import jax, jax.numpy as jnp
        import numpy as np
        CAPACITY_FACTOR = 1.25
        B, L, D = h.shape
        E = gate_w.shape[1]
        T = B * L
        C = max(1, math.ceil(CAPACITY_FACTOR * T / E))
        x = h.reshape(T, D)
        logits = x @ gate_w + gate_b
        probs = jax.nn.softmax(logits, axis=-1)
        idx = jnp.argmax(probs, axis=-1)
        prb = jnp.take_along_axis(probs, idx[:, None], axis=1)[:, 0]
        one_hot = jax.nn.one_hot(idx, E, dtype=jnp.float32)
        pos = (jnp.cumsum(one_hot, axis=0) * one_hot).sum(-1).astype(jnp.int32) - 1
        kept = pos < C
        pos_safe = jnp.where(kept, pos, C)
        buf = jnp.zeros((E, C, D), dtype=h.dtype).at[idx, pos_safe].set(x, mode='drop')
        hmid = jax.nn.relu(jnp.einsum('ecd,edf->ecf', buf, w1) + b1[:, None, :])
        ybuf = jnp.einsum('ecf,efd->ecd', hmid, w2) + b2[:, None, :]
        pos_g = jnp.minimum(pos, C - 1)
        y_tok = ybuf[idx, pos_g] * (prb * kept)[:, None]
        y = y_tok.reshape(B, L, D)
        y = jnp.nan_to_num(y, nan=0.0, posinf=10000.0, neginf=-10000.0)
        return y

    def _L1_gnn_ref(feat, W1, W2, b, src, dst):
        import jax, jax.numpy as jnp
        import numpy as np
        N_NODES = 25000
        N_EDGES = 25000
        D = 256
        n = feat.shape[0]
        ones = jnp.ones(src.shape[0], dtype=feat.dtype)
        out_deg = jnp.maximum(jax.ops.segment_sum(ones, src, num_segments=n), 1.0)
        in_cnt = jax.ops.segment_sum(ones, dst, num_segments=n)
        t1 = feat @ W1
        msg = t1[src] + feat[src] * feat[dst] @ W2
        scale = jnp.sqrt(out_deg[src]) * jnp.sqrt(out_deg[dst])
        msg = msg / scale[:, None]
        agg = jax.ops.segment_sum(msg, dst, num_segments=n)
        embed = jnp.where(in_cnt[:, None] > 0, t1 + agg, jnp.zeros_like(t1))
        embed = embed + b
        embed = jax.nn.leaky_relu(embed, negative_slope=0.01)
        norm = jnp.linalg.norm(embed, axis=1, keepdims=True)
        embed = embed / jnp.maximum(norm, 1e-12)
        return embed

    def _L1_mix_ref(x, Wqkv, ln1_g, ln1_b, W1, b1, W2, b2, ln2_g, ln2_b):
        import jax, jax.numpy as jnp
        import numpy as np
        N, F, C, H = (32, 256, 256, 8)
        D = C // H
        EPS_ATTN = 1e-06
        EPS_LN = 1e-05

        def layer_norm(x, g, b):
            mu = jnp.mean(x, axis=-1, keepdims=True)
            var = jnp.var(x, axis=-1, keepdims=True)
            return (x - mu) * jax.lax.rsqrt(var + EPS_LN) * g + b
        n, f, c = x.shape
        qkv = jnp.einsum('nfc,oc->nfo', x, Wqkv)
        q, k, v = jnp.split(qkv, 3, axis=-1)
        q = q.reshape(n, f, H, D)
        k = k.reshape(n, f, H, D)
        v = v.reshape(n, f, H, D)
        q = jax.nn.elu(q) + 1.0
        k = jax.nn.elu(k) + 1.0
        kv = jnp.einsum('nshd,nshm->nhmd', k, v)
        ksum = jnp.sum(k, axis=1)
        z = 1.0 / (jnp.einsum('nlhd,nhd->nlh', q, ksum) + EPS_ATTN)
        t = jnp.einsum('nlhd,nhmd,nlh->nlhm', q, kv, z)
        t = t.reshape(n, f, c)
        x1 = layer_norm(t + x, ln1_g, ln1_b)
        h = jax.nn.gelu(jnp.einsum('nfc,oc->nfo', x1, W1) + b1, approximate=False)
        y = jnp.einsum('nfc,oc->nfo', h, W2) + b2
        return layer_norm(y + x1, ln2_g, ln2_b)

    def _L1_ffn_ref(x, attention_mask, wr, br, w1, b1, w2, b2):
        import jax, jax.numpy as jnp
        import numpy as np
        B, S, D = (8, 256, 256)
        H = 4 * D
        CAPACITY = 0.5
        b, s, d = x.shape
        weights = (jnp.einsum('bsd,do->bso', x, wr) + br)[..., 0]
        k = max(1, int(CAPACITY * s))
        kk = k - 1 if k > 1 else 1
        _, idx = jax.lax.top_k(weights, k)
        sel_idx = idx[:, :kk]
        sel = jnp.take_along_axis(x, sel_idx[:, :, None], axis=1)
        h = jax.nn.gelu(jnp.einsum('bkd,dh->bkh', sel, w1) + b1)
        y = jnp.einsum('bkh,hd->bkd', h, w2) + b2
        w_sel = jnp.take_along_axis(weights, sel_idx, axis=1)
        y = y * w_sel[..., None]
        batch_idx = jnp.arange(b)[:, None]
        processed = jnp.zeros_like(x).at[batch_idx, sel_idx].set(y)
        return processed + x
    xn = _layernorm(x, axis=-1)
    x = x + _L0_gnn_ref(xn, edge_attr_64, src, dst, L0_gnn_Wq, L0_gnn_Wk, L0_gnn_Wv, L0_gnn_W1, L0_gnn_b1, L0_gnn_W2, L0_gnn_b2, L0_gnn_Wo, L0_gnn_bo) + _L0_mix_ref(xn[None], L0_mix_w_qkv, L0_mix_b_qkv, L0_mix_kln_g, L0_mix_kln_b, L0_mix_vln_g, L0_mix_vln_b, L0_mix_w1, L0_mix_b1, L0_mix_w2, L0_mix_b2)[0]
    x = x + _L0_ffn_ref(_layernorm(x, axis=-1)[None], L0_ffn_gate_w, L0_ffn_gate_b, L0_ffn_w1, L0_ffn_b1, L0_ffn_w2, L0_ffn_b2)[0]
    xn = _layernorm(x, axis=-1)
    x = x + _L1_gnn_ref(xn, L1_gnn_W1, L1_gnn_W2, L1_gnn_b, src, dst) + _L1_mix_ref(xn[None], L1_mix_Wqkv, L1_mix_ln1_g, L1_mix_ln1_b, L1_mix_W1, L1_mix_b1, L1_mix_W2, L1_mix_b2, L1_mix_ln2_g, L1_mix_ln2_b)[0]
    x = x + _L1_ffn_ref(_layernorm(x, axis=-1)[None], L1_ffn_attention_mask, L1_ffn_wr, L1_ffn_br, L1_ffn_w1, L1_ffn_b1, L1_ffn_w2, L1_ffn_b2)[0]
    return x

_drawn_inputs = setup_inputs


def setup_inputs(seed=0):
    import zlib

    import numpy as np

    out = dict(_drawn_inputs(seed))
    spreads = {'L0_gnn_b1': (0.0, 0.8),
     'L0_gnn_b2': (0.0, 0.8),
     'L0_gnn_bo': (0.0, 0.1),
     'L0_mix_b_qkv': (0.0, 0.1),
     'L0_mix_kln_g': (1.0, 0.6),
     'L0_mix_kln_b': (0.0, 0.399),
     'L0_mix_vln_g': (1.0, 0.55),
     'L0_mix_vln_b': (0.0, 0.361),
     'L0_mix_b1': (0.0, 0.1),
     'L0_mix_b2': (0.0, 0.1),
     'L0_ffn_gate_b': (0.0, 0.1),
     'L0_ffn_b1': (0.0, 0.8),
     'L0_ffn_b2': (0.0, 0.8),
     'L1_gnn_b': (0.0, 0.8),
     'L1_mix_ln1_g': (1.0, 0.2),
     'L1_mix_ln1_b': (0.0, 0.1),
     'L1_mix_ln2_g': (1.0, 0.2),
     'L1_mix_ln2_b': (0.0, 0.267),
     'L1_ffn_b1': (0.0, 0.8),
     'L1_ffn_b2': (0.0, 0.8)}
    factors = {'L1_gnn_W1': 3.498,
     'L1_gnn_W2': 8.0,
     'L1_mix_b1': 8.0,
     'L1_mix_b2': 4.88,
     'L1_ffn_wr': 7.212,
     'L1_ffn_w1': 8.0,
     'L1_ffn_w2': 7.6}
    for name, (base, spread) in spreads.items():
        noise = np.random.default_rng([zlib.crc32(name.encode()), seed]).standard_normal(out[name].shape)
        drawn = base * np.exp(spread * noise) if base else spread * noise
        out[name] = jnp.asarray(drawn.astype(out[name].dtype))
    for name, factor in factors.items():
        out[name] = (out[name] * factor).astype(out[name].dtype)
    return out
```

```python
from contextlib import ExitStack

import concourse.bass as bass
from concourse import mybir

F32 = mybir.dt.float32
BF16 = mybir.dt.bfloat16
I32 = mybir.dt.int32
ALU = mybir.AluOpType
ACT = mybir.ActivationFunctionType
AX_X = mybir.AxisListType.X

N, E, D, H, FE = 3125, 100000, 256, 8, 64
HD = D // H
P = 128
RT = 125
NT = N // RT
ET = E // RT
UN = 5
NG = NT // UN
GT = 16
EG = ET // GT
QT = 4
NQ = GT // QT
EP = 100
EK = ET // EP
KC = D // P
RW = D + H
BIG = 1.0e30
EPS = 1e-5
MAGIC = 12582912.0
EXPERTS, FF = 8, 1024
CAP = -(-5 * N // (4 * EXPERTS))
CAPR = 500
FC = FF // P
TOPK = N // 2 - 1
UT = 4
TU = 4
TKR = -(-TOPK // (UT * TU))

assert N % RT == 0 and E % RT == 0 and ET % GT == 0 and EG == 2 * NT and GT * H == P


class Kept:

    def __init__(self, kept):
        self.kept = kept


def stage(nc, s):
    ctx = ExitStack()

    def sb(name, shape, dt=F32):
        return ctx.enter_context(nc.sbuf_tensor(f"{s}_{name}", shape, dt))

    def ps(name, cols=512):
        return ctx.enter_context(nc.psum_tensor(f"{s}_{name}", [P, cols], F32))

    used = []

    def sem(name, kept=None):
        if kept is not None:
            return kept.enter_context(nc.semaphore(f"{s}_{name}"))
        used.append(ctx.enter_context(nc.semaphore(f"{s}_{name}")))
        return used[-1]

    def clear():
        nums = sorted(x.num for x in used)
        at = 0
        for n in range(1, len(nums) + 1):
            if n == len(nums) or nums[n] != nums[n - 1] + 1:
                nc.gpsimd.sem_clear(range(nums[at], nums[n - 1] + 1))
                at = n
        nc.all_engine_barrier()

    ctx.callback(clear)
    return ctx, sb, ps, sem


def bcast_row(ap1d, parts):
    return ap1d.rearrange("(o n) -> o n", o=1).to_broadcast([parts, ap1d.shape[0]])


def prepare(nc, K, I):
    ctx, sb, ps, sem = stage(nc, "prep")
    with ctx:
        src_i = sb("src_i", [EP, EK * RT], I32)
        dst_i = sb("dst_i", [EP, EK * RT], I32)
        prev_i = sb("prev_i", [EP, EK * RT], I32)
        pos_i = sb("pos_i", [EP, EK * RT], I32)
        base_i = sb("base_i", [EP, EK * RT], I32)
        col_i = sb("col_i", [P, P], I32)
        srcf = sb("srcf", [EP, EK * RT])
        dstf = sb("dstf", [EP, EK * RT])
        first = sb("first", [EP, EK * RT])
        mark = sb("mark", [EP, EK * RT])
        seg = sb("seg", [EP, EK * RT])
        seg0 = sb("seg0", [EP, EK * RT])
        neg = sb("neg", [EP, EK, RT + 1])
        stf = sb("stf", [RT, ET])
        dtf = sb("dtf", [RT, ET])
        tmp = sb("tmp", [RT, ET])
        tmp2 = sb("tmp2", [RT, ET])
        psT = [ps(f"psT{i}") for i in range(6)]
        edges_in = sem("edges_in")
        x_in = sem("x_in")
        zeroed = sem("zeroed")
        const_ready = sem("const_ready")
        step = sem("step")
        turned = sem("turned")
        spread = sem("spread")
        round_step = sem("round_step")
        neg_out = sem("neg_out")
        block = ctx.enter_context(nc.Block())
        e3 = "(p k) -> p k"

        @block.sync
        def _(sp):
            sp.dma_start(src_i[:], I["src"].rearrange(e3, p=EP)).then_inc(edges_in, 16)
            sp.dma_start(dst_i[:], I["dst"].rearrange(e3, p=EP)).then_inc(edges_in, 16)
            w = EK * RT
            sp.dma_start(prev_i[1:EP, :], I["dst"][w - 1:E - 1].rearrange(e3, p=EP - 1)).then_inc(edges_in, 16)
            sp.dma_start(prev_i[0:1, 1:w], I["dst"][0:w - 1].rearrange(e3, p=1)).then_inc(edges_in, 16)
            sp.dma_start(K.x[:], I["x"].rearrange("(i p) d -> p i d", p=RT)).then_inc(x_in, 16)
            sp.wait_ge(round_step, 5)
            sp.dma_start(K.neg_d.rearrange("(p k) j -> p k j", p=EP), neg[:]).then_inc(neg_out, 16)
            sp.wait_ge(round_step, 6)
            sp.dma_start(K.cont_d.rearrange(e3, p=EP), K.cont[:]).then_inc(neg_out, 16)
            sp.dma_start(K.single_d.rearrange(e3, p=EP), K.single[:]).then_inc(neg_out, 16)
            sp.wait_ge(neg_out, 48)
            sp.wait_ge(x_in, 16)

        @block.gpsimd
        def _(pool):
            pool.memset(K.ident[:], 0.0).then_inc(zeroed, 1)
            pool.memset(K.tri[:], 0.0).then_inc(zeroed, 1)
            pool.memset(K.ones[:], 1.0)
            pool.iota(pos_i[:], [[1, EK * RT]], base=0, channel_multiplier=0).then_inc(zeroed, 1)
            pool.iota(base_i[:], [[RT, EK], [0, RT]], base=0, channel_multiplier=0).then_inc(zeroed, 1)
            pool.iota(col_i[:], [[1, P]], base=0, channel_multiplier=0).then_inc(zeroed, 1)
            pool.iota(K.row_i[:], [[0, 1]], base=0, channel_multiplier=1).then_inc(zeroed, 1)
            pool.wait_ge(zeroed, 6)
            pool.affine_select(out=K.ident[:], in_=K.ident[:], compare_op=ALU.not_equal, fill=1.0, base=0,
                               pattern=[[-1, P]], channel_multiplier=1).then_inc(const_ready, 1)
            pool.affine_select(out=K.tri[:], in_=K.tri[:], compare_op=ALU.is_ge, fill=1.0, base=0,
                               pattern=[[-1, P]], channel_multiplier=1).then_inc(const_ready, 1)

        @block.vector
        def _(dve):
            dve.memset(prev_i[0:1, 0:1], -1).then_inc(step, 1)
            dve.memset(neg[:, :, RT:RT + 1], -BIG).then_inc(step, 1)
            dve.memset(K.src_t[:, ET:], 0)
            dve.memset(K.dst_t[:, ET:], 0)
            dve.wait_ge(edges_in, 64)
            dve.wait_ge(step, 1)
            dve.tensor_copy(srcf[:], src_i[:]).then_inc(step, 1)
            dve.tensor_copy(dstf[:], dst_i[:]).then_inc(step, 1)
            dve.tensor_tensor(first[:], dst_i[:], prev_i[:], ALU.not_equal).then_inc(step, 1)
            dve.wait_ge(step, 5)
            fv = first[:].rearrange("p (k j) -> p k j", j=RT)
            dve.tensor_scalar(K.cont[:], fv[:, :, 0], -1.0, 1.0, ALU.mult, ALU.add).then_inc(step, 1)
            dve.wait_ge(zeroed, 6)
            dve.tensor_copy(K.col[:], col_i[:]).then_inc(step, 1)
            dve.tensor_copy(K.colb[:], col_i[:]).then_inc(step, 1)
            dve.tensor_scalar(K.tilebase[:], col_i[:, 0:NT], float(RT), None, ALU.mult)
            dve.tensor_copy(K.rowf[:], K.row_i[:]).then_inc(step, 1)
            dve.tensor_copy(seg0[:], base_i[:]).then_inc(step, 1)
            dve.tensor_copy(seg[:], pos_i[:]).then_inc(step, 1)
            dve.wait_ge(step, 6)
            dve.memset(fv[:, :, 0:1], 1.0).then_inc(step, 1)
            dve.wait_ge(step, 12)
            dve.tensor_tensor(mark[:], first[:], seg[:], ALU.mult).then_inc(round_step, 1)
            dve.tensor_scalar(neg[:, :, 0:RT], fv, -BIG, None, ALU.mult).then_inc(round_step, 1)
            dve.wait_ge(round_step, 2)
            dve.tensor_tensor_scan(seg[:], mark[:], mark[:], 0.0, ALU.max, ALU.max).then_inc(round_step, 1)
            dve.wait_ge(round_step, 3)
            dve.tensor_tensor(mark[:], seg[:], seg0[:], ALU.subtract).then_inc(round_step, 1)
            dve.wait_ge(round_step, 4)
            mv = mark[:].rearrange("p (k j) -> p k j", j=RT)
            dve.tensor_scalar(K.single[:], mv[:, :, RT - 1], 0.0, None, ALU.is_equal).then_inc(round_step, 1)
            dv = dstf[:].rearrange("p (k j) -> p k j", j=RT)
            dve.scalar_tensor_tensor(out=K.dfirst[:], in0=dv[:, :, 0], scalar=1.0, in1=K.cont[:],
                                     op0=ALU.add, op1=ALU.mult).then_inc(round_step, 1)
            dve.wait_ge(round_step, 6)
            dve.tensor_scalar(K.dfirst[:], K.dfirst[:], -1.0, None, ALU.add).then_inc(round_step, 1)
            for n, (dsts, ints) in enumerate(((stf, K.src_t), (dtf, K.dst_t), (K.seg_t, None))):
                for b in range(2):
                    dve.wait_ge(turned, 2 * n + b + 1)
                    from_ps = psT[2 * n + b][0:RT, 0:4 * EP].rearrange("e (k p) -> e k p", k=4)
                    dve.tensor_copy(dsts[:].rearrange("e (p k) -> e k p", k=EK)[:, 4 * b:4 * b + 4, :],
                                    from_ps).then_inc(spread, 1)
                    if ints is not None:
                        dve.tensor_copy(ints[:, 0:ET].rearrange("e (p k) -> e k p", k=EK)[:, 4 * b:4 * b + 4, :],
                                        from_ps).then_inc(spread, 1)
            dve.wait_ge(spread, 10)
            k = 7
            for node, hi, lo in ((stf, K.src_hi, K.src_lo), (dtf, K.dst_hi, K.dst_lo)):
                dve.tensor_scalar(tmp[:], node[:], -float(RT // 2), 1.0 / RT, ALU.add, ALU.mult).then_inc(round_step, 1)
                dve.wait_ge(round_step, k + 1)
                dve.tensor_scalar(tmp2[:], tmp[:], MAGIC, None, ALU.add).then_inc(round_step, 1)
                dve.wait_ge(round_step, k + 2)
                dve.tensor_scalar(tmp[:], tmp2[:], -MAGIC, None, ALU.add).then_inc(round_step, 1)
                dve.wait_ge(round_step, k + 3)
                dve.tensor_copy(hi[:], tmp[:]).then_inc(round_step, 1)
                dve.scalar_tensor_tensor(out=lo[:], in0=tmp[:], scalar=-float(RT), in1=node[:],
                                         op0=ALU.mult, op1=ALU.add).then_inc(round_step, 1)
                dve.wait_ge(round_step, k + 5)
                k += 5

        @block.tensor
        def _(pe):
            pe.wait_ge(const_ready, 1)
            for n, (tab, s, v) in enumerate(((srcf, step, 3), (dstf, step, 4), (mark, round_step, 4))):
                pe.wait_ge(s, v)
                tv = tab[:].rearrange("p (k j) -> p k j", j=RT)
                for b in range(2):
                    for q in range(4):
                        t = pe.transpose(psT[2 * n + b][0:RT, q * EP:(q + 1) * EP], tv[:, 4 * b + q, :],
                                         K.ident[0:EP, 0:EP])
                    t.then_inc(turned, 1)


def turns(eng, body):
    body(0, False)
    with eng.Fori(1, NG) as g:
        body(g, True)


def load_chunks(sp, dst, src, done):
    sp.dma_start(dst, src.rearrange("(c p) n -> p c n", p=P)).then_inc(done, 16)


def load_cols(sp, dst, src, done):
    for c in range(src.shape[0] // P):
        sp.dma_start(dst[:, c:c + 1], src[c * P:(c + 1) * P].rearrange("(p o) -> p o", o=1)).then_inc(done, 16)


def node_tables(nc, K, I):
    ctx, sb, ps, sem = stage(nc, "tab")
    with ctx:
        wkv = sb("wkv", [P, KC, 2 * D])
        wq = sb("wq", [P, KC, D])
        wm = sb("wm", [P, KC, 2, D])
        bm = sb("bm", [1, 2, D])
        gam = sb("gam", [RT, 2, HD])
        bet = sb("bet", [RT, 2, HD])
        eps = sb("eps", [P, 1])
        zero = sb("zero", [P, D])
        blocks = sb("blocks", [P, P])
        xn = [sb(f"xn{u}", [RT, D]) for u in range(UN)]
        stats = sb("stats", [RT, UN, 6])
        mv = sb("mv", [RT, UN, 2])
        dev = sb("dev", [RT, UN])
        rdev = sb("rdev", [RT, UN])
        xt = [sb(f"xt{b}", [P, KC, RT]) for b in range(2)]
        kvrow = [sb(f"kvrow{b}", [RT, 2 * D]) for b in range(2)]
        qrow = [sb(f"qrow{b}", [RT, D]) for b in range(2)]
        cen = [sb(f"cen{b}", [RT, 2 * H, HD]) for b in range(2)]
        sq = sb("sq", [RT, 2 * H, HD])
        hsum = sb("hsum", [RT, 2 * H])
        hmean = sb("hmean", [RT, 2 * H])
        hvar = sb("hvar", [RT, 2 * H])
        hdev = sb("hdev", [RT, 2 * H])
        hrdev = sb("hrdev", [RT, 2 * H])
        nrm = [sb(f"nrm{b}", [RT, 2 * H, HD]) for b in range(2)]
        sca = sb("sca", [RT, 2 * H, HD])
        kvn = [sb(f"kvn{b}", [RT, 2 * D]) for b in range(2)]
        psT = [ps("psT")]
        psKV = ps("psKV")
        psQ = ps("psQ")
        psM = [ps("psM")]
        psS = ps("psS")
        w_in = sem("w_in")
        consts = sem("consts")
        ln_step = sem("ln_step")
        dev_ready = sem("dev_ready")
        xn_ready = sem("xn_ready")
        turned = sem("turned")
        xt_ready = sem("xt_ready")
        xt_kept = sem("xt_kept")
        x_added = sem("x_added")
        kv_done = sem("kv_done")
        q_done = sem("q_done")
        m_done = sem("m_done")
        kv_taken = sem("kv_taken")
        q_taken = sem("q_taken")
        kv_out = [sem(f"kv_out{b}") for b in range(2)]
        q_out = [sem(f"q_out{b}") for b in range(2)]
        m_step = sem("m_step")
        sq_ready = sem("sq_ready")
        hdev_ready = sem("hdev_ready")
        hrdev_done = sem("hrdev_done")
        sca_ready = sem("sca_ready")
        kvn_ready = sem("kvn_ready")
        summed = sem("summed")
        block = ctx.enter_context(nc.Block())

        @block.sync
        def _(sp):
            load_chunks(sp, wkv[:, :, 0:D], I["L0_gnn_Wk"], w_in)
            load_chunks(sp, wkv[:, :, D:2 * D], I["L0_gnn_Wv"], w_in)
            load_chunks(sp, wq[:], I["L0_gnn_Wq"], w_in)
            wv = I["L0_mix_w_qkv"].rearrange("(c p) (h t d) -> p c t h d", p=P, h=H, t=3)
            bv = I["L0_mix_b_qkv"].rearrange("(o h t d) -> o t h d", o=1, h=H, t=3)
            for t in range(2):
                for c in range(KC):
                    sp.dma_start(wm[:, c, t, :].rearrange("p (h d) -> p h d", h=H), wv[:, c, 1 + t]).then_inc(w_in, 16)
                sp.dma_start(bm[:, t, :].rearrange("p (h d) -> p h d", h=H), bv[:, 1 + t]).then_inc(w_in, 16)
            for t, (g, b) in enumerate((("L0_mix_kln_g", "L0_mix_kln_b"), ("L0_mix_vln_g", "L0_mix_vln_b"))):
                sp.dma_start(gam[:, t, :], bcast_row(I[g], RT)).then_inc(w_in, 16)
                sp.dma_start(bet[:, t, :], bcast_row(I[b], RT)).then_inc(w_in, 16)

            def store(g, again):
                for u in range(UN):
                    i = g * UN + u
                    sp.wait_ge(kv_taken, i + 1)
                    sp.dma_start(K.kv_d[bass.ds(i * RT, RT), :], kvrow[u % 2][:]).then_inc(kv_out[u % 2], 16)
                    sp.wait_ge(q_taken, i + 1)
                    sp.dma_start(K.q_d[bass.ds(i * RT, RT), :], qrow[u % 2][:]).then_inc(q_out[u % 2], 16)

            turns(sp, store)
            for b in range(2):
                sp.wait_ge(kv_out[b], 16 * NG * (3 - b))
                sp.wait_ge(q_out[b], 16 * NG * (3 - b))

        def slot_use(g, u):
            return g * (3 - u % 2) + u // 2

        W_IN = 16 * (3 + 6 + 4)

        @block.gpsimd
        def _(pool):
            pool.memset(zero[:], 0.0).then_inc(consts, 1)
            pool.memset(eps[:], EPS).then_inc(consts, 1)
            pool.memset(blocks[:], 0.0).then_inc(consts, 1)
            pool.wait_ge(consts, 3)
            for b in range(P // HD):
                pool.memset(blocks[b * HD:(b + 1) * HD, b * HD:(b + 1) * HD], 1.0 / N).then_inc(consts, 1)
            pool.wait_ge(consts, 3 + P // HD)
            pool.wait_ge(w_in, W_IN)

            def affine(g, again):
                for u in range(UN):
                    i = g * UN + u
                    pool.wait_ge(xn_ready, i + 1)
                    pool.tensor_tensor(K.x[:, bass.ds(i, 1), :], K.x[:, bass.ds(i, 1), :],
                                       xn[u][:].rearrange("p (o d) -> p o d", o=1), ALU.add).then_inc(x_added, 1)
                    pool.wait_ge(m_step, 5 * i + 5)
                    if again or u:
                        pool.wait_ge(kvn_ready, 2 * i)
                    for t in range(2):
                        pool.tensor_tensor(sca[:, t * H:(t + 1) * H, :], nrm[u % 2][:, t * H:(t + 1) * H, :],
                                           gam[:, t:t + 1, :].to_broadcast([RT, H, HD]), ALU.mult).then_inc(sca_ready, 1)
                    pool.wait_ge(sca_ready, 2 * i + 2)
                    if again or u >= 2:
                        pool.wait_ge(summed, i - (u > 0))
                    for t in range(2):
                        pool.tensor_tensor(kvn[u % 2][:, t * D:(t + 1) * D].rearrange("p (h d) -> p h d", h=H),
                                           sca[:, t * H:(t + 1) * H, :],
                                           bet[:, t:t + 1, :].to_broadcast([RT, H, HD]), ALU.add).then_inc(kvn_ready, 1)

            turns(pool, affine)

        @block.vector
        def _(dve):
            def body(g, again):
                if again:
                    dve.wait_ge(turned, UN * g)
                    dve.wait_ge(x_added, UN * g)
                for u in range(UN):
                    dve.bn_stats(stats[:, u, :], K.x[:, bass.ds(g * UN + u, 1), :].rearrange("p o d -> p (o d)")
                                 ).then_inc(ln_step, 1)
                dve.wait_ge(ln_step, 11 * g + 5)
                dve.nop(nofuse=True)
                for u in range(UN):
                    dve.bn_aggr(mv[:, u, :], stats[:, u, :]).then_inc(ln_step, 1)
                dve.wait_ge(dev_ready, g + 1)
                dve.reciprocal(rdev[:], dev[:]).then_inc(ln_step, 1)
                dve.wait_ge(ln_step, 11 * g + 11)
                for u in range(UN):
                    dve.tensor_scalar(xn[u][:], K.x[:, bass.ds(g * UN + u, 1), :].rearrange("p o d -> p (o d)"),
                                      mv[:, u, 0:1], rdev[:, u:u + 1], ALU.subtract, ALU.mult).then_inc(xn_ready, 1)
                for u in range(UN):
                    i = g * UN + u
                    dve.wait_ge(kv_done, i + 1)
                    if again or u >= 2:
                        dve.wait_ge(kv_out[u % 2], slot_use(g, u) * 16)
                    dve.tensor_copy(kvrow[u % 2][:], psKV[0:RT, :]).then_inc(kv_taken, 1)
                    dve.wait_ge(m_done, i + 1)
                    m3 = psM[0][0:RT, :].rearrange("p (h d) -> p h d", d=HD)
                    dve.tensor_reduce(hsum[:], m3, AX_X, ALU.add).then_inc(m_step, 1)
                    dve.wait_ge(m_step, 5 * i + 1)
                    dve.tensor_scalar(hmean[:], hsum[:], 1.0 / HD, None, ALU.mult).then_inc(m_step, 1)
                    dve.wait_ge(m_step, 5 * i + 2)
                    dve.tensor_tensor(cen[u % 2][:], m3, hmean[:].unsqueeze(2).to_broadcast([RT, 2 * H, HD]),
                                      ALU.subtract).then_inc(m_step, 1)
                    dve.wait_ge(sq_ready, i + 1)
                    dve.tensor_reduce(hvar[:], sq[:], AX_X, ALU.add).then_inc(m_step, 1)
                    dve.wait_ge(hdev_ready, i + 1)
                    dve.reciprocal(hrdev[:], hdev[:]).then_inc(hrdev_done, 1)
                    dve.wait_ge(hrdev_done, i + 1)
                    if again or u >= 2:
                        dve.wait_ge(sca_ready, 2 * (i - (u > 0)))
                    dve.tensor_tensor(nrm[u % 2][:], cen[u % 2][:],
                                      hrdev[:].unsqueeze(2).to_broadcast([RT, 2 * H, HD]), ALU.mult).then_inc(m_step, 1)

            turns(dve, body)
            dve.wait_ge(summed, NT)
            dve.wait_ge(consts, 3 + P // HD)
            for c in range(KC):
                dve.tensor_tensor(K.mkv[:, c, :], psS[:, c * P:(c + 1) * P], blocks[:], ALU.mult).then_inc(xn_ready, 1)

        @block.scalar
        def _(act):
            act.wait_ge(consts, 3)

            def body(g, again):
                act.wait_ge(ln_step, 11 * g + 10)
                act.activation(dev[:], mv[:, :, 1], ACT.Sqrt, bias=eps[0:RT, :]).then_inc(dev_ready, 1)
                for u in range(UN):
                    i = g * UN + u
                    act.wait_ge(turned, i + 1)
                    if again or u >= 2:
                        act.wait_ge(m_done, i - (u > 0))
                    t3 = psT[0][:, 0:KC * RT].rearrange("p (c n) -> p c n", c=KC)
                    act.activation(xt[u % 2][:], t3, ACT.Copy).then_inc(xt_ready, 1)
                    act.activation(K.xt[:, :, bass.ds(i * RT, RT)], t3, ACT.Copy).then_inc(xt_kept, 1)
                    act.wait_ge(q_done, i + 1)
                    if again or u >= 2:
                        act.wait_ge(q_out[u % 2], slot_use(g, u) * 16)
                    act.activation(qrow[u % 2][:], psQ[0:RT, 0:D], ACT.Copy, scale=float(HD) ** -0.5).then_inc(q_taken, 1)
                    act.wait_ge(m_step, 5 * i + 3)
                    act.activation(sq[:], cen[u % 2][:], ACT.Square).then_inc(sq_ready, 1)
                    act.wait_ge(m_step, 5 * i + 4)
                    act.activation(hdev[:], hvar[:], ACT.Sqrt, bias=eps[0:RT, :], scale=1.0 / HD).then_inc(hdev_ready, 1)

            turns(act, body)

        @block.tensor
        def _(pe):
            pe.wait_ge(w_in, W_IN)
            pe.wait_ge(consts, 1)
            pe.matmul(psS[:, 0:D], zero[:, 0:P], zero[:], start=True, stop=False, skip_group_check=True)

            def accumulate(i, u, last=False):
                pe.wait_ge(kvn_ready, 2 * i + 2)
                for c in range(KC):
                    m = pe.matmul(psS[:, c * P:(c + 1) * P], kvn[u % 2][:, c * P:(c + 1) * P],
                                  kvn[u % 2][:, D + c * P:D + (c + 1) * P], start=False, stop=last, skip_group_check=True)
                m.then_inc(summed, 1)

            def body(g, again):
                for u in range(UN):
                    i = g * UN + u
                    pe.wait_ge(xn_ready, i + 1)
                    if again or u:
                        pe.wait_ge(xt_kept, i)
                    for c in range(KC):
                        t = pe.transpose(psT[0][:, c * RT:(c + 1) * RT], xn[u][:, c * P:(c + 1) * P], K.ident[0:RT, 0:RT])
                    t.then_inc(turned, 1)
                    pe.wait_ge(xt_ready, i + 1)
                    if again or u:
                        pe.wait_ge(kv_taken, i)
                    for c in range(KC):
                        m = pe.matmul(psKV[0:RT, :], xt[u % 2][:, c, :], wkv[:, c, :], start=c == 0, stop=c == KC - 1)
                    m.then_inc(kv_done, 1)
                    if again or u:
                        pe.wait_ge(q_taken, i)
                    for c in range(KC):
                        m = pe.matmul(psQ[0:RT, 0:D], xt[u % 2][:, c, :], wq[:, c, :], start=c == 0, stop=c == KC - 1)
                    m.then_inc(q_done, 1)
                    if again or u:
                        pe.wait_ge(m_step, 5 * i - 2)
                    pe.matmul(psM[0][0:RT, :], K.ones[0:1, 0:RT], bm[:].rearrange("p t n -> p (t n)"), start=True, stop=False)
                    for c in range(KC):
                        m = pe.matmul(psM[0][0:RT, :], xt[u % 2][:, c, :], wm[:, c, :, :].rearrange("p t n -> p (t n)"),
                                      start=False, stop=c == KC - 1)
                    m.then_inc(m_done, 1)
                    if again or u:
                        accumulate(i - 1, (u - 1) % UN)

            turns(pe, body)
            accumulate(NT - 1, UN - 1, True)


def edge_attention(nc, K, I):
    ctx, sb, ps, sem = stage(nc, "edge")
    with ctx:
        w1 = sb("w1", [P, D])
        b1 = sb("b1", [P, KC])
        w2z = sb("w2z", [P, KC, (2 * GT - 1) * H])
        b2 = sb("b2", [P, 1])
        idx_s = [sb(f"idx_s{p}", [RT, GT], I32) for p in range(2)]
        idx_d = [sb(f"idx_d{p}", [RT, GT], I32) for p in range(2)]
        kv = [sb(f"kv{p}", [RT, GT, 2 * D]) for p in range(2)]
        qr = sb("qr", [RT, NQ, D * QT])
        ef = sb("ef", [RT, GT, FE])
        neg = [sb(f"neg{p}", [P, RT + 1]) for p in range(2)]
        eft = sb("eft", [P, GT // 2, RT])
        hid = sb("hid", [P, KC, GT // 2, 2, RT])
        sc = sb("sc", [RT, GT * H])
        st = sb("st", [P, RT])
        fmx = sb("fmx", [P, RT])
        gmx = sb("gmx", [P, RT])
        ex = sb("ex", [P, RT])
        exg = sb("exg", [RT, GT * H])
        vals = [sb(f"vals{b}", [RT, QT, RW]) for b in range(2)]
        onehot = [sb(f"onehot{b}", [RT, QT, RT]) for b in range(2)]
        rows = [sb(f"rows{b}", [RT, 2, RW]) for b in range(2)]
        olo = sb("olo", [RT, 2, QT, RT], BF16)
        ohi = sb("ohi", [RT, 2, QT, NT], BF16)
        ps_et = ps("ps_et")
        ps_h = [ps(f"ps_h{b}") for b in range(2)]
        ps_s = ps("ps_s")
        ps_n = ps("ps_n")
        ps_o = [ps(f"ps_o{b}") for b in range(2)]
        ps_m = ps("ps_m")
        mwq = sb("mwq", [P, KC, D])
        mbq = sb("mbq", [P, KC])
        mw1 = sb("mw1", [P, KC, D])
        mb1 = sb("mb1", [P, KC])
        mw2 = sb("mw2", [P, KC, D])
        mb2 = sb("mb2", [1, D])
        mq = sb("mq", [P, KC, RT])
        mr = sb("mr", [P, KC, RT])
        mh = mq
        w_in = sem("w_in")
        mbq_in = sem("mbq_in")
        w2_zeroed = sem("w2_zeroed")
        hist_zeroed = sem("hist_zeroed")
        idx_ready = sem("idx_ready")
        rows_in = [[sem(f"rows_in{p}{q}", kept=K.kept) for q in range(NQ)] for p in range(2)]
        ef_in = sem("ef_in")
        neg_in = [sem(f"neg_in{p}") for p in range(2)]
        ef_turned = sem("ef_turned")
        eft_ready = sem("eft_ready")
        hid_done = sem("hid_done")
        hid_ready = sem("hid_ready")
        prod_ready = sem("prod_ready")
        sc_ready = sem("sc_ready")
        st_done = sem("st_done")
        st_ready = sem("st_ready")
        fmx_ready = sem("fmx_ready")
        gmx_ready = sem("gmx_ready")
        dif_ready = sem("dif_ready")
        max_kept = sem("max_kept")
        ex_ready = sem("ex_ready")
        ex_turned = sem("ex_turned")
        exg_ready = sem("exg_ready")
        vals_ready = sem("vals_ready")
        out_done = sem("out_done")
        row_ready = sem("row_ready")
        rows_out = [sem(f"rows_out{b}") for b in range(2)]
        marks_ready = sem("marks_ready")
        counted = sem("counted")
        count_ready = sem("count_ready")
        mix_mm = sem("mix_mm")
        mix_act = sem("mix_act")
        mix_dve = sem("mix_dve")
        block = ctx.enter_context(nc.Block())
        W_IN = 16 * (2 + KC + KC + GT + KC + 2 + KC + 1)
        TURNS = EG // 2

        def both(eng, turn):
            turn(0, False)
            with eng.Fori(1, TURNS) as it:
                turn(it, True)

        def hist_view(ap, w):
            return ap.rearrange("p a (t j) -> p a t j", t=QT)

        @block.sync
        def _(sp):
            for half in range(2):
                sp.dma_start(w1[half * FE:(half + 1) * FE, :], I["L0_gnn_W1"]).then_inc(w_in, 16)
            sp.wait_ge(w2_zeroed, 1)
            for c in range(KC):
                sp.dma_start(w2z[:, c, (GT - 1) * H:GT * H], I["L0_gnn_W2"][c * P:(c + 1) * P, :]).then_inc(w_in, 16)
            load_cols(sp, b1[:], I["L0_gnn_b1"], w_in)
            for t in range(GT):
                sp.dma_start(b2[t * H:(t + 1) * H, :], I["L0_gnn_b2"].rearrange("(h o) -> h o", o=1)).then_inc(w_in, 16)
            wq = I["L0_mix_w_qkv"].rearrange("(c p) (h t d) -> p c t h d", p=P, h=H, t=3)
            bq = I["L0_mix_b_qkv"].rearrange("(h t d) -> h t d", h=H, t=3)
            for c in range(KC):
                sp.dma_start(mwq[:, c, :].rearrange("p (h d) -> p h d", h=H), wq[:, c, 0]).then_inc(w_in, 16)
                for h in range(H // KC):
                    sp.dma_start(mbq[h * HD:(h + 1) * HD, c:c + 1],
                                 bq[c * (H // KC) + h, 0, :].rearrange("(d o) -> d o", o=1)).then_inc(mbq_in, 16)
            load_chunks(sp, mw1[:], I["L0_mix_w1"], w_in)
            load_chunks(sp, mw2[:], I["L0_mix_w2"], w_in)
            load_cols(sp, mb1[:], I["L0_mix_b1"], w_in)
            sp.dma_start(mb2[:], I["L0_mix_b2"].rearrange("(o n) -> o n", o=1)).then_inc(w_in, 16)

            def load_ef(G):
                sp.dma_start(ef[:], K.ef[bass.ds(G * GT * RT, GT * RT), :].rearrange("(t e) f -> e t f", e=RT)
                             ).then_inc(ef_in, 16)

            def load_neg(G, p):
                sp.dma_start(neg[p][:], K.neg_d[bass.ds(G * GT, GT), :].unsqueeze(1).to_broadcast([GT, H, RT + 1])
                             ).then_inc(neg_in[p], 16)

            def turn(it, more):
                for p in range(2):
                    G = it * 2 + p
                    if more or p == 0:
                        sp.wait_ge(ef_turned, 2 * (G + 1))
                        load_ef(G + 1)
                    if more:
                        sp.wait_ge(gmx_ready, G + 1)
                        load_neg(G + 2, p)
                    for r in range(GT // 2):
                        R = G * (GT // 2) + r
                        sp.wait_ge(row_ready, 2 * (R + 1))
                        sp.dma_start(K.part_d[bass.ds(R * 2 * RT, 2 * RT), :].rearrange("(t j) f -> j t f", j=RT),
                                     rows[r % 2][:]).then_inc(rows_out[r % 2], 16)

            load_ef(0)
            load_neg(0, 0)
            load_neg(1, 1)
            with sp.Fori(0, TURNS - 1) as it:
                turn(it, True)
            turn(TURNS - 1, False)
            for b in range(2):
                sp.wait_ge(rows_out[b], 16 * ET // 4)

        @block.gpsimd
        def _(pool):
            pool.memset(w2z[:], 0.0).then_inc(w2_zeroed, 1)

            def turn(it, again):
                for p in range(2):
                    G = it * 2 + p
                    pool.wait_ge(idx_ready, 2 * (G + 1))
                    for q in range(NQ):
                        if again:
                            pool.wait_ge(vals_ready, 3 * (NQ * (G - 2) + q + 1))
                        if again or p:
                            pool.wait_ge(sc_ready, NQ * (G - 1) + q + 1)
                        pool.nop(nofuse=True)
                        for t in range(q * QT, (q + 1) * QT):
                            pool.indirect_dma_start(kv[p][:, t, :], None, K.kv_d,
                                                    bass.IndirectOffsetOnAxis(ap=idx_s[p][:, t:t + 1], axis=0)
                                                    ).then_inc(rows_in[p][q], 16)
                            pool.indirect_dma_start(qr[:, q, (t % QT) * D:(t % QT + 1) * D], None, K.q_d,
                                                    bass.IndirectOffsetOnAxis(ap=idx_d[p][:, t:t + 1], axis=0)
                                                    ).then_inc(rows_in[p][q], 16)

            both(pool, turn)

        @block.vector
        def _(dve):
            dve.memset(K.hist[:], 0.0).then_inc(hist_zeroed, 1)
            dve.wait_ge(hist_zeroed, 1)
            dve.wait_ge(w_in, W_IN)

            def indices(G, p):
                dve.tensor_copy(idx_s[p][:], K.src_t[:, bass.ds(G * GT, GT)]).then_inc(idx_ready, 1)
                dve.tensor_copy(idx_d[p][:], K.dst_t[:, bass.ds(G * GT, GT)]).then_inc(idx_ready, 1)

            def turn(it, again):
                if not again:
                    indices(0, 0)
                    indices(1, 1)
                for p in range(2):
                    G = it * 2 + p
                    for q in range(NQ):
                        Q = G * NQ + q
                        dve.wait_ge(rows_in[p][q], 2 * QT * 16 * (it + 1))
                        qv = qr[:, q, :].rearrange("e (t d) -> e t d", t=QT)
                        dve.tensor_tensor(qv, qv, kv[p][:, q * QT:(q + 1) * QT, 0:D], ALU.mult).then_inc(prod_ready, 1)
                        dve.wait_ge(prod_ready, Q + 1)
                        if (again or p) and q == 0:
                            dve.wait_ge(st_done, G)
                        dve.tensor_reduce(sc[:, q * QT * H:(q + 1) * QT * H],
                                          qr[:, q, :].rearrange("e (g d) -> e g d", d=HD), AX_X, ALU.add).then_inc(sc_ready, 1)
                    indices(G + 2, p)
                    dve.wait_ge(st_ready, G + 1)
                    dve.wait_ge(neg_in[p], 16 * (it + 1))
                    dve.tensor_tensor_scan(fmx[:], neg[p][:, 0:RT], st[:], -BIG, ALU.add, ALU.max).then_inc(fmx_ready, 1)
                    dve.wait_ge(fmx_ready, G + 1)
                    dve.tensor_tensor_scan(gmx[:, ::-1], neg[p][:, 1:RT + 1][:, ::-1], fmx[:, ::-1], -BIG,
                                           ALU.add, ALU.max).then_inc(gmx_ready, 1)
                    dve.wait_ge(gmx_ready, G + 1)
                    dve.tensor_tensor(st[:], st[:], gmx[:], ALU.subtract).then_inc(dif_ready, 1)
                    dve.tensor_copy(K.mfirst[:, bass.ds(G, 1)], gmx[:, 0:1]).then_inc(max_kept, 1)
                    dve.tensor_copy(K.mlast[:, bass.ds(G, 1)], fmx[:, RT - 1:RT]).then_inc(max_kept, 1)
                    if p == 0:
                        dve.wait_ge(mix_mm, 4 * it + 2)
                        dve.tensor_tensor(mr[:], ps_m[:, 0:KC * RT].rearrange("p (c n) -> p c n", c=KC),
                                          K.xt[:, :, bass.ds(it * RT, RT)], ALU.add).then_inc(mix_dve, 1)
                    else:
                        dve.wait_ge(mix_mm, 4 * it + 4)
                        xi = K.x[:, bass.ds(it, 1), :]
                        dve.tensor_tensor(xi, xi, ps_m[0:RT, 0:D].rearrange("p (o d) -> p o d", o=1),
                                          ALU.add).then_inc(mix_dve, 1)
                    dve.wait_ge(exg_ready, G + 1)
                    for q in range(NQ):
                        Q = G * NQ + q
                        b = q % 2
                        if again or p or q >= 2:
                            dve.wait_ge(out_done, QT * (Q - 1))
                        eq = exg[:, q * QT * H:(q + 1) * QT * H]
                        dve.tensor_tensor(vals[b][:, :, 0:D].rearrange("e t (h d) -> e t h d", h=H),
                                          kv[p][:, q * QT:(q + 1) * QT, D:2 * D].rearrange("e t (h d) -> e t h d", h=H),
                                          eq.rearrange("e (t h) -> e t h", t=QT).unsqueeze(3).to_broadcast([RT, QT, H, HD]),
                                          ALU.mult).then_inc(vals_ready, 1)
                        dve.tensor_copy(vals[b][:, :, D:RW], eq.rearrange("e (t h) -> e t h", t=QT)).then_inc(vals_ready, 1)
                        dve.tensor_tensor(onehot[b][:], K.col[0:RT, 0:RT].unsqueeze(1).to_broadcast([RT, QT, RT]),
                                          K.seg_t[:, bass.ds(Q * QT, QT)].unsqueeze(2).to_broadcast([RT, QT, RT]),
                                          ALU.is_equal).then_inc(vals_ready, 1)
                        if again or p or q:
                            dve.wait_ge(counted, Q)
                        for a, (hi, lo) in enumerate(((K.src_hi, K.src_lo), (K.dst_hi, K.dst_lo))):
                            dve.tensor_tensor(olo[:, a], K.colb[0:RT, 0:RT].unsqueeze(1).to_broadcast([RT, QT, RT]),
                                              lo[:, bass.ds(Q * QT, QT)].unsqueeze(2).to_broadcast([RT, QT, RT]),
                                              ALU.is_equal).then_inc(marks_ready, 1)
                            dve.tensor_tensor(ohi[:, a], K.colb[0:RT, 0:NT].unsqueeze(1).to_broadcast([RT, QT, NT]),
                                              hi[:, bass.ds(Q * QT, QT)].unsqueeze(2).to_broadcast([RT, QT, NT]),
                                              ALU.is_equal).then_inc(marks_ready, 1)
                        if q:
                            add_counts(Q - 1)
                    add_counts(G * NQ + NQ - 1)

            def add_counts(Q):
                dve.wait_ge(counted, Q + 1)
                dve.tensor_tensor(K.hist[:], K.hist[:], ps_n[0:RT, 0:2 * NT].rearrange("p (a n) -> p a n", a=2),
                                  ALU.add).then_inc(count_ready, 1)
                dve.wait_ge(count_ready, Q + 1)

            both(dve, turn)

        @block.scalar
        def _(act):
            act.wait_ge(w_in, W_IN)
            act.wait_ge(mbq_in, 16 * H)

            def turn(it, again):
                for p in range(2):
                    G = it * 2 + p
                    for half in range(2):
                        act.wait_ge(ef_turned, 2 * G + half + 1)
                        if again or p:
                            act.wait_ge(hid_done, 8 * (G - 1) + 4 * half + 4)
                        act.activation(eft[:, 4 * half:4 * half + 4, :],
                                       ps_et[:, 0:4 * RT].rearrange("p (b e) -> p b e", b=4), ACT.Copy).then_inc(eft_ready, 1)
                        for k in range(4):
                            n = 4 * half + k
                            c, par = k // 2, k % 2
                            act.wait_ge(hid_done, 8 * G + n + 1)
                            if (again or p) and n == 0:
                                act.wait_ge(st_done, G)
                            act.activation(hid[:, c, 4 * half:4 * half + 4, par, :],
                                           ps_h[n % 2][:, 0:4 * RT].rearrange("p (b e) -> p b e", b=4),
                                           ACT.Relu, bias=b1[:, c:c + 1]).then_inc(hid_ready, 1)
                    if p == 0:
                        act.wait_ge(mix_mm, 4 * it + 1)
                        for c in range(KC):
                            act.activation(mq[:, c, :], ps_m[:, c * RT:(c + 1) * RT], ACT.Identity,
                                           bias=mbq[:, c:c + 1]).then_inc(mix_act, 1)
                    else:
                        act.wait_ge(mix_mm, 4 * it + 3)
                        for c in range(KC):
                            act.activation(mh[:, c, :], ps_m[:, c * RT:(c + 1) * RT], ACT.Gelu,
                                           bias=mb1[:, c:c + 1]).then_inc(mix_act, 1)
                    act.wait_ge(st_done, G + 1)
                    act.activation(st[:], ps_s[:, 0:RT], ACT.Identity, bias=b2[:]).then_inc(st_ready, 1)
                    act.wait_ge(dif_ready, G + 1)
                    act.activation(ex[:], st[:], ACT.Exp).then_inc(ex_ready, 1)
                    act.wait_ge(ex_turned, G + 1)
                    if again or p:
                        act.wait_ge(vals_ready, 3 * NQ * G)
                    act.activation(exg[:], ps_s[0:RT, RT:RT + P], ACT.Copy).then_inc(exg_ready, 1)
                    for t in range(GT):
                        T = G * GT + t
                        r = t // 2
                        if t % 2 == 0 and (again or p or r >= 2):
                            act.wait_ge(rows_out[r % 2], 16 * (4 * G + r // 2))
                        act.wait_ge(out_done, T + 1)
                        act.activation(rows[r % 2][:, t % 2, :], ps_o[t % 2][0:RT, 0:RW], ACT.Copy).then_inc(row_ready, 1)

            both(act, turn)

        @block.tensor
        def _(pe):
            pe.wait_ge(w_in, W_IN)

            def turn(it, again):
                for p in range(2):
                    G = it * 2 + p
                    for half in range(2):
                        if half == 0:
                            pe.wait_ge(ef_in, 16 * (G + 1))
                        if again or p or half:
                            pe.wait_ge(eft_ready, 2 * G + half)
                        for b in range(4):
                            t = pe.transpose(ps_et[:, b * RT:(b + 1) * RT],
                                             ef[:, 8 * half + 2 * b:8 * half + 2 * b + 2, :].rearrange("e t f -> e (t f)"),
                                             K.ident[0:RT, 0:RT])
                        t.then_inc(ef_turned, 1)
                        pe.wait_ge(eft_ready, 2 * G + half + 1)
                        for k in range(4):
                            n = 4 * half + k
                            c, par = k // 2, k % 2
                            if again or p or n >= 2:
                                pe.wait_ge(hid_ready, 8 * G + n - 1)
                            pe.matmul(ps_h[n % 2][:, 0:4 * RT], w1[par * FE:(par + 1) * FE, c * P:(c + 1) * P],
                                      eft[par * FE:(par + 1) * FE, 4 * half:4 * half + 4, :].rearrange("p b e -> p (b e)"),
                                      start=True, stop=True).then_inc(hid_done, 1)
                    if p == 0:
                        if again:
                            pe.wait_ge(mix_act, 4 * it)
                            pe.wait_ge(mix_dve, 2 * it)
                        for co in range(KC):
                            for c in range(KC):
                                m = pe.matmul(ps_m[:, co * RT:(co + 1) * RT], mwq[:, c, co * P:(co + 1) * P],
                                              K.xt[:, c, bass.ds(it * RT, RT)], start=c == 0, stop=c == KC - 1)
                        m.then_inc(mix_mm, 1)
                    else:
                        pe.wait_ge(mix_dve, 2 * it + 1)
                        for co in range(KC):
                            for c in range(KC):
                                m = pe.matmul(ps_m[:, co * RT:(co + 1) * RT], mw1[:, c, co * P:(co + 1) * P],
                                              mr[:, c, :], start=c == 0, stop=c == KC - 1)
                        m.then_inc(mix_mm, 1)
                    pe.wait_ge(hid_ready, 8 * (G + 1))
                    if again or p:
                        pe.wait_ge(exg_ready, G)
                    for t in range(GT):
                        for c in range(KC):
                            pe.matmul(ps_s[:, 0:RT], w2z[:, c, (GT - 1 - t) * H:(GT - 1 - t) * H + P],
                                      hid[:, c, t // 2, t % 2, :], start=t == 0 and c == 0, stop=False)
                    pe.wait_ge(sc_ready, NQ * (G + 1))
                    pe.matmul(ps_s[:, 0:RT], sc[:], K.ident[0:RT, 0:RT], start=False, stop=True).then_inc(st_done, 1)
                    if p == 0:
                        pe.wait_ge(mix_act, 4 * it + 2)
                        for c in range(KC):
                            m = pe.matmul(ps_m[:, c * RT:(c + 1) * RT], K.mkv[:, c, :], mq[:, c, :], start=True, stop=True)
                        m.then_inc(mix_mm, 1)
                    else:
                        pe.wait_ge(mix_act, 4 * it + 4)
                        pe.matmul(ps_m[0:RT, 0:D], K.ones[0:1, 0:RT], mb2[:], start=True, stop=False)
                        for c in range(KC):
                            m = pe.matmul(ps_m[0:RT, 0:D], mh[:, c, :], mw2[:, c, :], start=False, stop=c == KC - 1)
                        m.then_inc(mix_mm, 1)
                    pe.wait_ge(ex_ready, G + 1)
                    pe.transpose(ps_s[0:RT, RT:RT + P], ex[:], K.ident[:]).then_inc(ex_turned, 1)
                    for q in range(NQ):
                        Q = G * NQ + q
                        pe.wait_ge(vals_ready, 3 * (Q + 1))
                        for t in range(QT):
                            T = Q * QT + t
                            if again or p or q or t >= 2:
                                pe.wait_ge(row_ready, T - 1)
                            pe.matmul(ps_o[t % 2][0:RT, 0:RW], onehot[q % 2][:, t, :], vals[q % 2][:, t, :],
                                      start=True, stop=True).then_inc(out_done, 1)
                        pe.wait_ge(marks_ready, 4 * (Q + 1))
                        if again or p or q:
                            pe.wait_ge(count_ready, Q)
                        for a in range(2):
                            for t in range(QT):
                                m = pe.matmul(ps_n[0:RT, a * NT:(a + 1) * NT], olo[:, a, t, :], ohi[:, a, t, :],
                                              start=t == 0, stop=t == QT - 1)
                        m.then_inc(counted, 1)

            both(pe, turn)


def run_starts(nc, K):
    ctx, sb, ps, sem = stage(nc, "starts")
    with ctx:
        flat = sb("flat", [RT, NT])
        scan = sb("scan", [RT, NT])
        tot = sb("tot", [RT, NT])
        start = sb("start", [RT, NT])
        deg = sb("deg", [RT, NT])
        root = sb("root", [RT, NT])
        psA = ps("psA")
        psB = ps("psB")
        step = sem("step")
        mm = sem("mm")
        root_ready = sem("root_ready")
        block = ctx.enter_context(nc.Block())

        @block.tensor
        def _(pe):
            pe.matmul(psA[0:RT, 0:NT], K.tri[0:RT, 0:RT], K.hist[:, 1, :], start=True, stop=True).then_inc(mm, 1)
            pe.matmul(psB[0:RT, 0:NT], K.ones[0:RT, 0:RT], K.hist[:, 1, :], start=True, stop=True).then_inc(mm, 1)

        @block.vector
        def _(dve):
            dve.tensor_scalar(K.has[:], K.hist[:, 1, :], 0.0, None, ALU.is_gt).then_inc(step, 1)
            dve.tensor_scalar(deg[:], K.hist[:, 0, :], 1.0, None, ALU.max).then_inc(step, 1)
            dve.memset(flat[:], 1.0).then_inc(step, 1)
            dve.wait_ge(mm, 2)
            dve.tensor_copy(tot[:], psB[0:RT, 0:NT]).then_inc(step, 1)
            dve.wait_ge(step, 4)
            dve.tensor_tensor_scan(scan[:], flat[:], tot[:], 0.0, ALU.mult, ALU.add).then_inc(step, 1)
            dve.wait_ge(step, 5)
            dve.tensor_tensor(start[:], scan[:], tot[:], ALU.subtract).then_inc(step, 1)
            dve.wait_ge(step, 6)
            dve.tensor_tensor(scan[:], start[:], psA[0:RT, 0:NT], ALU.add).then_inc(step, 1)
            dve.wait_ge(step, 7)
            dve.tensor_scalar(start[:], scan[:], float(E - 1), None, ALU.min).then_inc(step, 1)
            dve.wait_ge(step, 8)
            dve.tensor_copy(K.start[:], start[:]).then_inc(step, 1)
            dve.wait_ge(root_ready, 1)
            dve.reciprocal(K.rdeg[:], root[:]).then_inc(step, 1)

        @block.scalar
        def _(act):
            act.wait_ge(step, 2)
            act.activation(root[:], deg[:], ACT.Sqrt).then_inc(root_ready, 1)


def run_scales(nc, K):
    ctx, sb, ps, sem = stage(nc, "scales")
    with ctx:
        first = sb("first", [H, ET])
        last = sb("last", [H, ET])
        cont = sb("cont", [H, ET + 1])
        single = sb("single", [H, ET])
        carry = sb("carry", [H, ET])
        fopen = sb("fopen", [H, ET])
        bopen = sb("bopen", [H, ET])
        fmx = sb("fmx", [H, ET])
        bmx = sb("bmx", [H, ET])
        top = sb("top", [H, ET])
        ff = sb("ff", [H, ET])
        fh = sb("fh", [H, ET])
        head = sb("head", [H, ET])
        psT = ps("psT")
        kept = sem("kept")
        t_in = sem("t_in")
        step = sem("step")
        exps = sem("exps")
        mm = sem("mm")
        block = ctx.enter_context(nc.Block())

        @block.sync
        def _(sp):
            sp.dma_start(K.mfirst_d, K.mfirst[:]).then_inc(kept, 16)
            sp.dma_start(K.mlast_d, K.mlast[:]).then_inc(kept, 16)
            sp.wait_ge(kept, 32)
            for dst, src in ((first, K.mfirst_d), (last, K.mlast_d)):
                sp.dma_start(dst[:].rearrange("h (t g) -> h t g", t=GT), src.rearrange("(t h) g -> h t g", h=H)).then_inc(t_in, 16)
            sp.dma_start(cont[:, 0:ET], bcast_row(K.cont_d, H)).then_inc(t_in, 16)
            sp.dma_start(single[:], bcast_row(K.single_d, H)).then_inc(t_in, 16)

        @block.vector
        def _(dve):
            n = 0

            def then(ins):
                nonlocal n
                n += 1
                ins.then_inc(step, 1)
                dve.wait_ge(step, n)

            then(dve.memset(cont[:, ET:ET + 1], 0.0))
            dve.wait_ge(t_in, 64)
            then(dve.tensor_copy(fmx[:].rearrange("h (g t) -> h t g", t=GT), first[:].rearrange("h (t g) -> h t g", t=GT)))
            then(dve.tensor_copy(bmx[:].rearrange("h (g t) -> h t g", t=GT), last[:].rearrange("h (t g) -> h t g", t=GT)))
            then(dve.tensor_copy(first[:], fmx[:]))
            then(dve.tensor_copy(last[:], bmx[:]))
            then(dve.tensor_tensor(carry[:], single[:], cont[:, 0:ET], ALU.mult))
            then(dve.tensor_scalar(fopen[:], carry[:], -1.0, BIG, ALU.add, ALU.mult))
            then(dve.tensor_tensor(bopen[:], single[:], cont[:, 1:ET + 1], ALU.mult))
            then(dve.tensor_scalar(bopen[:], bopen[:], -1.0, BIG, ALU.add, ALU.mult))
            then(dve.tensor_tensor_scan(fmx[:], fopen[:], last[:], -BIG, ALU.add, ALU.max))
            then(dve.tensor_tensor_scan(bmx[:, ::-1], bopen[:, ::-1], first[:, ::-1], -BIG, ALU.add, ALU.max))
            then(dve.tensor_copy(top[:], bmx[:]))
            then(dve.tensor_tensor(top[:, 1:ET], fmx[:, 0:ET - 1], bmx[:, 1:ET], ALU.max))
            then(dve.tensor_tensor(ff[:], first[:], top[:], ALU.subtract))
            then(dve.memset(fh[:, 0:1], 0.0))
            then(dve.tensor_tensor(fh[:, 1:ET], last[:, 0:ET - 1], top[:, 1:ET], ALU.subtract))
            then(dve.tensor_scalar(fh[:], fh[:], 0.0, None, ALU.min))
            then(dve.memset(head[:, 0:1], 0.0))
            then(dve.tensor_scalar(head[:, 1:ET], carry[:, 0:ET - 1], -1.0, 1.0, ALU.mult, ALU.add))
            then(dve.tensor_tensor(head[:], head[:], cont[:, 0:ET], ALU.mult))
            dve.wait_ge(exps, 2)
            then(dve.tensor_tensor(ff[:], ff[:], cont[:, 0:ET], ALU.mult))
            then(dve.tensor_tensor(fh[:], fh[:], head[:], ALU.mult))
            dve.wait_ge(mm, 1)
            then(dve.tensor_copy(K.join[:, :, 0:2 * H],
                                 psT[0:EP, 0:EK * 3 * H].rearrange("p (k j) -> p k j", j=3 * H)[:, :, 0:2 * H]))
            then(dve.tensor_copy(K.join[:, :, 2 * H:2 * H + 1],
                                 psT[0:EP, 0:EK * 3 * H].rearrange("p (k j) -> p k j", j=3 * H)[:, :, 2 * H:2 * H + 1]))

        @block.scalar
        def _(act):
            act.wait_ge(step, 17)
            act.activation(ff[:], ff[:], ACT.Exp).then_inc(exps, 1)
            act.activation(fh[:], fh[:], ACT.Exp).then_inc(exps, 1)

        @block.tensor
        def _(pe):
            pe.wait_ge(step, 22)
            for k in range(EK):
                for j, tab in enumerate((ff, fh, head)):
                    t = pe.transpose(psT[0:EP, (3 * k + j) * H:(3 * k + j + 1) * H],
                                     tab[:].rearrange("h (p k) -> h k p", k=EK)[:, k, :], K.ident[0:H, 0:H])
            t.then_inc(mm, 1)


def join_attention(nc, K, I):
    ctx, sb, ps, sem = stage(nc, "join")
    with ctx:
        wo = sb("wo", [P, KC, D])
        bo = sb("bo", [1, D])
        edge0 = sb("edge0", [EP, EK, RW])
        JW = RW + H + 1
        rhs = sb("rhs", [EP, EK, JW])
        dsh = [sb(f"dsh{b}", [EP, EK]) for b in range(2)]
        hot = [sb(f"hot{b}", [EP, EK, RT]) for b in range(2)]
        row = [sb(f"row{u}", [RT, RW]) for u in range(UN)]
        idx = [sb(f"idx{b}", [RT, UN], I32) for b in range(2)]
        fac = sb("fac", [RT, H])
        one = sb("one", [RT, 1])
        sums = sb("sums", [RT, RW])
        prod = sb("prod", [RT, RW])
        den = sb("den", [RT, H])
        rden = sb("rden", [RT, H])
        outn = [sb(f"outn{b}", [RT, D]) for b in range(2)]
        outt = [sb(f"outt{b}", [P, KC, RT]) for b in range(2)]
        psJ = [ps(f"psJ{b}") for b in range(2)]
        psT = ps("psT")
        psO = ps("psO")
        w_in = sem("w_in")
        idx_ready = sem("idx_ready")
        row_in = [sem(f"row_in{u}", kept=K.kept) for u in range(UN)]
        rhs_ready = sem("rhs_ready")
        dsh_ready = sem("dsh_ready")
        hot_ready = sem("hot_ready")
        joined = sem("joined")
        step = sem("step")
        turned = sem("turned")
        outt_ready = sem("outt_ready")
        out_done = sem("out_done")
        x_ready = sem("x_ready")
        block = ctx.enter_context(nc.Block())

        @block.sync
        def _(sp):
            load_chunks(sp, wo[:], I["L0_gnn_Wo"], w_in)
            sp.dma_start(bo[:], I["L0_gnn_bo"].rearrange("(o n) -> o n", o=1)).then_inc(w_in, 16)
            sp.dma_start(edge0[:], K.part_d.rearrange("(p k j) f -> p k j f", p=EP, j=RT)[:, :, 0, :]).then_inc(w_in, 16)

        @block.gpsimd
        def _(pool):
            def body(g, again):
                pool.wait_ge(idx_ready, g + 1)
                for u in range(UN):
                    if again:
                        pool.wait_ge(step, 8 * (g - 1) * UN + 8 * (u + 1))
                        pool.nop(nofuse=True)
                    elif u == 0:
                        pool.nop(nofuse=True)
                    pool.indirect_dma_start(row[u][:], None, K.part_d,
                                            bass.IndirectOffsetOnAxis(ap=idx[0][:, u:u + 1], axis=0)).then_inc(row_in[u], 16)

            turns(pool, body)

        @block.vector
        def _(dve):
            dve.wait_ge(w_in, 64 - 16)
            for k in range(EK):
                dve.tensor_tensor(rhs[:, k, 0:D].rearrange("p (h d) -> p h d", h=H),
                                  edge0[:, k, 0:D].rearrange("p (h d) -> p h d", h=H),
                                  K.join[:, k, 0:H].unsqueeze(2).to_broadcast([EP, H, HD]), ALU.mult).then_inc(rhs_ready, 1)
            dve.tensor_tensor(rhs[:, :, D:RW], edge0[:, :, D:RW], K.join[:, :, 0:H], ALU.mult).then_inc(rhs_ready, 1)
            dve.tensor_copy(rhs[:, :, RW:JW], K.join[:, :, H:2 * H + 1]).then_inc(rhs_ready, 1)

            def body(g, again):
                if again:
                    for u in range(UN):
                        dve.wait_ge(row_in[u], 16 * g)
                dve.tensor_copy(idx[0][:], K.start[:, bass.ds(g * UN, UN)]).then_inc(idx_ready, 1)
                for u in range(UN):
                    i = g * UN + u
                    dve.tensor_scalar(dsh[0][:], K.dfirst[:], K.tilebase[0:EP, bass.ds(i, 1)], None,
                                      ALU.subtract).then_inc(dsh_ready, 1)
                    dve.wait_ge(dsh_ready, i + 1)
                    if again or u:
                        dve.wait_ge(joined, i)
                    dve.tensor_tensor(hot[0][:], K.col[0:EP, 0:RT].unsqueeze(1).to_broadcast([EP, EK, RT]),
                                      dsh[0][:].unsqueeze(2).to_broadcast([EP, EK, RT]), ALU.is_equal).then_inc(hot_ready, 1)
                    dve.wait_ge(joined, i + 1)
                    J = psJ[0][0:RT, :]
                    dve.tensor_scalar(one[:], J[:, JW - 1:JW], -1.0, 1.0, ALU.mult, ALU.add).then_inc(step, 1)
                    dve.wait_ge(step, 8 * i + 1)
                    dve.tensor_scalar(fac[:], J[:, RW:RW + H], one[:], K.has[:, bass.ds(i, 1)], ALU.add, ALU.mult).then_inc(step, 1)
                    dve.wait_ge(step, 8 * i + 2)
                    dve.wait_ge(row_in[u], 16 * (g + 1))
                    dve.tensor_tensor(prod[:, 0:D].rearrange("p (h d) -> p h d", h=H),
                                      row[u][:, 0:D].rearrange("p (h d) -> p h d", h=H),
                                      fac[:].unsqueeze(2).to_broadcast([RT, H, HD]), ALU.mult).then_inc(step, 1)
                    dve.tensor_tensor(prod[:, D:RW], row[u][:, D:RW], fac[:], ALU.mult).then_inc(step, 1)
                    dve.wait_ge(step, 8 * i + 4)
                    dve.tensor_tensor(sums[:], prod[:], J[:, 0:RW], ALU.add).then_inc(step, 1)
                    dve.wait_ge(step, 8 * i + 5)
                    dve.tensor_scalar(den[:], sums[:, D:RW], 1e-30, None, ALU.max).then_inc(step, 1)
                    dve.wait_ge(step, 8 * i + 6)
                    dve.reciprocal(rden[:], den[:]).then_inc(step, 1)
                    dve.wait_ge(step, 8 * i + 7)
                    if again or u:
                        dve.wait_ge(turned, i)
                    dve.tensor_tensor(outn[0][:].rearrange("p (h d) -> p h d", h=H),
                                      sums[:, 0:D].rearrange("p (h d) -> p h d", h=H),
                                      rden[:].unsqueeze(2).to_broadcast([RT, H, HD]), ALU.mult).then_inc(step, 1)
                    if again or u:
                        add(i - 1)

            def add(i):
                dve.wait_ge(out_done, i + 1)
                xi = K.x[:, bass.ds(i, 1), :]
                dve.tensor_tensor(xi, xi, psO[0:RT, 0:D].rearrange("p (o d) -> p o d", o=1), ALU.add).then_inc(x_ready, 1)

            turns(dve, body)
            add(NT - 1)

        @block.scalar
        def _(act):
            def body(g, again):
                for u in range(UN):
                    i = g * UN + u
                    act.wait_ge(turned, i + 1)
                    if again or u:
                        act.wait_ge(out_done, i)
                    act.activation(outt[0][:], psT[:, 0:KC * RT].rearrange("p (c n) -> p c n", c=KC),
                                   ACT.Copy).then_inc(outt_ready, 1)

            turns(act, body)

        @block.tensor
        def _(pe):
            pe.wait_ge(w_in, 48)
            pe.wait_ge(rhs_ready, EK + 2)

            def body(g, again):
                for u in range(UN):
                    i = g * UN + u
                    pe.wait_ge(hot_ready, i + 1)
                    if again or u:
                        pe.wait_ge(step, 8 * i - 3)
                    for k in range(EK):
                        m = pe.matmul(psJ[0][0:RT, 0:JW], hot[0][:, k, :], rhs[:, k, :], start=k == 0, stop=k == EK - 1)
                    m.then_inc(joined, 1)
                    pe.wait_ge(step, 8 * i + 8)
                    if again or u:
                        pe.wait_ge(outt_ready, i)
                    for c in range(KC):
                        t = pe.transpose(psT[:, c * RT:(c + 1) * RT], outn[0][:, c * P:(c + 1) * P], K.ident[0:RT, 0:RT])
                    t.then_inc(turned, 1)
                    pe.wait_ge(outt_ready, i + 1)
                    if again or u:
                        pe.wait_ge(x_ready, i)
                    pe.matmul(psO[0:RT, 0:D], K.ones[0:1, 0:RT], bo[:], start=True, stop=False)
                    for c in range(KC):
                        m = pe.matmul(psO[0:RT, 0:D], outt[0][:, c, :], wo[:, c, :], start=False, stop=c == KC - 1)
                    m.then_inc(out_done, 1)

            turns(pe, body)


class Norm:

    def __init__(self, K, sb, ps, sem):
        self.K = K
        self.eps = sb("ln_eps", [RT, 1])
        self.xn = [sb(f"ln_xn{u}", [RT, D]) for u in range(UN)]
        self.xt = [sb(f"ln_xt{b}", [P, KC, RT]) for b in range(2)]
        self.stats = sb("ln_stats", [RT, UN, 6])
        self.mv = sb("ln_mv", [RT, UN, 2])
        self.dev = sb("ln_dev", [RT, UN])
        self.rdev = sb("ln_rdev", [RT, UN])
        self.psT = ps("ln_psT")
        self.eps_set = sem("ln_eps_set")
        self.step = sem("ln_step")
        self.dev_ready = sem("ln_dev_ready")
        self.xn_ready = sem("ln_xn_ready")
        self.turned = sem("ln_turned")
        self.xt_ready = sem("ln_xt_ready")

    def dve_begin(self, dve):
        dve.memset(self.eps[:], EPS).then_inc(self.eps_set, 1)

    def dve_group(self, dve, g, again):
        x = self.K.x
        if again:
            dve.wait_ge(self.turned, UN * g)
        for u in range(UN):
            dve.bn_stats(self.stats[:, u, :], x[:, bass.ds(g * UN + u, 1), :].rearrange("p o d -> p (o d)")
                         ).then_inc(self.step, 1)
        dve.wait_ge(self.step, 11 * g + 5)
        dve.nop(nofuse=True)
        for u in range(UN):
            dve.bn_aggr(self.mv[:, u, :], self.stats[:, u, :]).then_inc(self.step, 1)
        dve.wait_ge(self.dev_ready, g + 1)
        dve.reciprocal(self.rdev[:], self.dev[:]).then_inc(self.step, 1)
        dve.wait_ge(self.step, 11 * g + 11)
        for u in range(UN):
            dve.tensor_scalar(self.xn[u][:], x[:, bass.ds(g * UN + u, 1), :].rearrange("p o d -> p (o d)"),
                              self.mv[:, u, 0:1], self.rdev[:, u:u + 1], ALU.subtract, ALU.mult).then_inc(self.xn_ready, 1)

    def act_group(self, act, g, again):
        if not again:
            act.wait_ge(self.eps_set, 1)
        act.wait_ge(self.step, 11 * g + 10)
        act.activation(self.dev[:], self.mv[:, :, 1], ACT.Sqrt, bias=self.eps[:]).then_inc(self.dev_ready, 1)

    def act_tile(self, act, g, u, again, used, per=1):
        i = g * UN + u
        act.wait_ge(self.turned, i + 1)
        if again or u >= 2:
            act.wait_ge(used, per * (i - (u > 0)))
        act.activation(self.xt[u % 2][:], self.psT[:, 0:KC * RT].rearrange("p (c n) -> p c n", c=KC),
                       ACT.Copy).then_inc(self.xt_ready, 1)

    def pe_tile(self, pe, g, u, again, psT_read=None):
        i = g * UN + u
        pe.wait_ge(self.xn_ready, i + 1)
        if again or u:
            pe.wait_ge(self.xt_ready, i)
            if psT_read is not None:
                pe.wait_ge(psT_read, i)
        for c in range(KC):
            t = pe.transpose(self.psT[:, c * RT:(c + 1) * RT], self.xn[u][:, c * P:(c + 1) * P],
                             self.K.ident[0:RT, 0:RT])
        t.then_inc(self.turned, 1)
        pe.wait_ge(self.xt_ready, i + 1)


def route_experts(nc, K, I):
    ctx, sb, ps, sem = stage(nc, "route")
    with ctx:
        gw = sb("gw", [P, KC, EXPERTS])
        gb = sb("gb", [1, EXPERTS])
        zero = sb("zero", [RT, 4, D])
        xall = sb("xall", [RT, NT, D])
        TE = [RT, NT, EXPERTS]
        logit = sb("logit", TE)
        eid = sb("eid", TE)
        eid_i = sb("eid_i", TE, I32)
        cand = sb("cand", TE)
        hot = sb("hot", TE)
        ET_ = [RT, EXPERTS, NT]
        hote = sb("hote", ET_)
        keep = sb("keep", ET_)
        pref = sb("pref", ET_)
        tot = sb("tot", ET_)
        run = sb("run", ET_)
        big = sb("big", [RT, NT])
        best = sb("best", [RT, NT])
        expert = sb("expert", [RT, NT])
        pos = sb("pos", [RT, NT])
        kept = sb("kept", [RT, NT])
        slot = sb("slot", [RT, NT])
        esum = sb("esum", [RT, NT])
        place = sb("place", [RT, NT], I32)
        psL = ps("psL")
        psA = ps("psA")
        psB = ps("psB")
        norm = Norm(K, sb, ps, sem)
        w_in = sem("w_in")
        consts = sem("consts")
        kept_rows = sem("kept_rows")
        l_done = sem("l_done")
        l_ready = sem("l_ready")
        step = sem("step")
        exp_ready = sem("exp_ready")
        mm = sem("mm")
        zeroed = sem("zeroed")
        placed = sem("placed", kept=K.kept)
        ROUTED = 24
        block = ctx.enter_context(nc.Block())

        @block.sync
        def _(sp):
            load_chunks(sp, gw[:], I["L0_ffn_gate_w"], w_in)
            sp.dma_start(gb[:], I["L0_ffn_gate_b"].rearrange("(o n) -> o n", o=1)).then_inc(w_in, 16)
            sp.wait_ge(consts, 1)
            for e in range(EXPERTS):
                sp.dma_start(K.ebuf_d[e * CAPR:(e + 1) * CAPR, :].rearrange("(t p) d -> p t d", p=RT), zero[:]).then_inc(zeroed, 16)

        @block.gpsimd
        def _(pool):
            pool.memset(zero[:], 0.0).then_inc(consts, 1)
            pool.iota(eid_i[:], [[0, NT], [1, EXPERTS]], base=-EXPERTS, channel_multiplier=0).then_inc(consts, 1)

            def body(g, again):
                for u in range(UN):
                    pool.wait_ge(norm.xn_ready, g * UN + u + 1)
                    pool.tensor_copy(xall[:, bass.ds(g * UN + u, 1), :].rearrange("p o d -> p (o d)"), norm.xn[u][:]
                                     ).then_inc(kept_rows, 1)

            turns(pool, body)
            pool.wait_ge(kept_rows, NT)
            pool.wait_ge(zeroed, 16 * EXPERTS)
            pool.wait_ge(step, ROUTED)
            for i in range(NT):
                pool.indirect_dma_start(K.ebuf_d, bass.IndirectOffsetOnAxis(ap=place[:, i:i + 1], axis=0), xall[:, i, :], None,
                                        bounds_check=EXPERTS * CAPR - 1, oob_is_err=False).then_inc(placed, 16)
            pool.wait_ge(placed, 16 * NT)

        @block.vector
        def _(dve):
            norm.dve_begin(dve)

            def body(g, again):
                if again:
                    dve.wait_ge(kept_rows, UN * g)
                norm.dve_group(dve, g, again)
                for u in range(UN):
                    i = g * UN + u
                    dve.wait_ge(l_done, i + 1)
                    dve.tensor_copy(logit[:, bass.ds(i, 1), :].rearrange("p o e -> p (o e)"),
                                    psL[0:RT, 0:EXPERTS]).then_inc(l_ready, 1)

            turns(dve, body)
            n = 0

            def then(ins):
                nonlocal n
                n += 1
                ins.then_inc(step, 1)
                dve.wait_ge(step, n)

            def wide(t):
                return t[:].unsqueeze(2).to_broadcast(TE)

            dve.wait_ge(l_ready, NT)
            dve.wait_ge(consts, 2)
            then(dve.tensor_copy(eid[:], eid_i[:]))
            then(dve.tensor_reduce(big[:], logit[:], AX_X, ALU.max))
            then(dve.tensor_tensor(logit[:], logit[:], wide(big), ALU.subtract))
            then(dve.tensor_scalar(hot[:], logit[:], 0.0, None, ALU.is_equal))
            then(dve.tensor_tensor(cand[:], hot[:], eid[:], ALU.mult))
            then(dve.tensor_reduce(best[:], cand[:], AX_X, ALU.min))
            then(dve.tensor_tensor(hot[:], eid[:], wide(best), ALU.is_equal))
            then(dve.tensor_copy(hote[:].rearrange("p e i -> p i e"), hot[:]))
            dve.wait_ge(exp_ready, 1)
            then(dve.tensor_reduce(esum[:], cand[:], AX_X, ALU.add))
            then(dve.memset(keep[:], 1.0))
            then(dve.memset(keep[:, :, 0:1], 0.0))
            then(dve.reciprocal(K.prob[:], esum[:]))
            dve.wait_ge(mm, 2)
            flat = "p e i -> p (e i)"
            then(dve.tensor_copy(tot[:].rearrange(flat), psB[0:RT, 0:EXPERTS * NT]))
            then(dve.tensor_tensor_scan(run[:].rearrange(flat), keep[:].rearrange(flat), tot[:].rearrange(flat), 0.0,
                                        ALU.mult, ALU.add))
            then(dve.tensor_tensor(pref[:], run[:], tot[:], ALU.subtract))
            then(dve.tensor_tensor(pref[:].rearrange(flat), pref[:].rearrange(flat), psA[0:RT, 0:EXPERTS * NT], ALU.add))
            then(dve.tensor_tensor(run[:], pref[:], hote[:], ALU.mult))
            then(dve.tensor_reduce(pos[:], run[:].rearrange("p e i -> p i e"), AX_X, ALU.add))
            then(dve.tensor_scalar(expert[:], best[:], float(EXPERTS), float(CAPR), ALU.add, ALU.mult))
            then(dve.tensor_scalar(kept[:], pos[:], float(CAP), None, ALU.is_lt))
            then(dve.scalar_tensor_tensor(out=slot[:], in0=pos[:], scalar=float(CAP - 1), in1=expert[:], op0=ALU.min, op1=ALU.add))
            then(dve.tensor_copy(K.slot[:], slot[:]))
            then(dve.scalar_tensor_tensor(out=slot[:], in0=kept[:], scalar=-float(EXPERTS * CAPR), in1=slot[:],
                                          op0=ALU.mult, op1=ALU.add))
            then(dve.tensor_scalar(place[:], slot[:], float(EXPERTS * CAPR), None, ALU.add))
            assert n == ROUTED
            then(dve.tensor_tensor(K.prob[:], K.prob[:], kept[:], ALU.mult))

        @block.scalar
        def _(act):
            def body(g, again):
                norm.act_group(act, g, again)
                for u in range(UN):
                    norm.act_tile(act, g, u, again, l_done)

            turns(act, body)
            act.wait_ge(step, 8)
            act.activation(cand[:], logit[:], ACT.Exp).then_inc(exp_ready, 1)

        @block.tensor
        def _(pe):
            pe.wait_ge(w_in, 32)

            def body(g, again):
                for u in range(UN):
                    i = g * UN + u
                    norm.pe_tile(pe, g, u, again)
                    if again or u:
                        pe.wait_ge(l_ready, i)
                    pe.matmul(psL[0:RT, 0:EXPERTS], K.ones[0:1, 0:RT], gb[:], start=True, stop=False)
                    for c in range(KC):
                        m = pe.matmul(psL[0:RT, 0:EXPERTS], norm.xt[u % 2][:, c, :], gw[:, c, :], start=False, stop=c == KC - 1)
                    m.then_inc(l_done, 1)

            turns(pe, body)
            pe.wait_ge(step, 8)
            flat = hote[:].rearrange("p e i -> p (e i)")
            pe.matmul(psA[0:RT, 0:EXPERTS * NT], K.tri[0:RT, 0:RT], flat, start=True, stop=True).then_inc(mm, 1)
            pe.matmul(psB[0:RT, 0:EXPERTS * NT], K.ones[0:RT, 0:RT], flat, start=True, stop=True).then_inc(mm, 1)


def networks(nc, K, s, units, rt, weights, bias1, bias2, func, src, dst):
    ctx, sb, ps, sem = stage(nc, s)
    MT = UT
    UR = MT * rt
    shared = not callable(weights)
    nb = 1 if shared else units
    with ctx:
        nw = 1 if shared else 2
        w1 = [sb(f"w1{b}", [P, KC, FF]) for b in range(nw)]
        w2 = [sb(f"w2{b}", [P, FC, D]) for b in range(nw)]
        b1r = sb("b1r", [nb * FC, P])
        b1 = sb("b1", [P, nb * FC])
        b2 = sb("b2", [1, nb * D])
        rows = [sb(f"rows{b}", [rt, MT, D]) for b in range(2)]
        rowt = sb("rowt", [P, KC, UR])
        hid = sb("hid", [P, FC, UR])
        y = [sb(f"y{b}", [rt, D]) for b in range(2)]
        b1u = sb("b1u", [P, FC])
        b2u = sb("b2u", [1, D])
        psT = [ps(f"psT{b}") for b in range(KC)]
        psH = [ps(f"psH{b}") for b in range(2)]
        psY = [ps(f"psY{b}") for b in range(2)]
        w_in = [sem(f"w_in{b}") for b in range(nw)]
        b_in = sem("b_in")
        b1_turned = sem("b1_turned")
        b1_ready = sem("b1_ready")
        bu_ready = sem("bu_ready")
        rows_in = [sem(f"rows_in{b}") for b in range(2)]
        turned = sem("turned")
        rowt_ready = sem("rowt_ready")
        hid_done = sem("hid_done")
        hid_ready = sem("hid_ready")
        y_done = sem("y_done")
        y_ready = sem("y_ready")
        y_out = [sem(f"y_out{b}") for b in range(2)]
        block = ctx.enter_context(nc.Block())

        def w_slot(p):
            return 0 if shared else p

        def pairs(eng, turn):
            turn(0, False)
            with eng.Fori(1, units // 2) as it:
                turn(it, True)

        @block.sync
        def _(sp):
            def load_rows(e, p):
                sp.dma_start(rows[p][:], src[bass.ds(e * UR, UR), :].rearrange("(t p) d -> p t d", p=rt)).then_inc(rows_in[p], 16)

            def load_weights(e, p):
                m1, m2 = weights if shared else weights(e)
                sp.dma_start(w1[p][:], m1.rearrange("(c p) f -> p c f", p=P)).then_inc(w_in[p], 16)
                sp.dma_start(w2[p][:], m2.rearrange("(c p) d -> p c d", p=P)).then_inc(w_in[p], 16)

            sp.dma_start(b1r[:], bias1).then_inc(b_in, 16)
            sp.dma_start(b2[:], bias2).then_inc(b_in, 16)
            load_rows(0, 0)
            load_weights(0, 0)
            load_rows(1, 1)
            if not shared:
                load_weights(1, 1)

            def turn(it, more):
                for p in range(2):
                    e = it * 2 + p
                    if more:
                        sp.wait_ge(turned, KC * (e + 1))
                        load_rows(e + 2, p)
                    for t in range(MT):
                        Y = e * MT + t
                        sp.wait_ge(y_ready, Y + 1)
                        sp.dma_start(dst[bass.ds(Y * rt, rt), :], y[t % 2][:]).then_inc(y_out[t % 2], 16)
                    if more and not shared:
                        load_weights(e + 2, p)

            with sp.Fori(0, units // 2 - 1) as it:
                turn(it, True)
            turn(units // 2 - 1, False)
            for b in range(2):
                sp.wait_ge(y_out[b], 16 * units * MT // 2)

        @block.tensor
        def _(pe):
            pe.wait_ge(b_in, 32)
            pe.transpose(psT[0][:, 0:nb * FC], b1r[:], K.ident[0:nb * FC, 0:nb * FC]).then_inc(b1_turned, 1)
            pe.wait_ge(b1_ready, 1)

            def turn(it, again):
                for p in range(2):
                    e = it * 2 + p
                    pe.wait_ge(rows_in[p], 16 * (it + 1))
                    for c in range(KC):
                        if again or p:
                            pe.wait_ge(rowt_ready, KC * (e - 1) + c + 1)
                        for t in range(MT):
                            m = pe.transpose(psT[c][:, t * rt:(t + 1) * rt], rows[p][:, t, c * P:(c + 1) * P], K.ident[0:rt, 0:rt])
                        m.then_inc(turned, 1)
                    pe.wait_ge(w_in[w_slot(p)], 32 if shared else 32 * (it + 1))
                    pe.wait_ge(rowt_ready, KC * (e + 1))
                    for f in range(FC):
                        if again or p or f >= 2:
                            pe.wait_ge(hid_ready, FC * e + f - 1)
                        for c in range(KC):
                            m = pe.matmul(psH[f % 2][:, 0:UR], w1[w_slot(p)][:, c, f * P:(f + 1) * P], rowt[:, c, :],
                                          start=c == 0, stop=c == KC - 1)
                        m.then_inc(hid_done, 1)
                    pe.wait_ge(hid_ready, FC * (e + 1))
                    pe.wait_ge(bu_ready, 2 * (e + 1))
                    for t in range(MT):
                        if again or p or t >= 2:
                            pe.wait_ge(y_ready, MT * e + t - 1)
                        pe.matmul(psY[t % 2][0:rt, 0:D], K.ones[0:1, 0:rt], b2u[:], start=True, stop=False)
                        for f in range(FC):
                            m = pe.matmul(psY[t % 2][0:rt, 0:D], hid[:, f, t * rt:(t + 1) * rt], w2[w_slot(p)][:, f, :],
                                          start=False, stop=f == FC - 1)
                        m.then_inc(y_done, 1)

            pairs(pe, turn)

        @block.scalar
        def _(act):
            def turn(it, again):
                for p in range(2):
                    e = it * 2 + p
                    act.wait_ge(bu_ready, 2 * (e + 1))
                    for f in range(FC):
                        act.wait_ge(hid_done, FC * e + f + 1)
                        act.activation(hid[:, f, :], psH[f % 2][:, 0:UR], func, bias=b1u[:, f:f + 1]).then_inc(hid_ready, 1)

            pairs(act, turn)

        @block.vector
        def _(dve):
            dve.wait_ge(b1_turned, 1)
            dve.tensor_copy(b1[:], psT[0][:, 0:nb * FC]).then_inc(b1_ready, 1)
            dve.wait_ge(b1_ready, 1)

            def turn(it, again):
                for p in range(2):
                    e = it * 2 + p
                    if again or p:
                        dve.wait_ge(hid_ready, FC * e)
                        dve.wait_ge(y_done, MT * e)
                    eb = 0 if shared else e
                    dve.tensor_copy(b1u[:], b1[:, bass.ds(eb * FC, FC)]).then_inc(bu_ready, 1)
                    dve.tensor_copy(b2u[:], b2[:, bass.ds(eb * D, D)]).then_inc(bu_ready, 1)
                    for c in range(KC):
                        dve.wait_ge(turned, KC * e + c + 1)
                        if again or p:
                            dve.wait_ge(hid_done, FC * e)
                        dve.tensor_copy(rowt[:, c, :], psT[c][:, 0:UR]).then_inc(rowt_ready, 1)
                    for t in range(MT):
                        Y = e * MT + t
                        dve.wait_ge(y_done, Y + 1)
                        if again or p or t >= 2:
                            dve.wait_ge(y_out[t % 2], 16 * (2 * e + t // 2))
                        dve.tensor_copy(y[t % 2][:], psY[t % 2][0:rt, 0:D]).then_inc(y_ready, 1)

            pairs(dve, turn)


def take_experts(nc, K):
    ctx, sb, ps, sem = stage(nc, "take")
    with ctx:
        row = [sb(f"row{u}", [RT, D]) for u in range(UN)]
        idx = sb("idx", [RT, UN], I32)
        val = [sb(f"val{b}", [RT, D]) for b in range(2)]
        clean = [sb(f"clean{b}", [RT, D]) for b in range(2)]
        isnum = sb("isnum", [RT, D], I32)
        over = sb("over", [RT, D], I32)
        under = sb("under", [RT, D], I32)
        top = sb("top", [RT, 1])
        bottom = sb("bottom", [RT, 1])
        idx_ready = sem("idx_ready")
        row_in = [sem(f"row_in{u}", kept=K.kept) for u in range(UN)]
        consts = sem("consts")
        step = sem("step")
        x_ready = sem("x_ready")
        block = ctx.enter_context(nc.Block())

        @block.gpsimd
        def _(pool):
            def body(g, again):
                pool.wait_ge(idx_ready, g + 1)
                if again:
                    pool.wait_ge(step, 8 * UN * g)
                pool.nop(nofuse=True)
                for u in range(UN):
                    pool.indirect_dma_start(row[u][:], None, K.ey_d, bass.IndirectOffsetOnAxis(ap=idx[:, u:u + 1], axis=0)
                                            ).then_inc(row_in[u], 16)

            turns(pool, body)

        @block.vector
        def _(dve):
            dve.memset(top[:], 1e4).then_inc(consts, 1)
            dve.memset(bottom[:], -1e4).then_inc(consts, 1)
            dve.wait_ge(consts, 2)

            def body(g, again):
                dve.tensor_copy(idx[:], K.slot[:, bass.ds(g * UN, UN)]).then_inc(idx_ready, 1)
                for u in range(UN):
                    i = g * UN + u
                    v, c = val[0], clean[0]
                    if again or u:
                        dve.wait_ge(x_ready, i)
                    dve.memset(c[:], 0.0).then_inc(step, 1)
                    dve.wait_ge(row_in[u], 16 * (g + 1))
                    dve.tensor_scalar(v[:], row[u][:], K.prob[:, bass.ds(i, 1)], None, ALU.mult).then_inc(step, 1)
                    dve.wait_ge(step, 8 * i + 2)
                    dve.tensor_tensor(isnum[:], v[:], v[:], ALU.is_equal).then_inc(step, 1)
                    dve.tensor_scalar(over[:], v[:], 3.4028235e38, None, ALU.is_gt).then_inc(step, 1)
                    dve.tensor_scalar(under[:], v[:], -3.4028235e38, None, ALU.is_lt).then_inc(step, 1)
                    for n, (mask, data) in enumerate(((isnum, v[:]), (over, top[:].to_broadcast([RT, D])),
                                                      (under, bottom[:].to_broadcast([RT, D])))):
                        dve.wait_ge(step, 8 * i + 5 + n)
                        dve.nop(nofuse=True)
                        dve.copy_predicated(c[:], mask[:], data).then_inc(step, 1)
                    dve.wait_ge(step, 8 * i + 8)
                    xi = K.x[:, bass.ds(i, 1), :]
                    dve.tensor_tensor(xi, xi, c[:].rearrange("p (o d) -> p o d", o=1), ALU.add).then_inc(x_ready, 1)

            turns(dve, body)


def turn_weights(nc, K, I):
    ctx, sb, ps, sem = stage(nc, "wturn")
    with ctx:
        parts = [("L1_mix_Wqkv", 3 * D, K.wqkv_t), ("L1_mix_W1", D, K.w1_t), ("L1_mix_W2", D, K.w2_t)]
        raw = [sb(f"raw{n}", [P, rows // P, D]) for n, (_, rows, _) in enumerate(parts)]
        psW = [ps(f"psW{b}") for b in range(2)]
        w_in = sem("w_in")
        turned = sem("turned")
        ready = sem("ready")
        block = ctx.enter_context(nc.Block())
        jobs = [(n, c) for n, (_, rows, _) in enumerate(parts) for c in range(KC)]

        @block.sync
        def _(sp):
            for n, (name, rows, _) in enumerate(parts):
                sp.dma_start(raw[n][:], I[name].rearrange("(o p) i -> p o i", p=P)).then_inc(w_in, 16)

        rounds = [(n, c, o0, min(4, parts[n][1] // P - o0)) for n, c in jobs for o0 in range(0, parts[n][1] // P, 4)]

        @block.tensor
        def _(pe):
            pe.wait_ge(w_in, 16 * len(parts))
            for r, (n, c, o0, k) in enumerate(rounds):
                if r >= 2:
                    pe.wait_ge(ready, r - 1)
                for o in range(k):
                    t = pe.transpose(psW[r % 2][:, o * P:(o + 1) * P], raw[n][:, o0 + o, c * P:(c + 1) * P], K.ident[:])
                t.then_inc(turned, 1)

        @block.vector
        def _(dve):
            for r, (n, c, o0, k) in enumerate(rounds):
                dve.wait_ge(turned, r + 1)
                dve.tensor_copy(parts[n][2][:, c, o0 * P:(o0 + k) * P], psW[r % 2][:, 0:k * P]).then_inc(ready, 1)


def message_tables(nc, K, I):
    ctx, sb, ps, sem = stage(nc, "mtab")
    with ctx:
        norm = Norm(K, sb, ps, sem)
        frow = [sb(f"frow{b}", [RT, D]) for b in range(2)]
        low = sb("low", [RT, D])
        expk = sb("expk", [RT, D])
        kk = [sb(f"kk{b}", [RT, D]) for b in range(2)]
        vv = [sb(f"vv{b}", [RT, D]) for b in range(2)]
        blocks = sb("blocks", [P, P])
        headcol = sb("headcol", [P, KC, H])
        zero = sb("zero", [P, KC * (P + 1)])
        ksum = sb("ksum", [P, KC])
        psK = ps("psK")
        psS = ps("psS")
        consts = sem("consts")
        frow_ready = sem("frow_ready")
        f_out = [sem(f"f_out{b}") for b in range(2)]
        xn_kept = sem("xn_kept")
        xt_kept = sem("xt_kept")
        kv_done = sem("kv_done")
        low_ready = sem("low_ready")
        exp_ready = sem("exp_ready")
        kk_ready = sem("kk_ready")
        vv_ready = sem("vv_ready")
        summed = sem("summed")
        step = sem("step")
        block = ctx.enter_context(nc.Block())

        def slot_use(g, u):
            return g * (3 - u % 2) + u // 2

        @block.sync
        def _(sp):
            def body(g, again):
                for u in range(UN):
                    i = g * UN + u
                    sp.wait_ge(frow_ready, i + 1)
                    sp.dma_start(K.f_d[bass.ds(i * RT, RT), :], frow[u % 2][:]).then_inc(f_out[u % 2], 16)

            turns(sp, body)
            for b in range(2):
                sp.wait_ge(f_out[b], 16 * NG * (3 - b))

        @block.gpsimd
        def _(pool):
            pool.memset(blocks[:], 0.0).then_inc(consts, 1)
            pool.memset(headcol[:], 0.0).then_inc(consts, 1)
            pool.memset(zero[:], 0.0).then_inc(consts, 1)
            pool.wait_ge(consts, 3)
            for b in range(P // HD):
                pool.memset(blocks[b * HD:(b + 1) * HD, b * HD:(b + 1) * HD], 1.0).then_inc(consts, 1)
                for c in range(KC):
                    h = c * (P // HD) + b
                    pool.memset(headcol[b * HD:(b + 1) * HD, c, h:h + 1], 1.0).then_inc(consts, 1)
            pool.wait_ge(consts, 3 + (1 + KC) * P // HD)

            def body(g, again):
                for u in range(UN):
                    pool.wait_ge(norm.xn_ready, g * UN + u + 1)
                    pool.tensor_copy(K.xrow[:, bass.ds(g * UN + u, 1), :].rearrange("p o d -> p (o d)"), norm.xn[u][:]
                                     ).then_inc(xn_kept, 1)

            turns(pool, body)

        @block.vector
        def _(dve):
            norm.dve_begin(dve)

            def body(g, again):
                if again:
                    dve.wait_ge(xn_kept, UN * g)
                    dve.wait_ge(frow_ready, UN * g)
                norm.dve_group(dve, g, again)
                for u in range(UN):
                    i = g * UN + u
                    dve.wait_ge(norm.xn_ready, i + 1)
                    if again or u >= 2:
                        dve.wait_ge(f_out[u % 2], 16 * slot_use(g, u))
                    dve.tensor_scalar(frow[u % 2][:], norm.xn[u][:], K.rdeg[:, bass.ds(i, 1)], None, ALU.mult
                                      ).then_inc(frow_ready, 1)
                    dve.wait_ge(kv_done, i + 1)
                    dve.tensor_scalar(low[:], psK[0:RT, 0:D], 0.0, None, ALU.min).then_inc(low_ready, 1)
                    if again or u >= 2:
                        dve.wait_ge(summed, i - (u > 0))
                    dve.tensor_copy(vv[u % 2][:], psK[0:RT, D:2 * D]).then_inc(vv_ready, 1)
                    dve.wait_ge(exp_ready, i + 1)
                    dve.scalar_tensor_tensor(out=kk[u % 2][:], in0=psK[0:RT, 0:D], scalar=0.0, in1=expk[:],
                                             op0=ALU.max, op1=ALU.add).then_inc(kk_ready, 1)

            turns(dve, body)
            dve.wait_ge(summed, NT)
            dve.wait_ge(consts, 3 + (1 + KC) * P // HD)
            for c in range(KC):
                dve.tensor_tensor(K.mkv[:, c, :], psS[:, c * P:(c + 1) * P], blocks[:], ALU.mult).then_inc(step, 1)
            dve.tensor_copy(ksum[:], psS[:, KC * P:KC * P + KC]).then_inc(step, 1)
            dve.wait_ge(step, 3)
            for c in range(KC):
                dve.tensor_scalar(K.mks[:, c, :], headcol[:, c, :], ksum[:, c:c + 1], None, ALU.mult).then_inc(step, 1)

        @block.scalar
        def _(act):
            def body(g, again):
                norm.act_group(act, g, again)
                for u in range(UN):
                    i = g * UN + u
                    norm.act_tile(act, g, u, again, kv_done)
                    act.activation(K.xt[:, :, bass.ds(i * RT, RT)],
                                   norm.psT[:, 0:KC * RT].rearrange("p (c n) -> p c n", c=KC), ACT.Copy).then_inc(xt_kept, 1)
                    act.wait_ge(low_ready, i + 1)
                    if again or u:
                        act.wait_ge(kk_ready, i)
                    act.activation(expk[:], low[:], ACT.Exp).then_inc(exp_ready, 1)

            turns(act, body)

        @block.tensor
        def _(pe):
            pe.wait_ge(consts, 3)
            pe.matmul(psS[:, 0:KC * (P + 1)], zero[:, 0:P], zero[:], start=True, stop=False, skip_group_check=True)

            def accumulate(i, u, last=False):
                pe.wait_ge(kk_ready, i + 1)
                pe.wait_ge(vv_ready, i + 1)
                for c in range(KC):
                    kc = kk[u % 2][:, c * P:(c + 1) * P]
                    pe.matmul(psS[:, c * P:(c + 1) * P], kc, vv[u % 2][:, c * P:(c + 1) * P], start=False, stop=False,
                              skip_group_check=True)
                    m = pe.matmul(psS[:, KC * P + c:KC * P + c + 1], kc, K.ones[0:RT, 0:1], start=False,
                                  stop=last and c == KC - 1, skip_group_check=True)
                m.then_inc(summed, 1)

            def body(g, again):
                for u in range(UN):
                    i = g * UN + u
                    norm.pe_tile(pe, g, u, again, xt_kept)
                    if again or u:
                        pe.wait_ge(kk_ready, i)
                        pe.wait_ge(vv_ready, i)
                    for c in range(KC):
                        m = pe.matmul(psK[0:RT, :], norm.xt[u % 2][:, c, :], K.wqkv_t[:, c, D:3 * D], start=c == 0, stop=c == KC - 1)
                    m.then_inc(kv_done, 1)
                    if again or u:
                        accumulate(i - 1, (u - 1) % UN)

            turns(pe, body)
            accumulate(NT - 1, UN - 1, True)


def edge_messages(nc, K, I):
    ctx, sb, ps, sem = stage(nc, "msg")
    with ctx:
        idx = [sb(f"idx{p}", [RT, GT], I32) for p in range(2)]
        fr = [sb(f"fr{p}", [RT, GT, D]) for p in range(2)]
        onehot = [sb(f"onehot{b}", [RT, QT, RT]) for b in range(2)]
        rows = [sb(f"rows{b}", [RT, QT, D]) for b in range(2)]
        gb = sb("gb", [RT, 4, D])
        b1 = sb("b1", [P, KC])
        b2 = sb("b2", [1, D])
        eps = sb("eps", [RT, 2])
        qlow = sb("qlow", [P, KC, RT])
        qexp = sb("qexp", [P, KC, RT])
        qe = sb("qe", [P, KC, RT])
        den = sb("den", [RT, H])
        rden = sb("rden", [RT, H])
        t1 = sb("t1", [RT, D])
        t2 = sb("t2", [RT, D])
        x1 = sb("x1", [RT, D])
        x1t = sb("x1t", [P, KC, RT])
        mh = sb("mh", [P, KC, RT])
        t3 = sb("t3", [RT, D])
        st = sb("st", [RT, 6])
        mv = sb("mv", [RT, 2])
        dev = sb("dev", [RT, 1])
        rdev = sb("rdev", [RT, 1])
        ps_o = [ps(f"ps_o{b}") for b in range(4)]
        ps_m = ps("ps_m")
        w_in = sem("w_in")
        idx_ready = sem("idx_ready")
        rows_in = [[sem(f"rows_in{p}{q}", kept=K.kept) for q in range(NQ)] for p in range(2)]
        hot_ready = sem("hot_ready")
        out_done = sem("out_done")
        row_ready = sem("row_ready")
        rows_out = [sem(f"rows_out{b}") for b in range(2)]
        mix_mm = sem("mix_mm")
        mix_act = sem("mix_act")
        mix_dve = sem("mix_dve")
        MM, MA, MD = 5, 6, 20
        W_IN = 16 * (4 + KC + 1) + 1
        block = ctx.enter_context(nc.Block())
        TURNS = EG // 2

        def both(eng, turn):
            turn(0, False)
            with eng.Fori(1, TURNS) as it:
                turn(it, True)

        @block.sync
        def _(sp):
            for k, name in enumerate(("L1_mix_ln1_g", "L1_mix_ln1_b", "L1_mix_ln2_g", "L1_mix_ln2_b")):
                sp.dma_start(gb[:, k, :], bcast_row(I[name], RT)).then_inc(w_in, 16)
            load_cols(sp, b1[:], I["L1_mix_b1"], w_in)
            sp.dma_start(b2[:], I["L1_mix_b2"].rearrange("(o n) -> o n", o=1)).then_inc(w_in, 16)

            def turn(it, again):
                for p in range(2):
                    for q in range(NQ):
                        Q = (it * 2 + p) * NQ + q
                        sp.wait_ge(row_ready, QT * (Q + 1))
                        sp.dma_start(K.part1_d[bass.ds(Q * QT * RT, QT * RT), :].rearrange("(t j) f -> j t f", j=RT),
                                     rows[q % 2][:]).then_inc(rows_out[q % 2], 16)

            both(sp, turn)
            for b in range(2):
                sp.wait_ge(rows_out[b], 16 * EG * NQ // 2)

        @block.gpsimd
        def _(pool):
            def turn(it, again):
                for p in range(2):
                    G = it * 2 + p
                    pool.wait_ge(idx_ready, G + 1)
                    for q in range(NQ):
                        if again:
                            pool.wait_ge(out_done, QT * (NQ * (G - 2) + q + 1))
                        pool.nop(nofuse=True)
                        for t in range(q * QT, (q + 1) * QT):
                            pool.indirect_dma_start(fr[p][:, t, :], None, K.f_d,
                                                    bass.IndirectOffsetOnAxis(ap=idx[p][:, t:t + 1], axis=0)
                                                    ).then_inc(rows_in[p][q], 16)

            both(pool, turn)

        @block.vector
        def _(dve):
            dve.memset(eps[:], EPS).then_inc(w_in, 1)
            dve.wait_ge(w_in, W_IN)

            def indices(G, p):
                dve.tensor_copy(idx[p][:], K.src_t[:, bass.ds(G * GT, GT)]).then_inc(idx_ready, 1)

            def onehots(Q, p, q, again):
                if again or p or q >= 2:
                    dve.wait_ge(out_done, QT * (Q - 1))
                dve.tensor_tensor(onehot[q % 2][:], K.col[0:RT, 0:RT].unsqueeze(1).to_broadcast([RT, QT, RT]),
                                  K.seg_t[:, bass.ds(Q * QT, QT)].unsqueeze(2).to_broadcast([RT, QT, RT]),
                                  ALU.is_equal).then_inc(hot_ready, 1)

            def turn(it, again):
                if not again:
                    indices(0, 0)
                    indices(1, 1)
                n = 0

                def then(ins):
                    nonlocal n
                    n += 1
                    ins.then_inc(mix_dve, 1)
                    dve.wait_ge(mix_dve, MD * it + n)

                def layernorm(src, out, gain, act_step):
                    then(dve.bn_stats(st[:], src))
                    dve.nop(nofuse=True)
                    then(dve.bn_aggr(mv[:], st[:]))
                    dve.wait_ge(mix_act, MA * it + act_step)
                    then(dve.reciprocal(rdev[:], dev[:]))
                    then(dve.tensor_scalar(t1[:], src, mv[:, 0:1], rdev[:], ALU.subtract, ALU.mult))
                    then(dve.tensor_tensor(t1[:], t1[:], gb[:, gain, :], ALU.mult))
                    then(dve.tensor_tensor(out, t1[:], gb[:, gain + 1, :], ALU.add))

                xi = K.xrow[:, bass.ds(it, 1), :].rearrange("p o d -> p (o d)")

                def piece(k):
                    if k == 0:
                        dve.wait_ge(mix_mm, MM * it + 1)
                        pq = ps_m[:, 0:KC * RT].rearrange("p (c n) -> p c n", c=KC)
                        then(dve.tensor_scalar(qlow[:], pq, 0.0, None, ALU.min))
                        dve.wait_ge(mix_act, MA * it + 1)
                        then(dve.scalar_tensor_tensor(out=qe[:], in0=pq, scalar=0.0, in1=qexp[:], op0=ALU.max, op1=ALU.add))
                    if k == 1:
                        dve.wait_ge(mix_mm, MM * it + 2)
                        then(dve.tensor_scalar(den[:], ps_m[0:RT, D:D + H], 1e-6, None, ALU.add))
                        then(dve.reciprocal(rden[:], den[:]))
                        then(dve.tensor_tensor(t1[:].rearrange("p (h d) -> p h d", h=H),
                                               ps_m[0:RT, 0:D].rearrange("p (h d) -> p h d", h=H),
                                               rden[:].unsqueeze(2).to_broadcast([RT, H, HD]), ALU.mult))
                        then(dve.tensor_tensor(t2[:], t1[:], xi, ALU.add))
                    if k == 2:
                        layernorm(t2[:], x1[:], 0, 2)
                    if k == 6:
                        dve.wait_ge(mix_mm, MM * it + 5)
                        then(dve.tensor_tensor(t3[:], ps_m[0:RT, 0:D], x1[:], ALU.add))
                        layernorm(t3[:], t2[:], 2, 6)
                        xo = K.x[:, bass.ds(it, 1), :].rearrange("p o d -> p (o d)")
                        then(dve.tensor_tensor(xo, xo, t2[:], ALU.add))

                for p in range(2):
                    G = it * 2 + p
                    for q in range(NQ):
                        onehots(G * NQ + q, p, q, again)
                        piece(p * NQ + q)
                    for q in range(NQ):
                        dve.wait_ge(rows_in[p][q], QT * 16 * (it + 1))
                    indices(G + 2, p)
                assert n == MD, n

            both(dve, turn)

        @block.scalar
        def _(act):
            act.wait_ge(w_in, W_IN)

            def turn(it, again):
                def piece(k):
                    if k == 0:
                        act.wait_ge(mix_dve, MD * it + 1)
                        act.activation(qexp[:], qlow[:], ACT.Exp).then_inc(mix_act, 1)
                    if k == 2:
                        act.wait_ge(mix_dve, MD * it + 8)
                        act.activation(dev[:], mv[:, 1:2], ACT.Sqrt, bias=eps[:, 0:1]).then_inc(mix_act, 1)
                    if k == 4:
                        act.wait_ge(mix_mm, MM * it + 3)
                        act.activation(x1t[:], ps_m[:, 0:KC * RT].rearrange("p (c n) -> p c n", c=KC), ACT.Copy).then_inc(mix_act, 1)
                    if k == 5:
                        act.wait_ge(mix_mm, MM * it + 4)
                        for c in range(KC):
                            act.activation(mh[:, c, :], ps_m[:, c * RT:(c + 1) * RT], ACT.Gelu, bias=b1[:, c:c + 1]).then_inc(mix_act, 1)
                    if k == 7:
                        act.wait_ge(mix_dve, MD * it + 15)
                        act.activation(dev[:], mv[:, 1:2], ACT.Sqrt, bias=eps[:, 1:2]).then_inc(mix_act, 1)

                for p in range(2):
                    G = it * 2 + p
                    for q in range(NQ):
                        piece(p * NQ + q)
                        for t in range(QT):
                            T = (G * NQ + q) * QT + t
                            if t == 0 and (again or p or q >= 2):
                                act.wait_ge(rows_out[q % 2], 16 * (2 * G + q // 2))
                            act.wait_ge(out_done, T + 1)
                            act.activation(rows[q % 2][:, t, :], ps_o[t][0:RT, 0:D], ACT.Copy).then_inc(row_ready, 1)

            both(act, turn)

        @block.tensor
        def _(pe):
            pe.wait_ge(w_in, W_IN)

            def turn(it, again):
                def piece(k):
                    if k == 0:
                        if again:
                            pe.wait_ge(mix_dve, MD * it)
                        for co in range(KC):
                            for c in range(KC):
                                m = pe.matmul(ps_m[:, co * RT:(co + 1) * RT], K.wqkv_t[:, c, co * P:(co + 1) * P],
                                              K.xt[:, c, bass.ds(it * RT, RT)], start=c == 0, stop=c == KC - 1)
                        m.then_inc(mix_mm, 1)
                    if k == 1:
                        pe.wait_ge(mix_dve, MD * it + 2)
                        for c in range(KC):
                            pe.matmul(ps_m[0:RT, c * P:(c + 1) * P], qe[:, c, :], K.mkv[:, c, :], start=True, stop=True)
                        for c in range(KC):
                            m = pe.matmul(ps_m[0:RT, D:D + H], qe[:, c, :], K.mks[:, c, :], start=c == 0, stop=c == KC - 1)
                        m.then_inc(mix_mm, 1)
                    if k == 4:
                        pe.wait_ge(mix_dve, MD * it + 12)
                        for c in range(KC):
                            m = pe.transpose(ps_m[:, c * RT:(c + 1) * RT], x1[:, c * P:(c + 1) * P], K.ident[0:RT, 0:RT])
                        m.then_inc(mix_mm, 1)
                    if k == 5:
                        pe.wait_ge(mix_act, MA * it + 3)
                        for co in range(KC):
                            for c in range(KC):
                                m = pe.matmul(ps_m[:, co * RT:(co + 1) * RT], K.w1_t[:, c, co * P:(co + 1) * P], x1t[:, c, :],
                                              start=c == 0, stop=c == KC - 1)
                        m.then_inc(mix_mm, 1)
                    if k == 6:
                        pe.wait_ge(mix_act, MA * it + 5)
                        pe.matmul(ps_m[0:RT, 0:D], K.ones[0:1, 0:RT], b2[:], start=True, stop=False)
                        for c in range(KC):
                            m = pe.matmul(ps_m[0:RT, 0:D], mh[:, c, :], K.w2_t[:, c, :], start=False, stop=c == KC - 1)
                        m.then_inc(mix_mm, 1)

                for p in range(2):
                    G = it * 2 + p
                    for q in range(NQ):
                        Q = G * NQ + q
                        piece(p * NQ + q)
                        pe.wait_ge(hot_ready, Q + 1)
                        pe.wait_ge(rows_in[p][q], QT * 16 * (it + 1))
                        for t in range(QT):
                            if again or p or q:
                                pe.wait_ge(row_ready, Q * QT + t - 3)
                            pe.matmul(ps_o[t][0:RT, 0:D], onehot[q % 2][:, t, :], fr[p][:, q * QT + t, :],
                                      start=True, stop=True).then_inc(out_done, 1)

            both(pe, turn)


def join_messages(nc, K, I):
    ctx, sb, ps, sem = stage(nc, "mjoin")
    with ctx:
        w1 = sb("w1", [P, KC, D])
        w2 = sb("w2", [P, KC, D])
        b = sb("b", [1, D])
        edge0 = sb("edge0", [EP, EK, D])
        dsh = sb("dsh", [EP, EK])
        hot = sb("hot", [EP, EK, RT])
        row = [sb(f"row{u}", [RT, D]) for u in range(UN)]
        idx = sb("idx", [RT, UN], I32)
        hrd = sb("hrd", [RT, NT])
        own = sb("own", [RT, D])
        sums = sb("sums", [RT, D])
        part = sb("part", [RT, D])
        ab = [sb(f"ab{k}", [RT, D]) for k in range(2)]
        abt = sb("abt", [P, 2 * KC, RT])
        emb = sb("emb", [RT, D])
        emb2 = sb("emb2", [RT, D])
        sqr = sb("sqr", [RT, D])
        nn = sb("nn", [RT, 1])
        nrm = sb("nrm", [RT, 1])
        nrc = sb("nrc", [RT, 1])
        rn = sb("rn", [RT, 1])
        psJ = ps("psJ")
        psT = ps("psT")
        psE = ps("psE")
        w_in = sem("w_in")
        idx_ready = sem("idx_ready")
        row_in = [sem(f"row_in{u}", kept=K.kept) for u in range(UN)]
        joined = sem("joined")
        step = sem("step")
        turned = sem("turned")
        abt_ready = sem("abt_ready")
        emb_done = sem("emb_done")
        emb_read = sem("emb_read")
        nrm_ready = sem("nrm_ready")
        SN = 13
        block = ctx.enter_context(nc.Block())

        @block.sync
        def _(sp):
            load_chunks(sp, w1[:], I["L1_gnn_W1"], w_in)
            load_chunks(sp, w2[:], I["L1_gnn_W2"], w_in)
            sp.dma_start(b[:], I["L1_gnn_b"].rearrange("(o n) -> o n", o=1)).then_inc(w_in, 16)
            sp.dma_start(edge0[:], K.part1_d.rearrange("(p k j) f -> p k j f", p=EP, j=RT)[:, :, 0, :]).then_inc(w_in, 16)

        @block.gpsimd
        def _(pool):
            def body(g, again):
                pool.wait_ge(idx_ready, g + 1)
                if again:
                    pool.wait_ge(step, SN * UN * g)
                pool.nop(nofuse=True)
                for u in range(UN):
                    pool.indirect_dma_start(row[u][:], None, K.part1_d, bass.IndirectOffsetOnAxis(ap=idx[:, u:u + 1], axis=0)
                                            ).then_inc(row_in[u], 16)

            turns(pool, body)

        @block.vector
        def _(dve):
            dve.tensor_tensor(hrd[:], K.has[:], K.rdeg[:], ALU.mult).then_inc(emb_read, 1)
            dve.wait_ge(emb_read, 1)

            def body(g, again):
                dve.tensor_copy(idx[:], K.start[:, bass.ds(g * UN, UN)]).then_inc(idx_ready, 1)
                for u in range(UN):
                    i = g * UN + u
                    n = 0

                    def then(ins):
                        nonlocal n
                        n += 1
                        ins.then_inc(step, 1)
                        dve.wait_ge(step, SN * i + n)

                    xi = K.xrow[:, bass.ds(i, 1), :].rearrange("p o d -> p (o d)")
                    then(dve.tensor_scalar(dsh[:], K.dfirst[:], K.tilebase[0:EP, bass.ds(i, 1)], None, ALU.subtract))
                    then(dve.tensor_tensor(hot[:], K.col[0:EP, 0:RT].unsqueeze(1).to_broadcast([EP, EK, RT]),
                                           dsh[:].unsqueeze(2).to_broadcast([EP, EK, RT]), ALU.is_equal))
                    then(dve.tensor_scalar(own[:], xi, K.has[:, bass.ds(i, 1)], None, ALU.mult))
                    dve.wait_ge(row_in[u], 16 * (g + 1))
                    dve.wait_ge(joined, i + 1)
                    then(dve.tensor_tensor(sums[:], row[u][:], psJ[0:RT, 0:D], ALU.add))
                    then(dve.tensor_scalar(part[:], sums[:], hrd[:, bass.ds(i, 1)], None, ALU.mult))
                    then(dve.tensor_tensor(ab[0][:], own[:], part[:], ALU.add))
                    then(dve.tensor_tensor(ab[1][:], own[:], part[:], ALU.mult))
                    dve.wait_ge(emb_done, i + 1)
                    then(dve.tensor_copy(emb[:], psE[0:RT, 0:D]))
                    then(dve.scalar_tensor_tensor(out=emb2[:], in0=emb[:], scalar=0.01, in1=emb[:], op0=ALU.mult, op1=ALU.max))
                    dve.wait_ge(nrm_ready, 2 * i + 2)
                    then(dve.tensor_scalar(nrc[:], nrm[:], 1e-12, None, ALU.max))
                    then(dve.reciprocal(rn[:], nrc[:]))
                    xo = K.x[:, bass.ds(i, 1), :].rearrange("p o d -> p (o d)")
                    then(dve.scalar_tensor_tensor(out=xo, in0=emb2[:], scalar=rn[:], in1=xo, op0=ALU.mult, op1=ALU.add))
                    then(dve.memset(nrc[:], 0.0))
                    assert n == SN

            turns(dve, body)

        @block.scalar
        def _(act):
            def body(g, again):
                for u in range(UN):
                    i = g * UN + u
                    act.wait_ge(turned, i + 1)
                    if again or u:
                        act.wait_ge(emb_done, i)
                    act.activation(abt[:], psT[:, 0:2 * KC * RT].rearrange("p (c n) -> p c n", c=2 * KC), ACT.Copy).then_inc(abt_ready, 1)
                    act.wait_ge(step, SN * i + 9)
                    act.activation(sqr[:], emb2[:], ACT.Square, accum_out=nn[:]).then_inc(nrm_ready, 1)
                    act.wait_ge(nrm_ready, 2 * i + 1)
                    act.activation(nrm[:], nn[:], ACT.Sqrt).then_inc(nrm_ready, 1)

            turns(act, body)

        @block.tensor
        def _(pe):
            pe.wait_ge(w_in, 64)

            def body(g, again):
                for u in range(UN):
                    i = g * UN + u
                    pe.wait_ge(step, SN * i + 2)
                    for k in range(EK):
                        m = pe.matmul(psJ[0:RT, 0:D], hot[:, k, :], edge0[:, k, :], start=k == 0, stop=k == EK - 1)
                    m.then_inc(joined, 1)
                    pe.wait_ge(step, SN * i + 7)
                    for k in range(2):
                        for c in range(KC):
                            t = pe.transpose(psT[:, (KC * k + c) * RT:(KC * k + c + 1) * RT], ab[k][:, c * P:(c + 1) * P],
                                             K.ident[0:RT, 0:RT])
                    t.then_inc(turned, 1)
                    pe.wait_ge(abt_ready, i + 1)
                    pe.matmul(psE[0:RT, 0:D], K.ones[0:1, 0:RT], b[:], start=True, stop=False)
                    for k, w in enumerate((w1, w2)):
                        for c in range(KC):
                            m = pe.matmul(psE[0:RT, 0:D], abt[:, KC * k + c, :], w[:, c, :], start=False,
                                          stop=k == 1 and c == KC - 1)
                    m.then_inc(emb_done, 1)

            turns(pe, body)


def route_topk(nc, K, I):
    ctx, sb, ps, sem = stage(nc, "topk")
    with ctx:
        wr = sb("wr", [P, KC])
        br = sb("br", [1, 1])
        zero = sb("zero", [TKR, 2 * UT, D])
        xall = sb("xall", [RT, NT, D])
        wall = sb("wall", [RT, N])
        before = sb("before", [RT, 2 * N], BF16)
        junk = sb("junk", [RT, N], BF16)
        more = sb("more", [RT, NT])
        ties = sb("ties", [RT, NT])
        rank = sb("rank", [RT, NT])
        late = sb("late", [RT, NT])
        place = sb("place", [RT, NT], I32)
        psW = ps("psW")
        norm = Norm(K, sb, ps, sem)
        w_in = sem("w_in")
        consts = sem("consts")
        kept_rows = sem("kept_rows")
        summed = sem("summed")
        w_done = sem("w_done")
        w_ready = sem("w_ready")
        w_out = sem("w_out")
        wall_in = sem("wall_in")
        counted = sem("counted")
        step = sem("step")
        zeroed = sem("zeroed")
        placed = sem("placed", kept=K.kept)
        block = ctx.enter_context(nc.Block())

        @block.sync
        def _(sp):
            load_cols(sp, wr[:], I["L1_ffn_wr"].rearrange("n o -> (n o)"), w_in)
            sp.dma_start(br[:], I["L1_ffn_br"].rearrange("(o n) -> o n", o=1)).then_inc(w_in, 16)
            sp.wait_ge(consts, 1)
            for h in range(2):
                sp.dma_start(K.tbuf_d[h * 2 * UT * TKR:(h + 1) * 2 * UT * TKR, :].rearrange("(t p) d -> p t d", p=TKR),
                             zero[:]).then_inc(zeroed, 16)
            sp.wait_ge(w_ready, NT)
            for i in range(NT):
                sp.dma_start(K.w_d[i * RT:(i + 1) * RT].rearrange("(p o) -> p o", o=1), K.weight[:, i:i + 1]).then_inc(w_out, 16)
            sp.wait_ge(w_out, 16 * NT)
            sp.dma_start(wall[:], bcast_row(K.w_d, RT)).then_inc(wall_in, 16)

        @block.gpsimd
        def _(pool):
            pool.memset(zero[:], 0.0).then_inc(consts, 1)
            pool.memset(before[:, 0:N], 1.0).then_inc(consts, 1)
            pool.memset(before[:, N:2 * N], 0.0).then_inc(consts, 1)
            pool.wait_ge(consts, 3)
            pool.affine_select(out=before[:, N:N + RT], in_=before[:, N:N + RT], compare_op=ALU.is_ge, fill=1.0, base=0,
                               pattern=[[1, RT]], channel_multiplier=-1).then_inc(consts, 1)

            def body(g, again):
                for u in range(UN):
                    pool.wait_ge(norm.xn_ready, g * UN + u + 1)
                    pool.tensor_copy(xall[:, bass.ds(g * UN + u, 1), :].rearrange("p o d -> p (o d)"), norm.xn[u][:]
                                     ).then_inc(kept_rows, 1)

            turns(pool, body)
            pool.wait_ge(kept_rows, NT)
            pool.tensor_tensor(K.x[:], K.x[:], xall[:], ALU.add).then_inc(summed, 1)
            pool.wait_ge(zeroed, 32)
            pool.wait_ge(step, 4)
            for i in range(NT):
                pool.indirect_dma_start(K.tbuf_d, bass.IndirectOffsetOnAxis(ap=place[:, i:i + 1], axis=0), xall[:, i, :], None,
                                        bounds_check=TOPK - 1, oob_is_err=False).then_inc(placed, 16)
            pool.wait_ge(placed, 16 * NT)

        @block.vector
        def _(dve):
            norm.dve_begin(dve)

            def body(g, again):
                if again:
                    dve.wait_ge(kept_rows, UN * g)
                norm.dve_group(dve, g, again)
                for u in range(UN):
                    i = g * UN + u
                    dve.wait_ge(w_done, i + 1)
                    dve.tensor_copy(K.weight[:, bass.ds(i, 1)], psW[0:RT, 0:1]).then_inc(w_ready, 1)

            turns(dve, body)
            dve.wait_ge(w_ready, NT)
            dve.wait_ge(wall_in, 16)
            dve.wait_ge(consts, 4)

            def count(i, first):
                if not first:
                    dve.wait_ge(counted, 2 * i)
                w = K.weight[:, bass.ds(i, 1)]
                dve.tensor_scalar(junk[:], wall[:], w, 0.0, ALU.is_gt, ALU.add, accum_out=more[:, bass.ds(i, 1)]).then_inc(counted, 1)
                dve.wait_ge(counted, 2 * i + 1)
                dve.scalar_tensor_tensor(out=junk[:], in0=wall[:], scalar=w, in1=before[:, bass.ds(N - i * RT, N)],
                                         op0=ALU.is_equal, op1=ALU.mult, accum_out=ties[:, bass.ds(i, 1)]).then_inc(counted, 1)

            count(0, True)
            with dve.Fori(1, NT) as i:
                count(i, False)
            dve.wait_ge(counted, 2 * NT)
            dve.tensor_tensor(rank[:], more[:], ties[:], ALU.add).then_inc(step, 1)
            dve.wait_ge(step, 1)
            dve.tensor_scalar(late[:], rank[:], float(TOPK), None, ALU.is_ge).then_inc(step, 1)
            dve.wait_ge(step, 2)
            dve.scalar_tensor_tensor(out=late[:], in0=late[:], scalar=float(N), in1=rank[:], op0=ALU.mult, op1=ALU.add).then_inc(step, 1)
            dve.wait_ge(step, 3)
            dve.tensor_copy(place[:], late[:]).then_inc(step, 1)
            dve.tensor_copy(K.slot[:], late[:]).then_inc(step, 1)

        @block.scalar
        def _(act):
            def body(g, again):
                norm.act_group(act, g, again)
                for u in range(UN):
                    norm.act_tile(act, g, u, again, w_done)

            turns(act, body)

        @block.tensor
        def _(pe):
            pe.wait_ge(w_in, 48)

            def body(g, again):
                for u in range(UN):
                    i = g * UN + u
                    norm.pe_tile(pe, g, u, again)
                    if again or u:
                        pe.wait_ge(w_ready, i)
                    pe.matmul(psW[0:RT, 0:1], K.ones[0:1, 0:RT], br[:], start=True, stop=False)
                    for c in range(KC):
                        m = pe.matmul(psW[0:RT, 0:1], norm.xt[u % 2][:, c, :], wr[:, c:c + 1], start=False, stop=c == KC - 1)
                    m.then_inc(w_done, 1)

            turns(pe, body)


def take_topk(nc, K, out):
    ctx, sb, ps, sem = stage(nc, "last")
    with ctx:
        row = [sb(f"row{u}", [RT, D]) for u in range(UN)]
        idx = sb("idx", [RT, UN], I32)
        res = [sb(f"res{u}", [RT, D]) for u in range(UN)]
        idx_ready = sem("idx_ready")
        cleared = sem("cleared")
        row_in = [sem(f"row_in{u}", kept=K.kept) for u in range(UN)]
        res_ready = sem("res_ready")
        res_out = [sem(f"res_out{u}") for u in range(UN)]
        block = ctx.enter_context(nc.Block())
        out_v = out.rearrange("(i p) d -> i p d", p=RT)

        @block.gpsimd
        def _(pool):
            def body(g, again):
                pool.wait_ge(idx_ready, g + 1)
                pool.wait_ge(cleared, UN * (g + 1))
                pool.nop(nofuse=True)
                for u in range(UN):
                    pool.indirect_dma_start(row[u][:], None, K.ty_d, bass.IndirectOffsetOnAxis(ap=idx[:, u:u + 1], axis=0),
                                            bounds_check=TOPK - 1, oob_is_err=False).then_inc(row_in[u], 16)

            turns(pool, body)

        @block.vector
        def _(dve):
            def body(g, again):
                if again:
                    dve.wait_ge(res_ready, UN * g)
                dve.tensor_copy(idx[:], K.slot[:, bass.ds(g * UN, UN)]).then_inc(idx_ready, 1)
                for u in range(UN):
                    dve.memset(row[u][:], 0.0).then_inc(cleared, 1)
                for u in range(UN):
                    i = g * UN + u
                    dve.wait_ge(row_in[u], 16 * (g + 1))
                    if again:
                        dve.wait_ge(res_out[u], 16 * g)
                    dve.scalar_tensor_tensor(out=res[u][:], in0=row[u][:], scalar=K.weight[:, bass.ds(i, 1)],
                                             in1=K.x[:, bass.ds(i, 1), :].rearrange("p o d -> p (o d)"),
                                             op0=ALU.mult, op1=ALU.add).then_inc(res_ready, 1)

            turns(dve, body)

        @block.sync
        def _(sp):
            def body(g, again):
                for u in range(UN):
                    i = g * UN + u
                    sp.wait_ge(res_ready, i + 1)
                    sp.dma_start(out[bass.ds(i * RT, RT), :], res[u][:]).then_inc(res_out[u], 16)

            turns(sp, body)
            for u in range(UN):
                sp.wait_ge(res_out[u], 16 * NG)


def layer0_experts(nc, K, I):
    route_experts(nc, K, I)
    networks(nc, K, "ffn0", EXPERTS, RT,
             lambda e: tuple(I[w][bass.ds(e, 1)].rearrange("o a b -> (o a) b") for w in ("L0_ffn_w1", "L0_ffn_w2")),
             I["L0_ffn_b1"].rearrange("e (c p) -> (e c) p", p=P), I["L0_ffn_b2"].rearrange("(o e) d -> o (e d)", o=1),
             ACT.Relu, K.ebuf_d, K.ey_d)
    take_experts(nc, K)


def program(nc, I, out, dbg=None):
    dbg = dbg or {}
    ctx = ExitStack()
    with ctx:
        def sb(name, shape, dt=F32):
            return ctx.enter_context(nc.sbuf_tensor(f"all_{name}", shape, dt))

        def dram(name, shape, dt=F32):
            return nc.dram_tensor(f"scratch_{name}", shape, dt).ap()

        K = Kept(ctx)
        K.x = sb("x", [RT, NT, D])
        K.ident = sb("ident", [P, P])
        K.tri = sb("tri", [P, P])
        K.ones = sb("ones", [P, P])
        K.col = sb("col", [P, P])
        K.colb = sb("colb", [P, P], BF16)
        K.row_i = sb("row_i", [P, 1], I32)
        K.rowf = sb("rowf", [P, 1])
        K.src_t = sb("src_t", [RT, ET + 2 * GT], I32)
        K.dst_t = sb("dst_t", [RT, ET + 2 * GT], I32)
        K.hist = sb("hist", [RT, 2, NT])
        K.mfirst = sb("mfirst", [P, EG])
        K.mlast = sb("mlast", [P, EG])
        K.part_d = dram("part", [E, RW])
        K.ef = I["edge_attr_64"]
        K.has = sb("has", [RT, NT])
        K.start = sb("start", [RT, NT], I32)
        K.rdeg = sb("rdeg", [RT, NT])
        K.join = sb("join", [EP, EK, 2 * H + 1])
        K.tilebase = sb("tilebase", [P, NT])
        K.prob = sb("prob", [RT, NT])
        K.slot = sb("slot", [RT, NT], I32)
        K.ebuf_d = dram("ebuf", [EXPERTS * CAPR, D])
        K.ey_d = dram("ey", [EXPERTS * CAPR, D])
        K.f_d = dram("f", [N, D])
        K.part1_d = dram("part1", [E, D])
        K.tbuf_d = dram("tbuf", [UT * TU * TKR, D])
        K.ty_d = dram("ty", [UT * TU * TKR, D])
        K.w_d = dram("w", [N])
        K.mks = sb("mks", [P, KC, H])
        K.weight = sb("weight", [RT, NT])
        K.mfirst_d = dram("mfirst", [P, EG])
        K.mlast_d = dram("mlast", [P, EG])
        K.seg_t = sb("seg_t", [RT, ET], BF16)
        K.src_hi, K.src_lo, K.dst_hi, K.dst_lo = (sb(n, [RT, ET], BF16) for n in ("shi", "slo", "dhi", "dlo"))
        K.cont = sb("cont", [EP, EK])
        K.single = sb("single", [EP, EK])
        K.dfirst = sb("dfirst", [EP, EK])
        K.xt = sb("xt", [P, KC, N])
        K.mkv = sb("mkv", [P, KC, P])
        K.kv_d = dram("kv", [N, 2 * D])
        K.q_d = dram("q", [N, D])
        K.neg_d = dram("neg", [ET, RT + 1])
        K.cont_d = dram("cont", [ET])
        K.single_d = dram("single", [ET])
        prepare(nc, K, I)
        if "prep" in dbg:
            dump(nc, dbg["prep"], [K.seg_t, K.src_t, K.dst_t, K.cont, K.single, K.dfirst, K.src_hi, K.src_lo])
        node_tables(nc, K, I)
        if "tab" in dbg:
            dump(nc, dbg["tab"], [K.xt, K.mkv, K.x, K.kv_d, K.q_d])
        edge_attention(nc, K, I)
        if "edge" in dbg:
            dump(nc, dbg["edge"], [K.hist, K.mfirst, K.mlast, K.x, K.part_d])
        run_starts(nc, K)
        run_scales(nc, K)
        join_attention(nc, K, I)
        if "x1" in dbg:
            dump(nc, dbg["x1"], [K.x])
            return
        layer0_experts(nc, K, I)
        if "x2" in dbg:
            dump(nc, dbg["x2"], [K.x])
            return
        K.wqkv_t = sb("wqkv_t", [P, KC, 3 * D])
        K.w1_t = sb("w1_t", [P, KC, D])
        K.w2_t = sb("w2_t", [P, KC, D])
        K.xrow = sb("xrow", [RT, NT, D])
        turn_weights(nc, K, I)
        message_tables(nc, K, I)
        edge_messages(nc, K, I)
        join_messages(nc, K, I)
        if "x3" in dbg:
            dump(nc, dbg["x3"], [K.x])
            return
        route_topk(nc, K, I)
        networks(nc, K, "ffn1", TU, TKR, (I["L1_ffn_w1"], I["L1_ffn_w2"]),
                 I["L1_ffn_b1"].rearrange("(c p) -> c p", p=P), I["L1_ffn_b2"].rearrange("(o d) -> o d", o=1),
                 ACT.Gelu_apprx_tanh, K.tbuf_d, K.ty_d)
        take_topk(nc, K, out)


def dump(nc, outs, tabs):
    ctx, sb, ps, sem = stage(nc, "dump%d" % id(outs))
    with ctx:
        o = sem("o")
        block = ctx.enter_context(nc.Block())

        @block.sync
        def _(sp):
            for a, b in zip(outs, tabs):
                sp.dma_start(a, b if isinstance(b, bass.AP) else b[:]).then_inc(o, 16)
            sp.wait_ge(o, 16 * len(outs))


_OUT = ((N, D), "float32")
_INS = ["x", "src", "dst", "edge_attr_64", "L0_gnn_Wq", "L0_gnn_Wk", "L0_gnn_Wv", "L0_gnn_W1", "L0_gnn_b1", "L0_gnn_W2",
        "L0_gnn_b2", "L0_gnn_Wo", "L0_gnn_bo", "L0_mix_w_qkv", "L0_mix_b_qkv", "L0_mix_kln_g", "L0_mix_kln_b",
        "L0_mix_vln_g", "L0_mix_vln_b", "L0_mix_w1", "L0_mix_b1", "L0_mix_w2", "L0_mix_b2", "L0_ffn_gate_w",
        "L0_ffn_gate_b", "L0_ffn_w1", "L0_ffn_b1", "L0_ffn_w2", "L0_ffn_b2", "L1_gnn_W1", "L1_gnn_W2", "L1_gnn_b",
        "L1_mix_Wqkv", "L1_mix_ln1_g", "L1_mix_ln1_b", "L1_mix_W1", "L1_mix_b1", "L1_mix_W2", "L1_mix_b2",
        "L1_mix_ln2_g", "L1_mix_ln2_b", "L1_ffn_wr", "L1_ffn_br", "L1_ffn_w1", "L1_ffn_b1", "L1_ffn_w2", "L1_ffn_b2"]


def kernel(**inputs):
    import numpy as _np
    import concourse.bacc as _bacc
    from concourse import mybir as _mybir
    from concourse.bass_utils import run_bass_kernel_spmd as _run

    nc = _bacc.Bacc("TRN2", target_bir_lowering=False, num_devices=1)
    arrays, args = {}, {}
    for name in _INS:
        a = _np.ascontiguousarray(inputs[name])
        arrays[f"in_{name}_dram"] = a
        args[name] = nc.dram_tensor(f"in_{name}_dram", a.shape, _mybir.dt.from_np(a.dtype), kind="ExternalInput").ap()
    shape, dtype = _OUT
    out = nc.dram_tensor("out_0_dram", shape, _mybir.dt.from_np(_np.dtype(dtype)), kind="ExternalOutput").ap()
    program(nc, args, out)
    r = _run(nc, [arrays], core_ids=[0])
    return r.results[0]["out_0_dram"]
```

```python
from contextlib import ExitStack

import concourse.bass as bass
from concourse import mybir

F32 = mybir.dt.float32
BF16 = mybir.dt.bfloat16
I32 = mybir.dt.int32
ALU = mybir.AluOpType
ACT = mybir.ActivationFunctionType
AX_X = mybir.AxisListType.X

N, E, D, H, FE = 3125, 100000, 256, 8, 64
HD = D // H
P = 128
RT = 125
NT = N // RT
ET = E // RT
UN = 5
NG = NT // UN
GT = 16
EG = ET // GT
QT = 4
NQ = GT // QT
EP = 100
EK = ET // EP
KC = D // P
RW = D + H
BIG = 1.0e30
EPS = 1e-5
MAGIC = 12582912.0
EXPERTS, FF = 8, 1024
CAP = -(-5 * N // (4 * EXPERTS))
CAPR = 500
FC = FF // P
TOPK = N // 2 - 1
UT = 4
TU = 4
TKR = -(-TOPK // (UT * TU))

assert N % RT == 0 and E % RT == 0 and ET % GT == 0 and EG == 2 * NT and GT * H == P


class Kept:

    def __init__(self, kept):
        self.kept = kept


def stage(nc, s):
    ctx = ExitStack()

    def sb(name, shape, dt=F32):
        return ctx.enter_context(nc.sbuf_tensor(f"{s}_{name}", shape, dt))

    def ps(name, cols=512):
        return ctx.enter_context(nc.psum_tensor(f"{s}_{name}", [P, cols], F32))

    used = []

    def sem(name, kept=None):
        if kept is not None:
            return kept.enter_context(nc.semaphore(f"{s}_{name}"))
        used.append(ctx.enter_context(nc.semaphore(f"{s}_{name}")))
        return used[-1]

    def clear():
        nums = sorted(x.num for x in used)
        at = 0
        for n in range(1, len(nums) + 1):
            if n == len(nums) or nums[n] != nums[n - 1] + 1:
                nc.gpsimd.sem_clear(range(nums[at], nums[n - 1] + 1))
                at = n
        nc.all_engine_barrier()

    ctx.callback(clear)
    return ctx, sb, ps, sem


def bcast_row(ap1d, parts):
    return ap1d.rearrange("(o n) -> o n", o=1).to_broadcast([parts, ap1d.shape[0]])


def prepare(nc, K, I):
    ctx, sb, ps, sem = stage(nc, "prep")
    with ctx:
        src_i = sb("src_i", [EP, EK * RT], I32)
        dst_i = sb("dst_i", [EP, EK * RT], I32)
        prev_i = sb("prev_i", [EP, EK * RT], I32)
        pos_i = sb("pos_i", [EP, EK * RT], I32)
        base_i = sb("base_i", [EP, EK * RT], I32)
        col_i = sb("col_i", [P, P], I32)
        srcf = sb("srcf", [EP, EK * RT])
        dstf = sb("dstf", [EP, EK * RT])
        first = sb("first", [EP, EK * RT])
        mark = sb("mark", [EP, EK * RT])
        seg = sb("seg", [EP, EK * RT])
        seg0 = sb("seg0", [EP, EK * RT])
        neg = sb("neg", [EP, EK, RT + 1])
        stf = sb("stf", [RT, ET])
        dtf = sb("dtf", [RT, ET])
        tmp = sb("tmp", [RT, ET])
        tmp2 = sb("tmp2", [RT, ET])
        psT = [ps(f"psT{i}") for i in range(6)]
        edges_in = sem("edges_in")
        x_in = sem("x_in")
        zeroed = sem("zeroed")
        const_ready = sem("const_ready")
        step = sem("step")
        turned = sem("turned")
        spread = sem("spread")
        round_step = sem("round_step")
        neg_out = sem("neg_out")
        block = ctx.enter_context(nc.Block())
        e3 = "(p k) -> p k"

        @block.sync
        def _(sp):
            sp.dma_start(src_i[:], I["src"].rearrange(e3, p=EP)).then_inc(edges_in, 16)
            sp.dma_start(dst_i[:], I["dst"].rearrange(e3, p=EP)).then_inc(edges_in, 16)
            w = EK * RT
            sp.dma_start(prev_i[1:EP, :], I["dst"][w - 1:E - 1].rearrange(e3, p=EP - 1)).then_inc(edges_in, 16)
            sp.dma_start(prev_i[0:1, 1:w], I["dst"][0:w - 1].rearrange(e3, p=1)).then_inc(edges_in, 16)
            sp.dma_start(K.x[:], I["x"].rearrange("(i p) d -> p i d", p=RT)).then_inc(x_in, 16)
            sp.wait_ge(round_step, 5)
            sp.dma_start(K.neg_d.rearrange("(p k) j -> p k j", p=EP), neg[:]).then_inc(neg_out, 16)
            sp.wait_ge(round_step, 6)
            sp.dma_start(K.cont_d.rearrange(e3, p=EP), K.cont[:]).then_inc(neg_out, 16)
            sp.dma_start(K.single_d.rearrange(e3, p=EP), K.single[:]).then_inc(neg_out, 16)
            sp.wait_ge(neg_out, 48)
            sp.wait_ge(x_in, 16)

        @block.gpsimd
        def _(pool):
            pool.memset(K.ident[:], 0.0).then_inc(zeroed, 1)
            pool.memset(K.tri[:], 0.0).then_inc(zeroed, 1)
            pool.memset(K.ones[:], 1.0)
            pool.iota(pos_i[:], [[1, EK * RT]], base=0, channel_multiplier=0).then_inc(zeroed, 1)
            pool.iota(base_i[:], [[RT, EK], [0, RT]], base=0, channel_multiplier=0).then_inc(zeroed, 1)
            pool.iota(col_i[:], [[1, P]], base=0, channel_multiplier=0).then_inc(zeroed, 1)
            pool.iota(K.row_i[:], [[0, 1]], base=0, channel_multiplier=1).then_inc(zeroed, 1)
            pool.wait_ge(zeroed, 6)
            pool.affine_select(out=K.ident[:], in_=K.ident[:], compare_op=ALU.not_equal, fill=1.0, base=0,
                               pattern=[[-1, P]], channel_multiplier=1).then_inc(const_ready, 1)
            pool.affine_select(out=K.tri[:], in_=K.tri[:], compare_op=ALU.is_ge, fill=1.0, base=0,
                               pattern=[[-1, P]], channel_multiplier=1).then_inc(const_ready, 1)

        @block.vector
        def _(dve):
            dve.memset(prev_i[0:1, 0:1], -1).then_inc(step, 1)
            dve.memset(neg[:, :, RT:RT + 1], -BIG).then_inc(step, 1)
            dve.memset(K.src_t[:, ET:], 0)
            dve.memset(K.dst_t[:, ET:], 0)
            dve.wait_ge(edges_in, 64)
            dve.wait_ge(step, 1)
            dve.tensor_copy(srcf[:], src_i[:]).then_inc(step, 1)
            dve.tensor_copy(dstf[:], dst_i[:]).then_inc(step, 1)
            dve.tensor_tensor(first[:], dst_i[:], prev_i[:], ALU.not_equal).then_inc(step, 1)
            dve.wait_ge(step, 5)
            fv = first[:].rearrange("p (k j) -> p k j", j=RT)
            dve.tensor_scalar(K.cont[:], fv[:, :, 0], -1.0, 1.0, ALU.mult, ALU.add).then_inc(step, 1)
            dve.wait_ge(zeroed, 6)
            dve.tensor_copy(K.col[:], col_i[:]).then_inc(step, 1)
            dve.tensor_copy(K.colb[:], col_i[:]).then_inc(step, 1)
            dve.tensor_scalar(K.tilebase[:], col_i[:, 0:NT], float(RT), None, ALU.mult)
            dve.tensor_copy(K.rowf[:], K.row_i[:]).then_inc(step, 1)
            dve.tensor_copy(seg0[:], base_i[:]).then_inc(step, 1)
            dve.tensor_copy(seg[:], pos_i[:]).then_inc(step, 1)
            dve.wait_ge(step, 6)
            dve.memset(fv[:, :, 0:1], 1.0).then_inc(step, 1)
            dve.wait_ge(step, 12)
            dve.tensor_tensor(mark[:], first[:], seg[:], ALU.mult).then_inc(round_step, 1)
            dve.tensor_scalar(neg[:, :, 0:RT], fv, -BIG, None, ALU.mult).then_inc(round_step, 1)
            dve.wait_ge(round_step, 2)
            dve.tensor_tensor_scan(seg[:], mark[:], mark[:], 0.0, ALU.max, ALU.max).then_inc(round_step, 1)
            dve.wait_ge(round_step, 3)
            dve.tensor_tensor(mark[:], seg[:], seg0[:], ALU.subtract).then_inc(round_step, 1)
            dve.wait_ge(round_step, 4)
            mv = mark[:].rearrange("p (k j) -> p k j", j=RT)
            dve.tensor_scalar(K.single[:], mv[:, :, RT - 1], 0.0, None, ALU.is_equal).then_inc(round_step, 1)
            dv = dstf[:].rearrange("p (k j) -> p k j", j=RT)
            dve.scalar_tensor_tensor(out=K.dfirst[:], in0=dv[:, :, 0], scalar=1.0, in1=K.cont[:],
                                     op0=ALU.add, op1=ALU.mult).then_inc(round_step, 1)
            dve.wait_ge(round_step, 6)
            dve.tensor_scalar(K.dfirst[:], K.dfirst[:], -1.0, None, ALU.add).then_inc(round_step, 1)
            for n, (dsts, ints) in enumerate(((stf, K.src_t), (dtf, K.dst_t), (K.seg_t, None))):
                for b in range(2):
                    dve.wait_ge(turned, 2 * n + b + 1)
                    from_ps = psT[2 * n + b][0:RT, 0:4 * EP].rearrange("e (k p) -> e k p", k=4)
                    dve.tensor_copy(dsts[:].rearrange("e (p k) -> e k p", k=EK)[:, 4 * b:4 * b + 4, :],
                                    from_ps).then_inc(spread, 1)
                    if ints is not None:
                        dve.tensor_copy(ints[:, 0:ET].rearrange("e (p k) -> e k p", k=EK)[:, 4 * b:4 * b + 4, :],
                                        from_ps).then_inc(spread, 1)
            dve.wait_ge(spread, 10)
            k = 7
            for node, hi, lo in ((stf, K.src_hi, K.src_lo), (dtf, K.dst_hi, K.dst_lo)):
                dve.tensor_scalar(tmp[:], node[:], -float(RT // 2), 1.0 / RT, ALU.add, ALU.mult).then_inc(round_step, 1)
                dve.wait_ge(round_step, k + 1)
                dve.tensor_scalar(tmp2[:], tmp[:], MAGIC, None, ALU.add).then_inc(round_step, 1)
                dve.wait_ge(round_step, k + 2)
                dve.tensor_scalar(tmp[:], tmp2[:], -MAGIC, None, ALU.add).then_inc(round_step, 1)
                dve.wait_ge(round_step, k + 3)
                dve.tensor_copy(hi[:], tmp[:]).then_inc(round_step, 1)
                dve.scalar_tensor_tensor(out=lo[:], in0=tmp[:], scalar=-float(RT), in1=node[:],
                                         op0=ALU.mult, op1=ALU.add).then_inc(round_step, 1)
                dve.wait_ge(round_step, k + 5)
                k += 5

        @block.tensor
        def _(pe):
            pe.wait_ge(const_ready, 1)
            for n, (tab, s, v) in enumerate(((srcf, step, 3), (dstf, step, 4), (mark, round_step, 4))):
                pe.wait_ge(s, v)
                tv = tab[:].rearrange("p (k j) -> p k j", j=RT)
                for b in range(2):
                    for q in range(4):
                        t = pe.transpose(psT[2 * n + b][0:RT, q * EP:(q + 1) * EP], tv[:, 4 * b + q, :],
                                         K.ident[0:EP, 0:EP])
                    t.then_inc(turned, 1)


def turns(eng, body):
    body(0, False)
    with eng.Fori(1, NG) as g:
        body(g, True)


def load_chunks(sp, dst, src, done):
    sp.dma_start(dst, src.rearrange("(c p) n -> p c n", p=P)).then_inc(done, 16)


def load_cols(sp, dst, src, done):
    for c in range(src.shape[0] // P):
        sp.dma_start(dst[:, c:c + 1], src[c * P:(c + 1) * P].rearrange("(p o) -> p o", o=1)).then_inc(done, 16)


def slot_tiles(i, u):
    return i - (u > 0)


class Norm:

    def __init__(self, K, sb, ps, sem):
        self.K = K
        self.eps = sb("ln_eps", [RT, 1])
        self.xn = [sb(f"ln_xn{u}", [RT, D]) for u in range(UN)]
        self.xt = [sb(f"ln_xt{u}", [P, KC, RT]) for u in range(UN)]
        self.stats = sb("ln_stats", [RT, NT, 6])
        self.mv = sb("ln_mv", [RT, NT, 2])
        self.dev = sb("ln_dev", [RT, NT])
        self.rdev = sb("ln_rdev", [RT, NT])
        self.psT = [ps(f"ln_psT{b}") for b in range(2)]
        self.eps_set = sem("ln_eps_set")
        self.step = sem("ln_step")
        self.dev_ready = sem("ln_dev_ready")
        self.xn_ready = sem("ln_xn_ready")
        self.turned = sem("ln_turned")
        self.xt_ready = sem("ln_xt_ready")

    def dve_deviations(self, dve):
        dve.memset(self.eps[:], EPS).then_inc(self.eps_set, 1)
        with dve.Fori(0, NG) as g:
            for u in range(UN):
                i = g * UN + u
                dve.bn_stats(self.stats[:, bass.ds(i, 1), :].rearrange("p o s -> p (o s)"),
                             self.K.x[:, bass.ds(i, 1), :].rearrange("p o d -> p (o d)")).then_inc(self.step, 1)
        dve.wait_ge(self.step, NT)
        for i in range(NT):
            dve.bn_aggr(self.mv[:, i, :], self.stats[:, i, :]).then_inc(self.step, 1)
        dve.wait_ge(self.dev_ready, 1)
        dve.reciprocal(self.rdev[:], self.dev[:]).then_inc(self.step, 1)
        dve.wait_ge(self.step, 2 * NT + 1)

    def act_deviations(self, act):
        act.wait_ge(self.eps_set, 1)
        act.wait_ge(self.step, 2 * NT)
        act.activation(self.dev[:], self.mv[:, :, 1], ACT.Sqrt, bias=self.eps[:]).then_inc(self.dev_ready, 1)

    def dve_tile(self, dve, i, u, again):
        if again:
            dve.wait_ge(self.turned, i - (UN - 1))
        dve.tensor_scalar(self.xn[u][:], self.K.x[:, bass.ds(i, 1), :].rearrange("p o d -> p (o d)"),
                          self.mv[:, bass.ds(i, 1), 0:1].rearrange("p o s -> p (o s)"), self.rdev[:, bass.ds(i, 1)],
                          ALU.subtract, ALU.mult).then_inc(self.xn_ready, 1)

    def act_tile(self, act, i, u, again, used):
        act.wait_ge(self.turned, i + 1)
        if again:
            act.wait_ge(used, i - (UN - 1))
        act.activation(self.xt[u][:], self.psT[u % 2][:, 0:KC * RT].rearrange("p (c n) -> p c n", c=KC),
                       ACT.Copy).then_inc(self.xt_ready, 1)

    def pe_turn(self, pe, i, u, again, psT_read=None):
        pe.wait_ge(self.xn_ready, i + 1)
        if again or u >= 2:
            pe.wait_ge(psT_read or self.xt_ready, slot_tiles(i, u))
        for c in range(KC):
            t = pe.transpose(self.psT[u % 2][:, c * RT:(c + 1) * RT], self.xn[u][:, c * P:(c + 1) * P],
                             self.K.ident[0:RT, 0:RT])
        t.then_inc(self.turned, 1)


def staggered(eng, *parts):
    def step(i, parts):
        for do, lag in parts:
            j = i - lag
            if 0 <= j < NT:
                do(j // UN, j, j % UN, j >= UN)

    for i in range(2 * UN):
        step(i, parts)
    with eng.Fori(2, NG) as g:
        for u in range(UN):
            for do, lag in parts:
                do(g - 1 if u < lag else g, g * UN + u - lag, (u - lag) % UN, True)
    for i in range(NT, NT + max(lag for _, lag in parts)):
        step(i, parts)


def lagged(eng, first, later, lag):
    staggered(eng, (first, 0), (later, lag))


def node_tables(nc, K, I):
    ctx, sb, ps, sem = stage(nc, "tab")
    with ctx:
        wkv = sb("wkv", [P, KC, 2 * D])
        wq = sb("wq", [P, KC, D])
        wm = sb("wm", [P, KC, 2, D])
        bm = sb("bm", [1, 2, D])
        gam = sb("gam", [RT, 2, HD])
        bet = sb("bet", [RT, 2, HD])
        eps = sb("eps", [P, 1])
        zero = sb("zero", [P, D])
        blocks = sb("blocks", [P, P])
        norm = Norm(K, sb, ps, sem)
        kvrow = [sb(f"kvrow{b}", [RT, 2 * D]) for b in range(2)]
        qrow = [sb(f"qrow{b}", [RT, D]) for b in range(2)]
        cen = sb("cen", [RT, 2 * H, HD])
        sq = sb("sq", [RT, 2 * H, HD])
        hsum = sb("hsum", [RT, 2 * H])
        hmean = sb("hmean", [RT, 2 * H])
        hvar = sb("hvar", [RT, 2 * H])
        hdev = sb("hdev", [RT, 2 * H])
        hrdev = sb("hrdev", [RT, 2 * H])
        nrm = [sb(f"nrm{b}", [RT, 2 * H, HD]) for b in range(2)]
        sca = sb("sca", [RT, 2 * H, HD])
        kvn = [sb(f"kvn{b}", [RT, 2 * D]) for b in range(2)]
        psKV = [ps(f"psKV{b}") for b in range(2)]
        psQ = ps("psQ")
        psM = [ps(f"psM{b}") for b in range(2)]
        psS = ps("psS")
        w_in = sem("w_in")
        consts = sem("consts")
        xt_kept = sem("xt_kept")
        x_added = sem("x_added")
        kv_done = sem("kv_done")
        q_done = sem("q_done")
        m_done = sem("m_done")
        kv_taken = sem("kv_taken")
        q_taken = sem("q_taken")
        kv_out = [sem(f"kv_out{b}") for b in range(2)]
        q_out = [sem(f"q_out{b}") for b in range(2)]
        m_step = sem("m_step")
        hvar_ready = sem("hvar_ready")
        nrm_ready = sem("nrm_ready")
        mkv_ready = sem("mkv_ready")
        sq_ready = sem("sq_ready")
        hdev_ready = sem("hdev_ready")
        hrdev_done = sem("hrdev_done")
        sca_ready = sem("sca_ready")
        kvn_ready = sem("kvn_ready")
        summed = sem("summed")
        block = ctx.enter_context(nc.Block())

        @block.sync
        def _(sp):
            load_chunks(sp, wkv[:, :, 0:D], I["L0_gnn_Wk"], w_in)
            load_chunks(sp, wkv[:, :, D:2 * D], I["L0_gnn_Wv"], w_in)
            load_chunks(sp, wq[:], I["L0_gnn_Wq"], w_in)
            wv = I["L0_mix_w_qkv"].rearrange("(c p) (h t d) -> p c t h d", p=P, h=H, t=3)
            bv = I["L0_mix_b_qkv"].rearrange("(o h t d) -> o t h d", o=1, h=H, t=3)
            for t in range(2):
                for c in range(KC):
                    sp.dma_start(wm[:, c, t, :].rearrange("p (h d) -> p h d", h=H), wv[:, c, 1 + t]).then_inc(w_in, 16)
                sp.dma_start(bm[:, t, :].rearrange("p (h d) -> p h d", h=H), bv[:, 1 + t]).then_inc(w_in, 16)
            for t, (g, b) in enumerate((("L0_mix_kln_g", "L0_mix_kln_b"), ("L0_mix_vln_g", "L0_mix_vln_b"))):
                sp.dma_start(gam[:, t, :], bcast_row(I[g], RT)).then_inc(w_in, 16)
                sp.dma_start(bet[:, t, :], bcast_row(I[b], RT)).then_inc(w_in, 16)

            def store(g, again):
                for u in range(UN):
                    i = g * UN + u
                    sp.wait_ge(q_taken, i + 1)
                    sp.dma_start(K.q_d[bass.ds(i * RT, RT), :], qrow[u % 2][:]).then_inc(q_out[u % 2], 16)
                    sp.wait_ge(kv_taken, i + 1)
                    sp.dma_start(K.kv_d[bass.ds(i * RT, RT), :], kvrow[u % 2][:]).then_inc(kv_out[u % 2], 16)

            turns(sp, store)
            for b in range(2):
                sp.wait_ge(kv_out[b], 16 * NG * (3 - b))
                sp.wait_ge(q_out[b], 16 * NG * (3 - b))

        def slot_use(g, u):
            return g * (3 - u % 2) + u // 2

        W_IN = 16 * (3 + 6 + 4)

        @block.gpsimd
        def _(pool):
            pool.memset(zero[:], 0.0).then_inc(consts, 1)
            pool.memset(eps[:], EPS).then_inc(consts, 1)
            pool.memset(blocks[:], 0.0).then_inc(consts, 1)
            pool.wait_ge(consts, 3)
            for b in range(P // HD):
                pool.memset(blocks[b * HD:(b + 1) * HD, b * HD:(b + 1) * HD], 1.0 / N).then_inc(consts, 1)
            pool.wait_ge(consts, 3 + P // HD)
            pool.wait_ge(w_in, W_IN)

            def add_x(g, i, u, again):
                pool.wait_ge(norm.xn_ready, i + 1)
                pool.tensor_tensor(K.x[:, bass.ds(i, 1), :], K.x[:, bass.ds(i, 1), :],
                                   norm.xn[u][:].rearrange("p (o d) -> p o d", o=1), ALU.add).then_inc(x_added, 1)

            def affine(g, i, u, again):
                pool.wait_ge(nrm_ready, i + 1)
                if again or u:
                    pool.wait_ge(kvn_ready, 2 * i)
                for t in range(2):
                    pool.tensor_tensor(sca[:, t * H:(t + 1) * H, :], nrm[u % 2][:, t * H:(t + 1) * H, :],
                                       gam[:, t:t + 1, :].to_broadcast([RT, H, HD]), ALU.mult).then_inc(sca_ready, 1)
                pool.wait_ge(sca_ready, 2 * i + 2)
                if again or u >= 2:
                    pool.wait_ge(summed, slot_tiles(i, u))
                for t in range(2):
                    pool.tensor_tensor(kvn[u % 2][:, t * D:(t + 1) * D].rearrange("p (h d) -> p h d", h=H),
                                       sca[:, t * H:(t + 1) * H, :],
                                       bet[:, t:t + 1, :].to_broadcast([RT, H, HD]), ALU.add).then_inc(kvn_ready, 1)

            staggered(pool, (add_x, 0), (affine, 3))

        @block.vector
        def _(dve):
            norm.dve_deviations(dve)

            def invert(g, i, u, again):
                dve.wait_ge(hdev_ready, i + 1)
                dve.reciprocal(hrdev[:], hdev[:]).then_inc(hrdev_done, 1)
                dve.wait_ge(hrdev_done, i + 1)
                if again or u >= 2:
                    dve.wait_ge(sca_ready, 2 * slot_tiles(i, u))
                dve.tensor_tensor(nrm[u % 2][:], cen[:], hrdev[:].unsqueeze(2).to_broadcast([RT, 2 * H, HD]),
                                  ALU.mult).then_inc(nrm_ready, 1)

            def centre(g, i, u, again):
                dve.wait_ge(kv_done, i + 1)
                if again or u >= 2:
                    dve.wait_ge(kv_out[u % 2], slot_use(g, u) * 16)
                dve.tensor_copy(kvrow[u % 2][:], psKV[u % 2][0:RT, :]).then_inc(kv_taken, 1)
                dve.wait_ge(m_done, i + 1)
                m3 = psM[u % 2][0:RT, :].rearrange("p (h d) -> p h d", d=HD)
                dve.tensor_reduce(hsum[:], m3, AX_X, ALU.add).then_inc(m_step, 1)
                dve.wait_ge(m_step, 3 * i + 1)
                dve.tensor_scalar(hmean[:], hsum[:], 1.0 / HD, None, ALU.mult).then_inc(m_step, 1)
                dve.wait_ge(m_step, 3 * i + 2)
                if again or u:
                    dve.wait_ge(nrm_ready, i)
                dve.tensor_tensor(cen[:], m3, hmean[:].unsqueeze(2).to_broadcast([RT, 2 * H, HD]),
                                  ALU.subtract).then_inc(m_step, 1)

            def normalise(g, i, u, again):
                if again:
                    dve.wait_ge(x_added, i - (UN - 1))
                norm.dve_tile(dve, i, u, again)

            def variance(g, i, u, again):
                dve.wait_ge(sq_ready, i + 1)
                dve.tensor_reduce(hvar[:], sq[:], AX_X, ALU.add).then_inc(hvar_ready, 1)

            staggered(dve, (normalise, 0), (invert, 3), (centre, 2), (variance, 2))
            dve.wait_ge(summed, NT)
            dve.wait_ge(consts, 3 + P // HD)
            for c in range(KC):
                dve.tensor_tensor(K.mkv[:, c, :], psS[:, c * P:(c + 1) * P], blocks[:], ALU.mult).then_inc(mkv_ready, 1)

        @block.scalar
        def _(act):
            act.wait_ge(consts, 3)

            norm.act_deviations(act)

            def turn(g, i, u, again):
                norm.act_tile(act, i, u, again, m_done)
                act.activation(K.xt[:, :, bass.ds(i * RT, RT)],
                               norm.psT[u % 2][:, 0:KC * RT].rearrange("p (c n) -> p c n", c=KC), ACT.Copy).then_inc(xt_kept, 1)

            def queries(g, i, u, again):
                act.wait_ge(q_done, i + 1)
                if again or u >= 2:
                    act.wait_ge(q_out[u % 2], slot_use(g, u) * 16)
                act.activation(qrow[u % 2][:], psQ[0:RT, 0:D], ACT.Copy, scale=float(HD) ** -0.5).then_inc(q_taken, 1)

            def squares(g, i, u, again):
                act.wait_ge(m_step, 3 * i + 3)
                if again or u:
                    act.wait_ge(hvar_ready, i)
                act.activation(sq[:], cen[:], ACT.Square).then_inc(sq_ready, 1)
                act.wait_ge(hvar_ready, i + 1)
                if again or u:
                    act.wait_ge(hrdev_done, i)
                act.activation(hdev[:], hvar[:], ACT.Sqrt, bias=eps[0:RT, :], scale=1.0 / HD).then_inc(hdev_ready, 1)

            staggered(act, (turn, 0), (squares, 2), (queries, 1))

        @block.tensor
        def _(pe):
            pe.wait_ge(w_in, W_IN)
            pe.wait_ge(consts, 1)
            pe.matmul(psS[:, 0:D], zero[:, 0:P], zero[:], start=True, stop=False, skip_group_check=True)

            def turn(g, i, u, again):
                norm.pe_turn(pe, i, u, again, xt_kept)

            def products(g, i, u, again):
                xt = norm.xt[u]
                pe.wait_ge(norm.xt_ready, i + 1)
                if again or u >= 2:
                    pe.wait_ge(kv_taken, slot_tiles(i, u))
                for c in range(KC):
                    m = pe.matmul(psKV[u % 2][0:RT, :], xt[:, c, :], wkv[:, c, :], start=c == 0, stop=c == KC - 1)
                m.then_inc(kv_done, 1)
                if again or u:
                    pe.wait_ge(q_taken, i)
                for c in range(KC):
                    m = pe.matmul(psQ[0:RT, 0:D], xt[:, c, :], wq[:, c, :], start=c == 0, stop=c == KC - 1)
                m.then_inc(q_done, 1)
                if again or u >= 2:
                    pe.wait_ge(m_step, 3 * slot_tiles(i, u))
                M = psM[u % 2][0:RT, :]
                pe.matmul(M, K.ones[0:1, 0:RT], bm[:].rearrange("p t n -> p (t n)"), start=True, stop=False)
                for c in range(KC):
                    m = pe.matmul(M, xt[:, c, :], wm[:, c, :, :].rearrange("p t n -> p (t n)"),
                                  start=False, stop=c == KC - 1)
                m.then_inc(m_done, 1)

            def accumulate(g, i, u, again):
                pe.wait_ge(kvn_ready, 2 * i + 2)
                for c in range(KC):
                    m = pe.matmul(psS[:, c * P:(c + 1) * P], kvn[u % 2][:, c * P:(c + 1) * P],
                                  kvn[u % 2][:, D + c * P:D + (c + 1) * P], start=False, stop=isinstance(i, int) and i == NT - 1,
                                  skip_group_check=True)
                m.then_inc(summed, 1)

            staggered(pe, (turn, 0), (products, 1), (accumulate, 4))


def edge_attention(nc, K, I):
    ctx, sb, ps, sem = stage(nc, "edge")
    with ctx:
        w1 = sb("w1", [P, D])
        b1 = sb("b1", [P, KC])
        w2z = sb("w2z", [P, KC, (2 * GT - 1) * H])
        b2 = sb("b2", [P, 1])
        idx_s = [sb(f"idx_s{p}", [RT, GT], I32) for p in range(2)]
        idx_d = [sb(f"idx_d{p}", [RT, GT], I32) for p in range(2)]
        kv = [sb(f"kv{p}", [RT, GT, 2 * D]) for p in range(2)]
        qr = sb("qr", [RT, NQ, D * QT])
        ef = sb("ef", [RT, GT, FE])
        neg = [sb(f"neg{p}", [P, RT + 1]) for p in range(2)]
        eft = sb("eft", [P, GT // 2, RT])
        hid = sb("hid", [P, KC, GT // 2, 2, RT])
        sc = sb("sc", [RT, GT * H])
        st = sb("st", [P, RT])
        fmx = sb("fmx", [P, RT])
        gmx = sb("gmx", [P, RT])
        ex = sb("ex", [P, RT])
        exg = sb("exg", [RT, GT * H])
        vals = [sb(f"vals{b}", [RT, QT, RW]) for b in range(2)]
        onehot = [sb(f"onehot{b}", [RT, QT, RT]) for b in range(2)]
        rows = [sb(f"rows{b}", [RT, 2, RW]) for b in range(2)]
        olo = sb("olo", [RT, 2, QT, RT], BF16)
        ohi = sb("ohi", [RT, 2, QT, NT], BF16)
        ps_et = ps("ps_et")
        ps_h = [ps(f"ps_h{b}") for b in range(2)]
        ps_s = ps("ps_s")
        ps_n = ps("ps_n")
        EC = 64
        ps_o = [ps(f"ps_o{b}") for b in range(2)]
        ps_m = ps("ps_m")
        mwq = sb("mwq", [P, KC, D])
        mbq = sb("mbq", [P, KC])
        mw1 = sb("mw1", [P, KC, D])
        mb1 = sb("mb1", [P, KC])
        mw2 = sb("mw2", [P, KC, D])
        mb2 = sb("mb2", [1, D])
        mq = sb("mq", [P, KC, RT])
        mr = sb("mr", [P, KC, RT])
        mh = mq
        w_in = sem("w_in")
        mbq_in = sem("mbq_in")
        w2_zeroed = sem("w2_zeroed")
        hist_zeroed = sem("hist_zeroed")
        idx_ready = sem("idx_ready")
        rows_in = [[sem(f"rows_in{p}{q}", kept=K.kept) for q in range(NQ)] for p in range(2)]
        ef_in = sem("ef_in")
        neg_in = [sem(f"neg_in{p}") for p in range(2)]
        ef_turned = sem("ef_turned")
        eft_ready = sem("eft_ready")
        hid_done = sem("hid_done")
        hid_ready = sem("hid_ready")
        prod_ready = sem("prod_ready")
        sc_ready = sem("sc_ready")
        st_done = sem("st_done")
        st_ready = sem("st_ready")
        fmx_ready = sem("fmx_ready")
        gmx_ready = sem("gmx_ready")
        dif_ready = sem("dif_ready")
        max_kept = sem("max_kept")
        ex_ready = sem("ex_ready")
        ex_turned = sem("ex_turned")
        exg_ready = sem("exg_ready")
        vals_ready = sem("vals_ready")
        out_done = sem("out_done")
        row_ready = sem("row_ready")
        rows_out = [sem(f"rows_out{b}") for b in range(2)]
        marks_ready = sem("marks_ready")
        counted = sem("counted")
        count_ready = sem("count_ready")
        mix_mm = sem("mix_mm")
        mix_act = sem("mix_act")
        mix_dve = sem("mix_dve")
        block = ctx.enter_context(nc.Block())
        W_IN = 16 * (2 + KC + KC + GT + KC + 2 + KC + 1)
        TURNS = EG // 2

        def both(eng, turn):
            turn(0, False)
            with eng.Fori(1, TURNS) as it:
                turn(it, True)

        def ahead(eng, turn):
            turn(0, False, True)
            with eng.Fori(1, TURNS - 1) as it:
                turn(it, True, True)
            turn(TURNS - 1, True, False)

        @block.sync
        def _(sp):
            for half in range(2):
                sp.dma_start(w1[half * FE:(half + 1) * FE, :], I["L0_gnn_W1"]).then_inc(w_in, 16)
            sp.wait_ge(w2_zeroed, 1)
            for c in range(KC):
                sp.dma_start(w2z[:, c, (GT - 1) * H:GT * H], I["L0_gnn_W2"][c * P:(c + 1) * P, :]).then_inc(w_in, 16)
            load_cols(sp, b1[:], I["L0_gnn_b1"], w_in)
            for t in range(GT):
                sp.dma_start(b2[t * H:(t + 1) * H, :], I["L0_gnn_b2"].rearrange("(h o) -> h o", o=1)).then_inc(w_in, 16)
            wq = I["L0_mix_w_qkv"].rearrange("(c p) (h t d) -> p c t h d", p=P, h=H, t=3)
            bq = I["L0_mix_b_qkv"].rearrange("(h t d) -> h t d", h=H, t=3)
            for c in range(KC):
                sp.dma_start(mwq[:, c, :].rearrange("p (h d) -> p h d", h=H), wq[:, c, 0]).then_inc(w_in, 16)
                for h in range(H // KC):
                    sp.dma_start(mbq[h * HD:(h + 1) * HD, c:c + 1],
                                 bq[c * (H // KC) + h, 0, :].rearrange("(d o) -> d o", o=1)).then_inc(mbq_in, 16)
            load_chunks(sp, mw1[:], I["L0_mix_w1"], w_in)
            load_chunks(sp, mw2[:], I["L0_mix_w2"], w_in)
            load_cols(sp, mb1[:], I["L0_mix_b1"], w_in)
            sp.dma_start(mb2[:], I["L0_mix_b2"].rearrange("(o n) -> o n", o=1)).then_inc(w_in, 16)

            def load_ef(G):
                sp.dma_start(ef[:], K.ef[bass.ds(G * GT * RT, GT * RT), :].rearrange("(t e) f -> e t f", e=RT)
                             ).then_inc(ef_in, 16)

            def load_neg(G, p):
                sp.dma_start(neg[p][:], K.neg_d[bass.ds(G * GT, GT), :].unsqueeze(1).to_broadcast([GT, H, RT + 1])
                             ).then_inc(neg_in[p], 16)

            def turn(it, more):
                for p in range(2):
                    G = it * 2 + p
                    if more:
                        sp.wait_ge(gmx_ready, G + 1)
                        load_neg(G + 2, p)
                    for r in range(GT // 2):
                        R = G * (GT // 2) + r
                        sp.wait_ge(row_ready, 2 * (R + 1))
                        sp.dma_start(K.part_d[bass.ds(R * 2 * RT, 2 * RT), :].rearrange("(t j) f -> j t f", j=RT),
                                     rows[r % 2][:]).then_inc(rows_out[r % 2], 16)
                        if more and r == GT // 4:
                            sp.wait_ge(ef_turned, 2 * (G + 2))
                            load_ef(G + 2)

            load_ef(0)
            load_neg(0, 0)
            load_neg(1, 1)
            sp.wait_ge(ef_turned, 2)
            load_ef(1)
            with sp.Fori(0, TURNS - 1) as it:
                turn(it, True)
            turn(TURNS - 1, False)
            for b in range(2):
                sp.wait_ge(rows_out[b], 16 * ET // 4)

        @block.gpsimd
        def _(pool):
            pool.memset(w2z[:], 0.0).then_inc(w2_zeroed, 1)

            def turn(it, again):
                for p in range(2):
                    G = it * 2 + p
                    pool.wait_ge(idx_ready, 2 * (G + 1))
                    for q in range(NQ):
                        if again:
                            pool.wait_ge(vals_ready, 3 * (NQ * (G - 2) + q + 1))
                        if again or p:
                            pool.wait_ge(sc_ready, NQ * (G - 1) + q + 1)
                        pool.nop(nofuse=True)
                        for t in range(q * QT, (q + 1) * QT):
                            pool.indirect_dma_start(kv[p][:, t, :], None, K.kv_d,
                                                    bass.IndirectOffsetOnAxis(ap=idx_s[p][:, t:t + 1], axis=0)
                                                    ).then_inc(rows_in[p][q], 16)
                            pool.indirect_dma_start(qr[:, q, (t % QT) * D:(t % QT + 1) * D], None, K.q_d,
                                                    bass.IndirectOffsetOnAxis(ap=idx_d[p][:, t:t + 1], axis=0)
                                                    ).then_inc(rows_in[p][q], 16)

            both(pool, turn)

        @block.vector
        def _(dve):
            dve.memset(K.hist[:], 0.0).then_inc(hist_zeroed, 1)
            dve.wait_ge(hist_zeroed, 1)

            def indices(G, p):
                dve.tensor_copy(idx_s[p][:], K.src_t[:, bass.ds(G * GT, GT)]).then_inc(idx_ready, 1)
                dve.tensor_copy(idx_d[p][:], K.dst_t[:, bass.ds(G * GT, GT)]).then_inc(idx_ready, 1)

            def query_key(G, p, q, turn_, again):
                Q = G * NQ + q
                dve.wait_ge(rows_in[p][q], 2 * QT * 16 * (turn_ + 1))
                qv = qr[:, q, :].rearrange("e (t d) -> e t d", t=QT)
                dve.tensor_tensor(qv, qv, kv[p][:, q * QT:(q + 1) * QT, 0:D], ALU.mult).then_inc(prod_ready, 1)
                dve.wait_ge(prod_ready, Q + 1)
                if again and q == 0:
                    dve.wait_ge(st_done, G)
                dve.tensor_reduce(sc[:, q * QT * H:(q + 1) * QT * H],
                                  qr[:, q, :].rearrange("e (g d) -> e g d", d=HD), AX_X, ALU.add).then_inc(sc_ready, 1)

            def turn(it, again, more):
                if not again:
                    indices(0, 0)
                    indices(1, 1)
                    for q in range(NQ):
                        query_key(0, 0, q, 0, False)
                    indices(2, 0)
                for p in range(2):
                    G = it * 2 + p
                    dve.wait_ge(st_ready, G + 1)
                    dve.wait_ge(neg_in[p], 16 * (it + 1))
                    dve.tensor_tensor_scan(fmx[:], neg[p][:, 0:RT], st[:], -BIG, ALU.add, ALU.max).then_inc(fmx_ready, 1)
                    dve.wait_ge(fmx_ready, G + 1)
                    dve.tensor_tensor_scan(gmx[:, ::-1], neg[p][:, 1:RT + 1][:, ::-1], fmx[:, ::-1], -BIG,
                                           ALU.add, ALU.max).then_inc(gmx_ready, 1)
                    dve.wait_ge(gmx_ready, G + 1)
                    dve.tensor_tensor(st[:], st[:], gmx[:], ALU.subtract).then_inc(dif_ready, 1)
                    dve.tensor_copy(K.mfirst[:, bass.ds(G, 1)], gmx[:, 0:1]).then_inc(max_kept, 1)
                    dve.tensor_copy(K.mlast[:, bass.ds(G, 1)], fmx[:, RT - 1:RT]).then_inc(max_kept, 1)
                    if again or p:
                        add_counts(NQ * G - 1)
                    for q in range(NQ):
                        Q = G * NQ + q
                        b = q % 2
                        if again or p or q >= 2:
                            dve.wait_ge(out_done, QT * (Q - 1))
                        dve.tensor_tensor(onehot[b][:], K.col[0:RT, 0:RT].unsqueeze(1).to_broadcast([RT, QT, RT]),
                                          K.seg_t[:, bass.ds(Q * QT, QT)].unsqueeze(2).to_broadcast([RT, QT, RT]),
                                          ALU.is_equal).then_inc(vals_ready, 1)
                        if q == 0:
                            dve.wait_ge(exg_ready, G + 1)
                        eq = exg[:, q * QT * H:(q + 1) * QT * H]
                        dve.tensor_tensor(vals[b][:, :, 0:D].rearrange("e t (h d) -> e t h d", h=H),
                                          kv[p][:, q * QT:(q + 1) * QT, D:2 * D].rearrange("e t (h d) -> e t h d", h=H),
                                          eq.rearrange("e (t h) -> e t h", t=QT).unsqueeze(3).to_broadcast([RT, QT, H, HD]),
                                          ALU.mult).then_inc(vals_ready, 1)
                        dve.tensor_copy(vals[b][:, :, D:RW], eq.rearrange("e (t h) -> e t h", t=QT)).then_inc(vals_ready, 1)
                        if q:
                            add_counts(Q - 1)
                        for a, (hi, lo) in enumerate(((K.src_hi, K.src_lo), (K.dst_hi, K.dst_lo))):
                            dve.tensor_tensor(olo[:, a], K.colb[0:RT, 0:RT].unsqueeze(1).to_broadcast([RT, QT, RT]),
                                              lo[:, bass.ds(Q * QT, QT)].unsqueeze(2).to_broadcast([RT, QT, RT]),
                                              ALU.is_equal).then_inc(marks_ready, 1)
                            dve.tensor_tensor(ohi[:, a], K.colb[0:RT, 0:NT].unsqueeze(1).to_broadcast([RT, QT, NT]),
                                              hi[:, bass.ds(Q * QT, QT)].unsqueeze(2).to_broadcast([RT, QT, NT]),
                                              ALU.is_equal).then_inc(marks_ready, 1)
                        if q == 1 and p == 0:
                            dve.wait_ge(mix_mm, 4 * it + 2)
                            dve.tensor_tensor(mr[:], ps_m[:, 0:KC * RT].rearrange("p (c n) -> p c n", c=KC),
                                              K.xt[:, :, bass.ds(it * RT, RT)], ALU.add).then_inc(mix_dve, 1)
                        elif q == 1:
                            dve.wait_ge(mix_mm, 4 * it + 4)
                            xi = K.x[:, bass.ds(it, 1), :]
                            dve.tensor_tensor(xi, xi, ps_m[0:RT, 0:D].rearrange("p (o d) -> p o d", o=1),
                                              ALU.add).then_inc(mix_dve, 1)
                        if more or p == 0:
                            query_key(G + 1, 1 - p, q, it + p, True)
                    if more or p == 0:
                        indices(G + 3, 1 - p)
                if not more:
                    add_counts(ET // QT - 1)

            def add_counts(Q):
                dve.wait_ge(counted, Q + 1)
                dve.tensor_tensor(K.hist[:], K.hist[:], ps_n[0:RT, 0:2 * NT].rearrange("p (a n) -> p a n", a=2),
                                  ALU.add).then_inc(count_ready, 1)
                dve.wait_ge(count_ready, Q + 1)

            ahead(dve, turn)

        @block.scalar
        def _(act):
            act.wait_ge(w_in, W_IN)
            act.wait_ge(mbq_in, 16 * H)

            def edge_turn(G, half, again):
                act.wait_ge(ef_turned, 2 * G + half + 1)
                if again:
                    act.wait_ge(hid_done, 8 * (G - 1) + 4 * half + 4)
                act.activation(eft[:, 4 * half:4 * half + 4, :],
                               ps_et[:, 0:4 * RT].rearrange("p (b e) -> p b e", b=4), ACT.Copy).then_inc(eft_ready, 1)

            def edge_hidden(G, half, again):
                for k in range(4):
                    n = 4 * half + k
                    c, par = k // 2, k % 2
                    act.wait_ge(hid_done, 8 * G + n + 1)
                    if again and n == 0:
                        act.wait_ge(st_done, G)
                    act.activation(hid[:, c, 4 * half:4 * half + 4, par, :],
                                   ps_h[n % 2][:, 0:4 * RT].rearrange("p (b e) -> p b e", b=4),
                                   ACT.Relu, bias=b1[:, c:c + 1]).then_inc(hid_ready, 1)

            def turn(it, again, more):
                if not again:
                    for half in range(2):
                        edge_turn(0, half, False)
                        edge_hidden(0, half, False)
                for p in range(2):
                    G = it * 2 + p
                    act.wait_ge(st_done, G + 1)
                    act.activation(st[:], ps_s[:, 0:RT], ACT.Identity, bias=b2[:]).then_inc(st_ready, 1)
                    if more or p == 0:
                        edge_turn(G + 1, 0, True)
                    act.wait_ge(dif_ready, G + 1)
                    act.activation(ex[:], st[:], ACT.Exp).then_inc(ex_ready, 1)
                    act.wait_ge(mix_mm, 4 * it + 2 * p + 1)
                    for c in range(KC):
                        act.activation((mh if p else mq)[:, c, :], ps_m[:, c * RT:(c + 1) * RT],
                                       ACT.Gelu if p else ACT.Identity, bias=(mb1 if p else mbq)[:, c:c + 1]).then_inc(mix_act, 1)
                    act.wait_ge(ex_turned, G + 1)
                    if again or p:
                        act.wait_ge(vals_ready, 3 * NQ * G)
                    act.activation(exg[:], ps_n[0:RT, EC:EC + P], ACT.Copy).then_inc(exg_ready, 1)
                    for t in range(GT):
                        if (more or p == 0) and t == 0:
                            edge_hidden(G + 1, 0, True)
                        if (more or p == 0) and t == GT // 2:
                            edge_turn(G + 1, 1, True)
                            edge_hidden(G + 1, 1, True)
                        T = G * GT + t
                        r = t // 2
                        if t % 2 == 0 and (again or p or r >= 2):
                            act.wait_ge(rows_out[r % 2], 16 * (4 * G + r // 2))
                        act.wait_ge(out_done, T + 1)
                        act.activation(rows[r % 2][:, t % 2, :], ps_o[t % 2][0:RT, 0:RW], ACT.Copy).then_inc(row_ready, 1)

            ahead(act, turn)

        @block.tensor
        def _(pe):
            pe.wait_ge(w_in, W_IN)

            def edge_turn(G, half, again):
                if half == 0:
                    pe.wait_ge(ef_in, 16 * (G + 1))
                if again or half:
                    pe.wait_ge(eft_ready, 2 * G + half)
                for b in range(4):
                    t = pe.transpose(ps_et[:, b * RT:(b + 1) * RT],
                                     ef[:, 8 * half + 2 * b:8 * half + 2 * b + 2, :].rearrange("e t f -> e (t f)"),
                                     K.ident[0:RT, 0:RT])
                t.then_inc(ef_turned, 1)

            def edge_hidden(G, half, again):
                pe.wait_ge(eft_ready, 2 * G + half + 1)
                for k in range(4):
                    n = 4 * half + k
                    c, par = k // 2, k % 2
                    if again or n >= 2:
                        pe.wait_ge(hid_ready, 8 * G + n - 1)
                    pe.matmul(ps_h[n % 2][:, 0:4 * RT], w1[par * FE:(par + 1) * FE, c * P:(c + 1) * P],
                              eft[par * FE:(par + 1) * FE, 4 * half:4 * half + 4, :].rearrange("p b e -> p (b e)"),
                              start=True, stop=True).then_inc(hid_done, 1)

            def edge_scores(G, half):
                pe.wait_ge(hid_ready, 8 * G + 4 * half + 4)
                for t in range(half * GT // 2, (half + 1) * GT // 2):
                    for c in range(KC):
                        pe.matmul(ps_s[:, 0:RT], w2z[:, c, (GT - 1 - t) * H:(GT - 1 - t) * H + P],
                                  hid[:, c, t // 2, t % 2, :], start=t == 0 and c == 0, stop=False)

            def turn(it, again, more):
                if not again:
                    for half in range(2):
                        edge_turn(0, half, False)
                        edge_hidden(0, half, False)
                        edge_scores(0, half)
                for p in range(2):
                    G = it * 2 + p
                    pe.wait_ge(sc_ready, NQ * (G + 1))
                    pe.matmul(ps_s[:, 0:RT], sc[:], K.ident[0:RT, 0:RT], start=False, stop=True).then_inc(st_done, 1)
                    if more or p == 0:
                        edge_turn(G + 1, 0, True)
                    if p == 0:
                        if again:
                            pe.wait_ge(mix_act, 4 * it)
                            pe.wait_ge(mix_dve, 2 * it)
                        for co in range(KC):
                            for c in range(KC):
                                m = pe.matmul(ps_m[:, co * RT:(co + 1) * RT], mwq[:, c, co * P:(co + 1) * P],
                                              K.xt[:, c, bass.ds(it * RT, RT)], start=c == 0, stop=c == KC - 1)
                        m.then_inc(mix_mm, 1)
                    else:
                        pe.wait_ge(mix_dve, 2 * it + 1)
                        for co in range(KC):
                            for c in range(KC):
                                m = pe.matmul(ps_m[:, co * RT:(co + 1) * RT], mw1[:, c, co * P:(co + 1) * P],
                                              mr[:, c, :], start=c == 0, stop=c == KC - 1)
                        m.then_inc(mix_mm, 1)
                    pe.wait_ge(ex_ready, G + 1)
                    if again or p:
                        pe.wait_ge(count_ready, NQ * G)
                    pe.transpose(ps_n[0:RT, EC:EC + P], ex[:], K.ident[:]).then_inc(ex_turned, 1)
                    if more or p == 0:
                        edge_hidden(G + 1, 0, True)
                    if p == 0:
                        pe.wait_ge(mix_act, 4 * it + 2)
                        for c in range(KC):
                            m = pe.matmul(ps_m[:, c * RT:(c + 1) * RT], K.mkv[:, c, :], mq[:, c, :], start=True, stop=True)
                        m.then_inc(mix_mm, 1)
                    else:
                        pe.wait_ge(mix_act, 4 * it + 4)
                        pe.matmul(ps_m[0:RT, 0:D], K.ones[0:1, 0:RT], mb2[:], start=True, stop=False)
                        for c in range(KC):
                            m = pe.matmul(ps_m[0:RT, 0:D], mh[:, c, :], mw2[:, c, :], start=False, stop=c == KC - 1)
                        m.then_inc(mix_mm, 1)
                    for q in range(NQ):
                        Q = G * NQ + q
                        if (more or p == 0) and q == 1:
                            pe.wait_ge(st_ready, G + 1)
                            edge_scores(G + 1, 0)
                        elif (more or p == 0) and q == 2:
                            edge_turn(G + 1, 1, True)
                            edge_hidden(G + 1, 1, True)
                        elif (more or p == 0) and q == 3:
                            edge_scores(G + 1, 1)
                        pe.wait_ge(vals_ready, 3 * (Q + 1))
                        for t in range(QT):
                            T = Q * QT + t
                            if again or p or q or t >= 2:
                                pe.wait_ge(row_ready, T - 1)
                            pe.matmul(ps_o[t % 2][0:RT, 0:RW], onehot[q % 2][:, t, :], vals[q % 2][:, t, :],
                                      start=True, stop=True).then_inc(out_done, 1)
                        pe.wait_ge(marks_ready, 4 * (Q + 1))
                        if again or p or q:
                            pe.wait_ge(count_ready, Q)
                        for a in range(2):
                            for t in range(QT):
                                m = pe.matmul(ps_n[0:RT, a * NT:(a + 1) * NT], olo[:, a, t, :], ohi[:, a, t, :],
                                              start=t == 0, stop=t == QT - 1)
                        m.then_inc(counted, 1)

            ahead(pe, turn)


def run_starts(nc, K):
    ctx, sb, ps, sem = stage(nc, "starts")
    with ctx:
        flat = sb("flat", [RT, NT])
        scan = sb("scan", [RT, NT])
        tot = sb("tot", [RT, NT])
        start = sb("start", [RT, NT])
        deg = sb("deg", [RT, NT])
        root = sb("root", [RT, NT])
        psA = ps("psA")
        psB = ps("psB")
        step = sem("step")
        mm = sem("mm")
        root_ready = sem("root_ready")
        block = ctx.enter_context(nc.Block())

        @block.tensor
        def _(pe):
            pe.matmul(psA[0:RT, 0:NT], K.tri[0:RT, 0:RT], K.hist[:, 1, :], start=True, stop=True).then_inc(mm, 1)
            pe.matmul(psB[0:RT, 0:NT], K.ones[0:RT, 0:RT], K.hist[:, 1, :], start=True, stop=True).then_inc(mm, 1)

        @block.vector
        def _(dve):
            dve.tensor_scalar(K.has[:], K.hist[:, 1, :], 0.0, None, ALU.is_gt).then_inc(step, 1)
            dve.tensor_scalar(deg[:], K.hist[:, 0, :], 1.0, None, ALU.max).then_inc(step, 1)
            dve.memset(flat[:], 1.0).then_inc(step, 1)
            dve.wait_ge(mm, 2)
            dve.tensor_copy(tot[:], psB[0:RT, 0:NT]).then_inc(step, 1)
            dve.wait_ge(step, 4)
            dve.tensor_tensor_scan(scan[:], flat[:], tot[:], 0.0, ALU.mult, ALU.add).then_inc(step, 1)
            dve.wait_ge(step, 5)
            dve.tensor_tensor(start[:], scan[:], tot[:], ALU.subtract).then_inc(step, 1)
            dve.wait_ge(step, 6)
            dve.tensor_tensor(scan[:], start[:], psA[0:RT, 0:NT], ALU.add).then_inc(step, 1)
            dve.wait_ge(step, 7)
            dve.tensor_scalar(start[:], scan[:], float(E - 1), None, ALU.min).then_inc(step, 1)
            dve.wait_ge(step, 8)
            dve.tensor_copy(K.start[:], start[:]).then_inc(step, 1)
            dve.wait_ge(root_ready, 1)
            dve.reciprocal(K.rdeg[:], root[:]).then_inc(step, 1)

        @block.scalar
        def _(act):
            act.wait_ge(step, 2)
            act.activation(root[:], deg[:], ACT.Sqrt).then_inc(root_ready, 1)


def run_scales(nc, K):
    ctx, sb, ps, sem = stage(nc, "scales")
    with ctx:
        first = sb("first", [H, ET])
        last = sb("last", [H, ET])
        cont = sb("cont", [H, ET + 1])
        single = sb("single", [H, ET])
        carry = sb("carry", [H, ET])
        fopen = sb("fopen", [H, ET])
        bopen = sb("bopen", [H, ET])
        fmx = sb("fmx", [H, ET])
        bmx = sb("bmx", [H, ET])
        top = sb("top", [H, ET])
        ff = sb("ff", [H, ET])
        fh = sb("fh", [H, ET])
        head = sb("head", [H, ET])
        psT = ps("psT")
        kept = sem("kept")
        t_in = sem("t_in")
        step = sem("step")
        exps = sem("exps")
        mm = sem("mm")
        block = ctx.enter_context(nc.Block())

        @block.sync
        def _(sp):
            sp.dma_start(K.mfirst_d, K.mfirst[:]).then_inc(kept, 16)
            sp.dma_start(K.mlast_d, K.mlast[:]).then_inc(kept, 16)
            sp.wait_ge(kept, 32)
            for dst, src in ((first, K.mfirst_d), (last, K.mlast_d)):
                sp.dma_start(dst[:].rearrange("h (t g) -> h t g", t=GT), src.rearrange("(t h) g -> h t g", h=H)).then_inc(t_in, 16)
            sp.dma_start(cont[:, 0:ET], bcast_row(K.cont_d, H)).then_inc(t_in, 16)
            sp.dma_start(single[:], bcast_row(K.single_d, H)).then_inc(t_in, 16)

        @block.vector
        def _(dve):
            n = 0

            def then(ins):
                nonlocal n
                n += 1
                ins.then_inc(step, 1)
                dve.wait_ge(step, n)

            then(dve.memset(cont[:, ET:ET + 1], 0.0))
            dve.wait_ge(t_in, 64)
            then(dve.tensor_copy(fmx[:].rearrange("h (g t) -> h t g", t=GT), first[:].rearrange("h (t g) -> h t g", t=GT)))
            then(dve.tensor_copy(bmx[:].rearrange("h (g t) -> h t g", t=GT), last[:].rearrange("h (t g) -> h t g", t=GT)))
            then(dve.tensor_copy(first[:], fmx[:]))
            then(dve.tensor_copy(last[:], bmx[:]))
            then(dve.tensor_tensor(carry[:], single[:], cont[:, 0:ET], ALU.mult))
            then(dve.tensor_scalar(fopen[:], carry[:], -1.0, BIG, ALU.add, ALU.mult))
            then(dve.tensor_tensor(bopen[:], single[:], cont[:, 1:ET + 1], ALU.mult))
            then(dve.tensor_scalar(bopen[:], bopen[:], -1.0, BIG, ALU.add, ALU.mult))
            then(dve.tensor_tensor_scan(fmx[:], fopen[:], last[:], -BIG, ALU.add, ALU.max))
            then(dve.tensor_tensor_scan(bmx[:, ::-1], bopen[:, ::-1], first[:, ::-1], -BIG, ALU.add, ALU.max))
            then(dve.tensor_copy(top[:], bmx[:]))
            then(dve.tensor_tensor(top[:, 1:ET], fmx[:, 0:ET - 1], bmx[:, 1:ET], ALU.max))
            then(dve.tensor_tensor(ff[:], first[:], top[:], ALU.subtract))
            then(dve.memset(fh[:, 0:1], 0.0))
            then(dve.tensor_tensor(fh[:, 1:ET], last[:, 0:ET - 1], top[:, 1:ET], ALU.subtract))
            then(dve.tensor_scalar(fh[:], fh[:], 0.0, None, ALU.min))
            then(dve.memset(head[:, 0:1], 0.0))
            then(dve.tensor_scalar(head[:, 1:ET], carry[:, 0:ET - 1], -1.0, 1.0, ALU.mult, ALU.add))
            then(dve.tensor_tensor(head[:], head[:], cont[:, 0:ET], ALU.mult))
            dve.wait_ge(exps, 2)
            then(dve.tensor_tensor(ff[:], ff[:], cont[:, 0:ET], ALU.mult))
            then(dve.tensor_tensor(fh[:], fh[:], head[:], ALU.mult))
            dve.wait_ge(mm, 1)
            then(dve.tensor_copy(K.join[:, :, 0:2 * H],
                                 psT[0:EP, 0:EK * 3 * H].rearrange("p (k j) -> p k j", j=3 * H)[:, :, 0:2 * H]))
            then(dve.tensor_copy(K.join[:, :, 2 * H:2 * H + 1],
                                 psT[0:EP, 0:EK * 3 * H].rearrange("p (k j) -> p k j", j=3 * H)[:, :, 2 * H:2 * H + 1]))

        @block.scalar
        def _(act):
            act.wait_ge(step, 17)
            act.activation(ff[:], ff[:], ACT.Exp).then_inc(exps, 1)
            act.activation(fh[:], fh[:], ACT.Exp).then_inc(exps, 1)

        @block.tensor
        def _(pe):
            pe.wait_ge(step, 22)
            for k in range(EK):
                for j, tab in enumerate((ff, fh, head)):
                    t = pe.transpose(psT[0:EP, (3 * k + j) * H:(3 * k + j + 1) * H],
                                     tab[:].rearrange("h (p k) -> h k p", k=EK)[:, k, :], K.ident[0:H, 0:H])
            t.then_inc(mm, 1)


def join_attention(nc, K, I):
    ctx, sb, ps, sem = stage(nc, "join")
    with ctx:
        wo = sb("wo", [P, KC, D])
        bo = sb("bo", [1, D])
        edge0 = sb("edge0", [EP, EK, RW])
        JW = RW + H + 1
        rhs = sb("rhs", [EP, EK, JW])
        dsh = sb("dsh", [EP, EK])
        hot = [sb(f"hot{u}", [EP, EK, RT]) for u in range(UN)]
        row = [sb(f"row{u}", [RT, RW]) for u in range(UN)]
        idx = sb("idx", [RT, UN], I32)
        fac = sb("fac", [RT, H])
        one = sb("one", [RT, 1])
        sums = sb("sums", [RT, RW])
        prod = sb("prod", [RT, RW])
        den = sb("den", [RT, H])
        rden = sb("rden", [RT, H])
        outn = sb("outn", [RT, D])
        outt = sb("outt", [P, KC, RT])
        psJ = [ps(f"psJ{u}") for u in range(UN)]
        psT = ps("psT")
        psO = ps("psO")
        w_in = sem("w_in")
        idx_ready = sem("idx_ready")
        row_in = [sem(f"row_in{u}", kept=K.kept) for u in range(UN)]
        rhs_ready = sem("rhs_ready")
        dsh_ready = sem("dsh_ready")
        hot_ready = sem("hot_ready")
        joined = sem("joined")
        step = sem("step")
        turned = sem("turned")
        outt_ready = sem("outt_ready")
        out_done = sem("out_done")
        x_ready = sem("x_ready")
        block = ctx.enter_context(nc.Block())

        @block.sync
        def _(sp):
            load_chunks(sp, wo[:], I["L0_gnn_Wo"], w_in)
            sp.dma_start(bo[:], I["L0_gnn_bo"].rearrange("(o n) -> o n", o=1)).then_inc(w_in, 16)
            sp.dma_start(edge0[:], K.part_d.rearrange("(p k j) f -> p k j f", p=EP, j=RT)[:, :, 0, :]).then_inc(w_in, 16)

        @block.gpsimd
        def _(pool):
            def body(g, again):
                pool.wait_ge(idx_ready, g + 1)
                for u in range(UN):
                    if again:
                        pool.wait_ge(step, 8 * (g - 1) * UN + 8 * (u + 1))
                        pool.nop(nofuse=True)
                    elif u == 0:
                        pool.nop(nofuse=True)
                    pool.indirect_dma_start(row[u][:], None, K.part_d,
                                            bass.IndirectOffsetOnAxis(ap=idx[:, u:u + 1], axis=0)).then_inc(row_in[u], 16)

            turns(pool, body)

        @block.vector
        def _(dve):
            dve.wait_ge(w_in, 64 - 16)
            for k in range(EK):
                dve.tensor_tensor(rhs[:, k, 0:D].rearrange("p (h d) -> p h d", h=H),
                                  edge0[:, k, 0:D].rearrange("p (h d) -> p h d", h=H),
                                  K.join[:, k, 0:H].unsqueeze(2).to_broadcast([EP, H, HD]), ALU.mult).then_inc(rhs_ready, 1)
            dve.tensor_tensor(rhs[:, :, D:RW], edge0[:, :, D:RW], K.join[:, :, 0:H], ALU.mult).then_inc(rhs_ready, 1)
            dve.tensor_copy(rhs[:, :, RW:JW], K.join[:, :, H:2 * H + 1]).then_inc(rhs_ready, 1)

            def owners(g, i, u, again):
                if again or u:
                    dve.wait_ge(hot_ready, i)
                dve.tensor_scalar(dsh[:], K.dfirst[:], K.tilebase[0:EP, bass.ds(i, 1)], None,
                                  ALU.subtract).then_inc(dsh_ready, 1)
                dve.wait_ge(dsh_ready, i + 1)
                if again:
                    dve.wait_ge(joined, i - (UN - 1))
                dve.tensor_tensor(hot[u][:], K.col[0:EP, 0:RT].unsqueeze(1).to_broadcast([EP, EK, RT]),
                                  dsh[:].unsqueeze(2).to_broadcast([EP, EK, RT]), ALU.is_equal).then_inc(hot_ready, 1)

            def mean(g, i, u, again):
                dve.wait_ge(joined, i + 1)
                J = psJ[u][0:RT, :]
                dve.tensor_scalar(one[:], J[:, JW - 1:JW], -1.0, 1.0, ALU.mult, ALU.add).then_inc(step, 1)
                dve.wait_ge(step, 8 * i + 1)
                dve.tensor_scalar(fac[:], J[:, RW:RW + H], one[:], K.has[:, bass.ds(i, 1)], ALU.add, ALU.mult).then_inc(step, 1)
                dve.wait_ge(step, 8 * i + 2)
                dve.wait_ge(row_in[u], 16 * (g + 1))
                dve.tensor_tensor(prod[:, 0:D].rearrange("p (h d) -> p h d", h=H),
                                  row[u][:, 0:D].rearrange("p (h d) -> p h d", h=H),
                                  fac[:].unsqueeze(2).to_broadcast([RT, H, HD]), ALU.mult).then_inc(step, 1)
                dve.tensor_tensor(prod[:, D:RW], row[u][:, D:RW], fac[:], ALU.mult).then_inc(step, 1)
                dve.wait_ge(step, 8 * i + 4)
                dve.tensor_tensor(sums[:], prod[:], J[:, 0:RW], ALU.add).then_inc(step, 1)
                dve.wait_ge(step, 8 * i + 5)
                dve.tensor_scalar(den[:], sums[:, D:RW], 1e-30, None, ALU.max).then_inc(step, 1)
                dve.wait_ge(step, 8 * i + 6)
                dve.reciprocal(rden[:], den[:]).then_inc(step, 1)
                dve.wait_ge(step, 8 * i + 7)
                if again or u:
                    dve.wait_ge(turned, i)
                dve.tensor_tensor(outn[:].rearrange("p (h d) -> p h d", h=H),
                                  sums[:, 0:D].rearrange("p (h d) -> p h d", h=H),
                                  rden[:].unsqueeze(2).to_broadcast([RT, H, HD]), ALU.mult).then_inc(step, 1)

            def indices(g, i, u, again):
                if u == 0:
                    if again:
                        for v in range(UN):
                            dve.wait_ge(row_in[v], 16 * g)
                    dve.tensor_copy(idx[:], K.start[:, bass.ds(g * UN, UN)]).then_inc(idx_ready, 1)

            def add(g, i, u, again):
                dve.wait_ge(out_done, i + 1)
                xi = K.x[:, bass.ds(i, 1), :]
                dve.tensor_tensor(xi, xi, psO[0:RT, 0:D].rearrange("p (o d) -> p o d", o=1), ALU.add).then_inc(x_ready, 1)

            staggered(dve, (indices, 0), (mean, 3), (owners, 0), (add, 4))

        @block.scalar
        def _(act):
            def body(g, again):
                for u in range(UN):
                    i = g * UN + u
                    act.wait_ge(turned, i + 1)
                    if again or u:
                        act.wait_ge(out_done, i)
                    act.activation(outt[:], psT[:, 0:KC * RT].rearrange("p (c n) -> p c n", c=KC),
                                   ACT.Copy).then_inc(outt_ready, 1)

            turns(act, body)

        @block.tensor
        def _(pe):
            pe.wait_ge(w_in, 48)
            pe.wait_ge(rhs_ready, EK + 2)

            def join(g, i, u, again):
                pe.wait_ge(hot_ready, i + 1)
                if again:
                    pe.wait_ge(step, 8 * (i - (UN - 1)))
                for k in range(EK):
                    m = pe.matmul(psJ[u][0:RT, 0:JW], hot[u][:, k, :], rhs[:, k, :], start=k == 0, stop=k == EK - 1)
                m.then_inc(joined, 1)

            def turn(g, i, u, again):
                pe.wait_ge(step, 8 * i + 8)
                if again or u:
                    pe.wait_ge(outt_ready, i)
                for c in range(KC):
                    t = pe.transpose(psT[:, c * RT:(c + 1) * RT], outn[:, c * P:(c + 1) * P], K.ident[0:RT, 0:RT])
                t.then_inc(turned, 1)

            def product(g, i, u, again):
                pe.wait_ge(outt_ready, i + 1)
                if again or u:
                    pe.wait_ge(x_ready, i)
                pe.matmul(psO[0:RT, 0:D], K.ones[0:1, 0:RT], bo[:], start=True, stop=False)
                for c in range(KC):
                    m = pe.matmul(psO[0:RT, 0:D], outt[:, c, :], wo[:, c, :], start=False, stop=c == KC - 1)
                m.then_inc(out_done, 1)

            staggered(pe, (turn, 3), (join, 1), (product, 3))


def route_experts(nc, K, I):
    ctx, sb, ps, sem = stage(nc, "route")
    with ctx:
        gw = sb("gw", [P, KC, EXPERTS])
        gb = sb("gb", [1, EXPERTS])
        zero = sb("zero", [RT, 4, D])
        xall = sb("xall", [RT, NT, D])
        TE = [RT, NT, EXPERTS]
        logit = sb("logit", TE)
        eid = sb("eid", TE)
        eid_i = sb("eid_i", TE, I32)
        cand = sb("cand", TE)
        hot = sb("hot", TE)
        ET_ = [RT, EXPERTS, NT]
        hote = sb("hote", ET_)
        keep = sb("keep", ET_)
        pref = sb("pref", ET_)
        tot = sb("tot", ET_)
        run = sb("run", ET_)
        big = sb("big", [RT, NT])
        best = sb("best", [RT, NT])
        expert = sb("expert", [RT, NT])
        pos = sb("pos", [RT, NT])
        kept = sb("kept", [RT, NT])
        slot = sb("slot", [RT, NT])
        esum = sb("esum", [RT, NT])
        place = sb("place", [RT, NT], I32)
        psL = [ps(f"psL{b}") for b in range(2)]
        psA = ps("psA")
        psB = ps("psB")
        norm = Norm(K, sb, ps, sem)
        w_in = sem("w_in")
        consts = sem("consts")
        kept_rows = sem("kept_rows")
        l_done = sem("l_done")
        l_ready = sem("l_ready")
        step = sem("step")
        exp_ready = sem("exp_ready")
        mm = sem("mm")
        zeroed = sem("zeroed")
        placed = sem("placed", kept=K.kept)
        ROUTED = 24
        block = ctx.enter_context(nc.Block())

        @block.sync
        def _(sp):
            load_chunks(sp, gw[:], I["L0_ffn_gate_w"], w_in)
            sp.dma_start(gb[:], I["L0_ffn_gate_b"].rearrange("(o n) -> o n", o=1)).then_inc(w_in, 16)
            sp.wait_ge(consts, 1)
            for e in range(EXPERTS):
                sp.dma_start(K.ebuf_d[e * CAPR:(e + 1) * CAPR, :].rearrange("(t p) d -> p t d", p=RT), zero[:]).then_inc(zeroed, 16)

        @block.gpsimd
        def _(pool):
            pool.memset(zero[:], 0.0).then_inc(consts, 1)
            pool.iota(eid_i[:], [[0, NT], [1, EXPERTS]], base=-EXPERTS, channel_multiplier=0).then_inc(consts, 1)

            def body(g, again):
                for u in range(UN):
                    pool.wait_ge(norm.xn_ready, g * UN + u + 1)
                    pool.tensor_copy(xall[:, bass.ds(g * UN + u, 1), :].rearrange("p o d -> p (o d)"), norm.xn[u][:]
                                     ).then_inc(kept_rows, 1)

            turns(pool, body)
            pool.wait_ge(kept_rows, NT)
            pool.wait_ge(zeroed, 16 * EXPERTS)
            pool.wait_ge(step, ROUTED)
            for i in range(NT):
                pool.indirect_dma_start(K.ebuf_d, bass.IndirectOffsetOnAxis(ap=place[:, i:i + 1], axis=0), xall[:, i, :], None,
                                        bounds_check=EXPERTS * CAPR - 1, oob_is_err=False).then_inc(placed, 16)
            pool.wait_ge(placed, 16 * NT)

        @block.vector
        def _(dve):
            norm.dve_deviations(dve)

            def normalise(g, i, u, again):
                if again:
                    dve.wait_ge(kept_rows, i - (UN - 1))
                norm.dve_tile(dve, i, u, again)

            def keep_logits(g, i, u, again):
                dve.wait_ge(l_done, i + 1)
                dve.tensor_copy(logit[:, bass.ds(i, 1), :].rearrange("p o e -> p (o e)"),
                                psL[u % 2][0:RT, 0:EXPERTS]).then_inc(l_ready, 1)

            lagged(dve, normalise, keep_logits, 2)
            n = 0

            def then(ins):
                nonlocal n
                n += 1
                ins.then_inc(step, 1)
                dve.wait_ge(step, n)

            def wide(t):
                return t[:].unsqueeze(2).to_broadcast(TE)

            dve.wait_ge(l_ready, NT)
            dve.wait_ge(consts, 2)
            then(dve.tensor_copy(eid[:], eid_i[:]))
            then(dve.tensor_reduce(big[:], logit[:], AX_X, ALU.max))
            then(dve.tensor_tensor(logit[:], logit[:], wide(big), ALU.subtract))
            then(dve.tensor_scalar(hot[:], logit[:], 0.0, None, ALU.is_equal))
            then(dve.tensor_tensor(cand[:], hot[:], eid[:], ALU.mult))
            then(dve.tensor_reduce(best[:], cand[:], AX_X, ALU.min))
            then(dve.tensor_tensor(hot[:], eid[:], wide(best), ALU.is_equal))
            then(dve.tensor_copy(hote[:].rearrange("p e i -> p i e"), hot[:]))
            dve.wait_ge(exp_ready, 1)
            then(dve.tensor_reduce(esum[:], cand[:], AX_X, ALU.add))
            then(dve.memset(keep[:], 1.0))
            then(dve.memset(keep[:, :, 0:1], 0.0))
            then(dve.reciprocal(K.prob[:], esum[:]))
            dve.wait_ge(mm, 2)
            flat = "p e i -> p (e i)"
            then(dve.tensor_copy(tot[:].rearrange(flat), psB[0:RT, 0:EXPERTS * NT]))
            then(dve.tensor_tensor_scan(run[:].rearrange(flat), keep[:].rearrange(flat), tot[:].rearrange(flat), 0.0,
                                        ALU.mult, ALU.add))
            then(dve.tensor_tensor(pref[:], run[:], tot[:], ALU.subtract))
            then(dve.tensor_tensor(pref[:].rearrange(flat), pref[:].rearrange(flat), psA[0:RT, 0:EXPERTS * NT], ALU.add))
            then(dve.tensor_tensor(run[:], pref[:], hote[:], ALU.mult))
            then(dve.tensor_reduce(pos[:], run[:].rearrange("p e i -> p i e"), AX_X, ALU.add))
            then(dve.tensor_scalar(expert[:], best[:], float(EXPERTS), float(CAPR), ALU.add, ALU.mult))
            then(dve.tensor_scalar(kept[:], pos[:], float(CAP), None, ALU.is_lt))
            then(dve.scalar_tensor_tensor(out=slot[:], in0=pos[:], scalar=float(CAP - 1), in1=expert[:], op0=ALU.min, op1=ALU.add))
            then(dve.tensor_copy(K.slot[:], slot[:]))
            then(dve.scalar_tensor_tensor(out=slot[:], in0=kept[:], scalar=-float(EXPERTS * CAPR), in1=slot[:],
                                          op0=ALU.mult, op1=ALU.add))
            then(dve.tensor_scalar(place[:], slot[:], float(EXPERTS * CAPR), None, ALU.add))
            assert n == ROUTED
            then(dve.tensor_tensor(K.prob[:], K.prob[:], kept[:], ALU.mult))

        @block.scalar
        def _(act):
            norm.act_deviations(act)

            def body(g, again):
                for u in range(UN):
                    norm.act_tile(act, g * UN + u, u, again, l_done)

            turns(act, body)
            act.wait_ge(step, 8)
            act.activation(cand[:], logit[:], ACT.Exp).then_inc(exp_ready, 1)

        @block.tensor
        def _(pe):
            pe.wait_ge(w_in, 32)

            def logits(g, i, u, again):
                pe.wait_ge(norm.xt_ready, i + 1)
                if again or u >= 2:
                    pe.wait_ge(l_ready, slot_tiles(i, u))
                L = psL[u % 2][0:RT, 0:EXPERTS]
                pe.matmul(L, K.ones[0:1, 0:RT], gb[:], start=True, stop=False)
                for c in range(KC):
                    m = pe.matmul(L, norm.xt[u][:, c, :], gw[:, c, :], start=False, stop=c == KC - 1)
                m.then_inc(l_done, 1)

            lagged(pe, lambda g, i, u, again: norm.pe_turn(pe, i, u, again), logits, 1)
            pe.wait_ge(step, 8)
            flat = hote[:].rearrange("p e i -> p (e i)")
            pe.matmul(psA[0:RT, 0:EXPERTS * NT], K.tri[0:RT, 0:RT], flat, start=True, stop=True).then_inc(mm, 1)
            pe.matmul(psB[0:RT, 0:EXPERTS * NT], K.ones[0:RT, 0:RT], flat, start=True, stop=True).then_inc(mm, 1)


def networks(nc, K, s, units, rt, weights, bias1, bias2, func, src, dst):
    ctx, sb, ps, sem = stage(nc, s)
    MT = UT
    UR = MT * rt
    shared = not callable(weights)
    nb = 1 if shared else units
    with ctx:
        nw = 1 if shared else 2
        w1 = [sb(f"w1{b}", [P, KC, FF]) for b in range(nw)]
        w2 = [sb(f"w2{b}", [P, FC, D]) for b in range(nw)]
        b1r = sb("b1r", [nb * FC, P])
        b1 = sb("b1", [P, nb * FC])
        b2 = sb("b2", [1, nb * D])
        rows = [sb(f"rows{b}", [rt, MT, D]) for b in range(2)]
        rowt = [sb(f"rowt{b}", [P, KC, UR]) for b in range(2)]
        hid = sb("hid", [P, FC, UR])
        y = [sb(f"y{b}", [rt, D]) for b in range(2)]
        b1u = sb("b1u", [P, FC])
        b2u = sb("b2u", [1, D])
        psT = [ps(f"psT{b}") for b in range(KC)]
        psH = [ps(f"psH{b}") for b in range(2)]
        psY = [ps(f"psY{b}") for b in range(2)]
        w_in = [sem(f"w_in{b}") for b in range(nw)]
        b_in = sem("b_in")
        b1_turned = sem("b1_turned")
        b1_ready = sem("b1_ready")
        bu_ready = sem("bu_ready")
        rows_in = [sem(f"rows_in{b}") for b in range(2)]
        turned = sem("turned")
        rowt_ready = sem("rowt_ready")
        hid_done = sem("hid_done")
        hid_ready = sem("hid_ready")
        y_done = sem("y_done")
        y_ready = sem("y_ready")
        y_out = [sem(f"y_out{b}") for b in range(2)]
        block = ctx.enter_context(nc.Block())

        def w_slot(p):
            return 0 if shared else p

        def pairs(eng, turn):
            last = units // 2 - 1
            turn(0, False, True)
            if last > 1:
                with eng.Fori(1, last) as it:
                    turn(it, True, True)
            turn(last, True, False)

        @block.sync
        def _(sp):
            def load_rows(e, p):
                sp.dma_start(rows[p][:], src[bass.ds(e * UR, UR), :].rearrange("(t p) d -> p t d", p=rt)).then_inc(rows_in[p], 16)

            def load_weights(e, p):
                m1, m2 = weights if shared else weights(e)
                sp.dma_start(w1[p][:], m1.rearrange("(c p) f -> p c f", p=P)).then_inc(w_in[p], 16)
                sp.dma_start(w2[p][:], m2.rearrange("(c p) d -> p c d", p=P)).then_inc(w_in[p], 16)

            sp.dma_start(b1r[:], bias1).then_inc(b_in, 16)
            sp.dma_start(b2[:], bias2).then_inc(b_in, 16)
            load_rows(0, 0)
            load_weights(0, 0)
            load_rows(1, 1)
            if not shared:
                load_weights(1, 1)

            def turn(it, more):
                for p in range(2):
                    e = it * 2 + p
                    if more:
                        sp.wait_ge(turned, KC * (e + 1))
                        load_rows(e + 2, p)
                    for t in range(MT):
                        Y = e * MT + t
                        sp.wait_ge(y_ready, Y + 1)
                        sp.dma_start(dst[bass.ds(Y * rt, rt), :], y[t % 2][:]).then_inc(y_out[t % 2], 16)
                    if more and not shared:
                        load_weights(e + 2, p)

            with sp.Fori(0, units // 2 - 1) as it:
                turn(it, True)
            turn(units // 2 - 1, False)
            for b in range(2):
                sp.wait_ge(y_out[b], 16 * units * MT // 2)

        @block.tensor
        def _(pe):
            pe.wait_ge(b_in, 32)
            pe.transpose(psT[0][:, 0:nb * FC], b1r[:], K.ident[0:nb * FC, 0:nb * FC]).then_inc(b1_turned, 1)
            pe.wait_ge(b1_ready, 1)

            def turn_rows(e, p, it, first):
                pe.wait_ge(rows_in[p], 16 * (it + 1))
                for c in range(KC):
                    if not first:
                        pe.wait_ge(rowt_ready, KC * (e - 1) + c + 1)
                    for t in range(MT):
                        m = pe.transpose(psT[c][:, t * rt:(t + 1) * rt], rows[p][:, t, c * P:(c + 1) * P], K.ident[0:rt, 0:rt])
                    m.then_inc(turned, 1)

            def turn(it, again, more):
                if not again:
                    turn_rows(0, 0, 0, True)
                for p in range(2):
                    e = it * 2 + p
                    pe.wait_ge(w_in[w_slot(p)], 32 if shared else 32 * (it + 1))
                    pe.wait_ge(rowt_ready, KC * (e + 1))
                    for f in range(FC):
                        if again or p or f >= 2:
                            pe.wait_ge(hid_ready, FC * e + f - 1)
                        for c in range(KC):
                            m = pe.matmul(psH[f % 2][:, 0:UR], w1[w_slot(p)][:, c, f * P:(f + 1) * P], rowt[p][:, c, :],
                                          start=c == 0, stop=c == KC - 1)
                        m.then_inc(hid_done, 1)
                    if more or p == 0:
                        turn_rows(e + 1, 1 - p, it + p, False)
                    pe.wait_ge(hid_ready, FC * (e + 1))
                    pe.wait_ge(bu_ready, 2 * (e + 1))
                    for t in range(MT):
                        if again or p or t >= 2:
                            pe.wait_ge(y_ready, MT * e + t - 1)
                        pe.matmul(psY[t % 2][0:rt, 0:D], K.ones[0:1, 0:rt], b2u[:], start=True, stop=False)
                        for f in range(FC):
                            m = pe.matmul(psY[t % 2][0:rt, 0:D], hid[:, f, t * rt:(t + 1) * rt], w2[w_slot(p)][:, f, :],
                                          start=False, stop=f == FC - 1)
                        m.then_inc(y_done, 1)

            pairs(pe, turn)

        @block.scalar
        def _(act):
            def turn(it, again, more):
                for p in range(2):
                    e = it * 2 + p
                    act.wait_ge(bu_ready, 2 * (e + 1))
                    for f in range(FC):
                        act.wait_ge(hid_done, FC * e + f + 1)
                        act.activation(hid[:, f, :], psH[f % 2][:, 0:UR], func, bias=b1u[:, f:f + 1]).then_inc(hid_ready, 1)

            pairs(act, turn)

        @block.vector
        def _(dve):
            dve.wait_ge(b1_turned, 1)
            dve.tensor_copy(b1[:], psT[0][:, 0:nb * FC]).then_inc(b1_ready, 1)
            dve.wait_ge(b1_ready, 1)

            def keep_turned(e, p, again):
                for c in range(KC):
                    dve.wait_ge(turned, KC * e + c + 1)
                    if again:
                        dve.wait_ge(hid_done, FC * (e - 1))
                    dve.tensor_copy(rowt[p][:, c, :], psT[c][:, 0:UR]).then_inc(rowt_ready, 1)

            def turn(it, again, more):
                if not again:
                    keep_turned(0, 0, False)
                for p in range(2):
                    e = it * 2 + p
                    if again or p:
                        dve.wait_ge(hid_ready, FC * e)
                        dve.wait_ge(y_done, MT * e)
                    eb = 0 if shared else e
                    dve.tensor_copy(b1u[:], b1[:, bass.ds(eb * FC, FC)]).then_inc(bu_ready, 1)
                    dve.tensor_copy(b2u[:], b2[:, bass.ds(eb * D, D)]).then_inc(bu_ready, 1)
                    if more or p == 0:
                        keep_turned(e + 1, 1 - p, again or p)
                    for t in range(MT):
                        Y = e * MT + t
                        dve.wait_ge(y_done, Y + 1)
                        if again or p or t >= 2:
                            dve.wait_ge(y_out[t % 2], 16 * (2 * e + t // 2))
                        dve.tensor_copy(y[t % 2][:], psY[t % 2][0:rt, 0:D]).then_inc(y_ready, 1)

            pairs(dve, turn)


def take_experts(nc, K):
    ctx, sb, ps, sem = stage(nc, "take")
    with ctx:
        GW = [RT, UN, D]
        row = sb("row", [RT, NT, D])
        clean = [sb(f"clean{b}", GW) for b in range(2)]
        isnum = sb("isnum", GW, I32)
        over = sb("over", GW, I32)
        under = sb("under", GW, I32)
        top = sb("top", [RT, 1])
        bottom = sb("bottom", [RT, 1])
        row_in = [sem(f"row_in{g}", kept=K.kept) for g in range(NG)]
        zeroed = sem("zeroed")
        consts = sem("consts")
        step = sem("step")
        x_ready = sem("x_ready")
        block = ctx.enter_context(nc.Block())

        @block.gpsimd
        def _(pool):
            for b in range(2):
                pool.memset(clean[b][:], 0.0).then_inc(zeroed, 1)
            for i in range(NT):
                pool.indirect_dma_start(row[:, i, :], None, K.ey_d, bass.IndirectOffsetOnAxis(ap=K.slot[:, i:i + 1], axis=0)
                                        ).then_inc(row_in[i // UN], 16)
            for g in range(NG):
                xg = K.x[:, g * UN:(g + 1) * UN, :]
                pool.wait_ge(step, 7 * g + 7)
                pool.tensor_tensor(xg, xg, clean[g % 2][:], ALU.add).then_inc(x_ready, 1)
                if g + 2 < NG:
                    pool.wait_ge(x_ready, g + 1)
                    pool.memset(clean[g % 2][:], 0.0).then_inc(zeroed, 1)

        @block.vector
        def _(dve):
            dve.memset(top[:], 1e4).then_inc(consts, 1)
            dve.memset(bottom[:], -1e4).then_inc(consts, 1)
            dve.wait_ge(consts, 2)
            for g in range(NG):
                v = row[:, g * UN:(g + 1) * UN, :]
                dve.wait_ge(row_in[g], 16 * UN)
                dve.tensor_tensor(v, v, K.prob[:, g * UN:(g + 1) * UN].unsqueeze(2).to_broadcast(GW), ALU.mult).then_inc(step, 1)
                dve.wait_ge(step, 7 * g + 1)
                dve.tensor_tensor(isnum[:], v, v, ALU.is_equal).then_inc(step, 1)
                dve.tensor_scalar(over[:], v, 3.4028235e38, None, ALU.is_gt).then_inc(step, 1)
                dve.tensor_scalar(under[:], v, -3.4028235e38, None, ALU.is_lt).then_inc(step, 1)
                dve.wait_ge(zeroed, g + 1)
                for n, (mask, data) in enumerate(((isnum, v), (over, top[:].unsqueeze(2).to_broadcast(GW)),
                                                  (under, bottom[:].unsqueeze(2).to_broadcast(GW)))):
                    dve.wait_ge(step, 7 * g + 4 + n)
                    dve.copy_predicated(clean[g % 2][:], mask[:], data).then_inc(step, 1)


def turn_weights(nc, K, I):
    ctx, sb, ps, sem = stage(nc, "wturn")
    with ctx:
        parts = [("L1_mix_Wqkv", 3 * D, K.wqkv_t), ("L1_mix_W1", D, K.w1_t), ("L1_mix_W2", D, K.w2_t)]
        raw = [sb(f"raw{n}", [P, rows // P, D]) for n, (_, rows, _) in enumerate(parts)]
        psW = [ps(f"psW{b}") for b in range(2)]
        w_in = sem("w_in")
        turned = sem("turned")
        ready = sem("ready")
        block = ctx.enter_context(nc.Block())
        jobs = [(n, c) for n, (_, rows, _) in enumerate(parts) for c in range(KC)]

        @block.sync
        def _(sp):
            for n, (name, rows, _) in enumerate(parts):
                sp.dma_start(raw[n][:], I[name].rearrange("(o p) i -> p o i", p=P)).then_inc(w_in, 16)

        rounds = [(n, c, o0, min(4, parts[n][1] // P - o0)) for n, c in jobs for o0 in range(0, parts[n][1] // P, 4)]

        @block.tensor
        def _(pe):
            pe.wait_ge(w_in, 16 * len(parts))
            for r, (n, c, o0, k) in enumerate(rounds):
                if r >= 2:
                    pe.wait_ge(ready, r - 1)
                for o in range(k):
                    t = pe.transpose(psW[r % 2][:, o * P:(o + 1) * P], raw[n][:, o0 + o, c * P:(c + 1) * P], K.ident[:])
                t.then_inc(turned, 1)

        @block.vector
        def _(dve):
            for r, (n, c, o0, k) in enumerate(rounds):
                dve.wait_ge(turned, r + 1)
                dve.tensor_copy(parts[n][2][:, c, o0 * P:(o0 + k) * P], psW[r % 2][:, 0:k * P]).then_inc(ready, 1)


def message_tables(nc, K, I):
    ctx, sb, ps, sem = stage(nc, "mtab")
    with ctx:
        norm = Norm(K, sb, ps, sem)
        frow = [sb(f"frow{b}", [RT, D]) for b in range(2)]
        low = sb("low", [RT, D])
        expk = sb("expk", [RT, D])
        kk = [sb(f"kk{u}", [RT, D]) for u in range(UN)]
        vv = [sb(f"vv{u}", [RT, D]) for u in range(UN)]
        blocks = sb("blocks", [P, P])
        headcol = sb("headcol", [P, KC, H])
        zero = sb("zero", [P, KC * (P + 1)])
        ksum = sb("ksum", [P, KC])
        psK = [ps(f"psK{u}") for u in range(UN)]
        psS = ps("psS")
        consts = sem("consts")
        frow_ready = sem("frow_ready")
        f_out = [sem(f"f_out{b}") for b in range(2)]
        xn_kept = sem("xn_kept")
        xt_kept = sem("xt_kept")
        kv_done = sem("kv_done")
        low_ready = sem("low_ready")
        exp_ready = sem("exp_ready")
        kk_ready = sem("kk_ready")
        vv_ready = sem("vv_ready")
        summed = sem("summed")
        step = sem("step")
        block = ctx.enter_context(nc.Block())

        def slot_use(g, u):
            return g * (3 - u % 2) + u // 2

        @block.sync
        def _(sp):
            def body(g, again):
                for u in range(UN):
                    i = g * UN + u
                    sp.wait_ge(frow_ready, i + 1)
                    sp.dma_start(K.f_d[bass.ds(i * RT, RT), :], frow[u % 2][:]).then_inc(f_out[u % 2], 16)

            turns(sp, body)
            for b in range(2):
                sp.wait_ge(f_out[b], 16 * NG * (3 - b))

        @block.gpsimd
        def _(pool):
            pool.memset(blocks[:], 0.0).then_inc(consts, 1)
            pool.memset(headcol[:], 0.0).then_inc(consts, 1)
            pool.memset(zero[:], 0.0).then_inc(consts, 1)
            pool.wait_ge(consts, 3)
            for b in range(P // HD):
                pool.memset(blocks[b * HD:(b + 1) * HD, b * HD:(b + 1) * HD], 1.0).then_inc(consts, 1)
                for c in range(KC):
                    h = c * (P // HD) + b
                    pool.memset(headcol[b * HD:(b + 1) * HD, c, h:h + 1], 1.0).then_inc(consts, 1)
            pool.wait_ge(consts, 3 + (1 + KC) * P // HD)

            def body(g, again):
                for u in range(UN):
                    pool.wait_ge(norm.xn_ready, g * UN + u + 1)
                    pool.tensor_copy(K.xrow[:, bass.ds(g * UN + u, 1), :].rearrange("p o d -> p (o d)"), norm.xn[u][:]
                                     ).then_inc(xn_kept, 1)

            turns(pool, body)

        @block.vector
        def _(dve):
            norm.dve_deviations(dve)

            def normalise(g, i, u, again):
                if again:
                    dve.wait_ge(xn_kept, i - (UN - 1))
                    dve.wait_ge(frow_ready, i - (UN - 1))
                norm.dve_tile(dve, i, u, again)
                dve.wait_ge(norm.xn_ready, i + 1)
                if again or u >= 2:
                    dve.wait_ge(f_out[u % 2], 16 * slot_use(g, u))
                dve.tensor_scalar(frow[u % 2][:], norm.xn[u][:], K.rdeg[:, bass.ds(i, 1)], None, ALU.mult
                                  ).then_inc(frow_ready, 1)

            def values(g, i, u, again):
                dve.wait_ge(kv_done, i + 1)
                if again or u:
                    dve.wait_ge(exp_ready, i)
                dve.tensor_scalar(low[:], psK[u][0:RT, 0:D], 0.0, None, ALU.min).then_inc(low_ready, 1)
                if again:
                    dve.wait_ge(summed, i - (UN - 1))
                dve.tensor_copy(vv[u][:], psK[u][0:RT, D:2 * D]).then_inc(vv_ready, 1)

            def keys(g, i, u, again):
                dve.wait_ge(exp_ready, i + 1)
                dve.scalar_tensor_tensor(out=kk[u][:], in0=psK[u][0:RT, 0:D], scalar=0.0, in1=expk[:],
                                         op0=ALU.max, op1=ALU.add).then_inc(kk_ready, 1)

            staggered(dve, (normalise, 0), (keys, 3), (values, 2))
            dve.wait_ge(summed, NT)
            dve.wait_ge(consts, 3 + (1 + KC) * P // HD)
            for c in range(KC):
                dve.tensor_tensor(K.mkv[:, c, :], psS[:, c * P:(c + 1) * P], blocks[:], ALU.mult).then_inc(step, 1)
            dve.tensor_copy(ksum[:], psS[:, KC * P:KC * P + KC]).then_inc(step, 1)
            dve.wait_ge(step, 3)
            for c in range(KC):
                dve.tensor_scalar(K.mks[:, c, :], headcol[:, c, :], ksum[:, c:c + 1], None, ALU.mult).then_inc(step, 1)

        @block.scalar
        def _(act):
            norm.act_deviations(act)

            def keep_turned(g, i, u, again):
                norm.act_tile(act, i, u, again, kv_done)
                act.activation(K.xt[:, :, bass.ds(i * RT, RT)],
                               norm.psT[u % 2][:, 0:KC * RT].rearrange("p (c n) -> p c n", c=KC), ACT.Copy).then_inc(xt_kept, 1)

            def exponential(g, i, u, again):
                act.wait_ge(low_ready, i + 1)
                if again or u:
                    act.wait_ge(kk_ready, i)
                act.activation(expk[:], low[:], ACT.Exp).then_inc(exp_ready, 1)

            lagged(act, keep_turned, exponential, 2)

        @block.tensor
        def _(pe):
            pe.wait_ge(consts, 3)
            pe.matmul(psS[:, 0:KC * (P + 1)], zero[:, 0:P], zero[:], start=True, stop=False, skip_group_check=True)

            def turn(g, i, u, again):
                norm.pe_turn(pe, i, u, again, xt_kept)

            def key_value(g, i, u, again):
                pe.wait_ge(norm.xt_ready, i + 1)
                if again:
                    pe.wait_ge(kk_ready, i - (UN - 1))
                    pe.wait_ge(vv_ready, i - (UN - 1))
                for c in range(KC):
                    m = pe.matmul(psK[u][0:RT, :], norm.xt[u][:, c, :], K.wqkv_t[:, c, D:3 * D], start=c == 0, stop=c == KC - 1)
                m.then_inc(kv_done, 1)

            def accumulate(g, i, u, again):
                last = isinstance(i, int) and i == NT - 1
                pe.wait_ge(kk_ready, i + 1)
                pe.wait_ge(vv_ready, i + 1)
                for c in range(KC):
                    kc = kk[u][:, c * P:(c + 1) * P]
                    pe.matmul(psS[:, c * P:(c + 1) * P], kc, vv[u][:, c * P:(c + 1) * P], start=False, stop=False,
                              skip_group_check=True)
                    m = pe.matmul(psS[:, KC * P + c:KC * P + c + 1], kc, K.ones[0:RT, 0:1], start=False,
                                  stop=last and c == KC - 1, skip_group_check=True)
                m.then_inc(summed, 1)

            staggered(pe, (turn, 0), (key_value, 1), (accumulate, 4))


def edge_messages(nc, K, I):
    ctx, sb, ps, sem = stage(nc, "msg")
    with ctx:
        idx = [sb(f"idx{p}", [RT, GT], I32) for p in range(2)]
        fr = [sb(f"fr{p}", [RT, GT, D]) for p in range(2)]
        onehot = [sb(f"onehot{b}", [RT, QT, RT]) for b in range(2)]
        rows = [sb(f"rows{b}", [RT, QT, D]) for b in range(2)]
        gb = sb("gb", [RT, 4, D])
        b1 = sb("b1", [P, KC])
        b2 = sb("b2", [1, D])
        eps = sb("eps", [RT, 2])
        qlow = sb("qlow", [P, KC, RT])
        qexp = sb("qexp", [P, KC, RT])
        qe = sb("qe", [P, KC, RT])
        den = sb("den", [RT, H])
        rden = sb("rden", [RT, H])
        t1 = sb("t1", [RT, D])
        t2 = sb("t2", [RT, D])
        x1 = sb("x1", [RT, D])
        x1t = sb("x1t", [P, KC, RT])
        mh = sb("mh", [P, KC, RT])
        t3 = sb("t3", [RT, D])
        st = sb("st", [RT, 6])
        mv = sb("mv", [RT, 2])
        dev = sb("dev", [RT, 1])
        rdev = sb("rdev", [RT, 1])
        ps_o = [ps(f"ps_o{b}") for b in range(4)]
        ps_m = ps("ps_m")
        w_in = sem("w_in")
        idx_ready = sem("idx_ready")
        rows_in = [[sem(f"rows_in{p}{q}", kept=K.kept) for q in range(NQ)] for p in range(2)]
        hot_ready = sem("hot_ready")
        out_done = sem("out_done")
        row_ready = sem("row_ready")
        rows_out = [sem(f"rows_out{b}") for b in range(2)]
        mix_mm = sem("mix_mm")
        mix_act = sem("mix_act")
        mix_dve = sem("mix_dve")
        MM, MA, MD = 5, 6, 20
        W_IN = 16 * (4 + KC + 1) + 1
        block = ctx.enter_context(nc.Block())
        TURNS = EG // 2

        def both(eng, turn):
            turn(0, False)
            with eng.Fori(1, TURNS) as it:
                turn(it, True)

        @block.sync
        def _(sp):
            for k, name in enumerate(("L1_mix_ln1_g", "L1_mix_ln1_b", "L1_mix_ln2_g", "L1_mix_ln2_b")):
                sp.dma_start(gb[:, k, :], bcast_row(I[name], RT)).then_inc(w_in, 16)
            load_cols(sp, b1[:], I["L1_mix_b1"], w_in)
            sp.dma_start(b2[:], I["L1_mix_b2"].rearrange("(o n) -> o n", o=1)).then_inc(w_in, 16)

            def turn(it, again):
                for p in range(2):
                    for q in range(NQ):
                        Q = (it * 2 + p) * NQ + q
                        sp.wait_ge(row_ready, QT * (Q + 1))
                        sp.dma_start(K.part1_d[bass.ds(Q * QT * RT, QT * RT), :].rearrange("(t j) f -> j t f", j=RT),
                                     rows[q % 2][:]).then_inc(rows_out[q % 2], 16)

            both(sp, turn)
            for b in range(2):
                sp.wait_ge(rows_out[b], 16 * EG * NQ // 2)

        @block.gpsimd
        def _(pool):
            def turn(it, again):
                for p in range(2):
                    G = it * 2 + p
                    pool.wait_ge(idx_ready, G + 1)
                    for q in range(NQ):
                        if again:
                            pool.wait_ge(out_done, QT * (NQ * (G - 2) + q + 1))
                        pool.nop(nofuse=True)
                        for t in range(q * QT, (q + 1) * QT):
                            pool.indirect_dma_start(fr[p][:, t, :], None, K.f_d,
                                                    bass.IndirectOffsetOnAxis(ap=idx[p][:, t:t + 1], axis=0)
                                                    ).then_inc(rows_in[p][q], 16)

            both(pool, turn)

        @block.vector
        def _(dve):
            dve.memset(eps[:], EPS).then_inc(w_in, 1)

            def indices(G, p):
                dve.tensor_copy(idx[p][:], K.src_t[:, bass.ds(G * GT, GT)]).then_inc(idx_ready, 1)

            def onehots(Q, p, q, again):
                if again or p or q >= 2:
                    dve.wait_ge(out_done, QT * (Q - 1))
                dve.tensor_tensor(onehot[q % 2][:], K.col[0:RT, 0:RT].unsqueeze(1).to_broadcast([RT, QT, RT]),
                                  K.seg_t[:, bass.ds(Q * QT, QT)].unsqueeze(2).to_broadcast([RT, QT, RT]),
                                  ALU.is_equal).then_inc(hot_ready, 1)

            def turn(it, again):
                if not again:
                    indices(0, 0)
                    indices(1, 1)
                    dve.wait_ge(w_in, W_IN)
                n = 0

                def then(ins):
                    nonlocal n
                    n += 1
                    ins.then_inc(mix_dve, 1)
                    dve.wait_ge(mix_dve, MD * it + n)

                def layernorm(src, out, gain, act_step):
                    then(dve.bn_stats(st[:], src))
                    dve.nop(nofuse=True)
                    then(dve.bn_aggr(mv[:], st[:]))
                    dve.wait_ge(mix_act, MA * it + act_step)
                    then(dve.reciprocal(rdev[:], dev[:]))
                    then(dve.tensor_scalar(t1[:], src, mv[:, 0:1], rdev[:], ALU.subtract, ALU.mult))
                    then(dve.tensor_tensor(t1[:], t1[:], gb[:, gain, :], ALU.mult))
                    then(dve.tensor_tensor(out, t1[:], gb[:, gain + 1, :], ALU.add))

                xi = K.xrow[:, bass.ds(it, 1), :].rearrange("p o d -> p (o d)")

                def piece(k):
                    if k == 0:
                        dve.wait_ge(mix_mm, MM * it + 1)
                        pq = ps_m[:, 0:KC * RT].rearrange("p (c n) -> p c n", c=KC)
                        then(dve.tensor_scalar(qlow[:], pq, 0.0, None, ALU.min))
                        dve.wait_ge(mix_act, MA * it + 1)
                        then(dve.scalar_tensor_tensor(out=qe[:], in0=pq, scalar=0.0, in1=qexp[:], op0=ALU.max, op1=ALU.add))
                    if k == 1:
                        dve.wait_ge(mix_mm, MM * it + 2)
                        then(dve.tensor_scalar(den[:], ps_m[0:RT, D:D + H], 1e-6, None, ALU.add))
                        then(dve.reciprocal(rden[:], den[:]))
                        then(dve.tensor_tensor(t1[:].rearrange("p (h d) -> p h d", h=H),
                                               ps_m[0:RT, 0:D].rearrange("p (h d) -> p h d", h=H),
                                               rden[:].unsqueeze(2).to_broadcast([RT, H, HD]), ALU.mult))
                        then(dve.tensor_tensor(t2[:], t1[:], xi, ALU.add))
                    if k == 2:
                        layernorm(t2[:], x1[:], 0, 2)
                    if k == 6:
                        dve.wait_ge(mix_mm, MM * it + 5)
                        then(dve.tensor_tensor(t3[:], ps_m[0:RT, 0:D], x1[:], ALU.add))
                        layernorm(t3[:], t2[:], 2, 6)
                        xo = K.x[:, bass.ds(it, 1), :].rearrange("p o d -> p (o d)")
                        then(dve.tensor_tensor(xo, xo, t2[:], ALU.add))

                for p in range(2):
                    G = it * 2 + p
                    for q in range(NQ):
                        onehots(G * NQ + q, p, q, again)
                        piece(p * NQ + q)
                    for q in range(NQ):
                        dve.wait_ge(rows_in[p][q], QT * 16 * (it + 1))
                    indices(G + 2, p)
                assert n == MD, n

            both(dve, turn)

        @block.scalar
        def _(act):
            act.wait_ge(w_in, W_IN)

            def turn(it, again):
                def piece(k):
                    if k == 0:
                        act.wait_ge(mix_dve, MD * it + 1)
                        act.activation(qexp[:], qlow[:], ACT.Exp).then_inc(mix_act, 1)
                    if k == 2:
                        act.wait_ge(mix_dve, MD * it + 8)
                        act.activation(dev[:], mv[:, 1:2], ACT.Sqrt, bias=eps[:, 0:1]).then_inc(mix_act, 1)
                    if k == 4:
                        act.wait_ge(mix_mm, MM * it + 3)
                        act.activation(x1t[:], ps_m[:, 0:KC * RT].rearrange("p (c n) -> p c n", c=KC), ACT.Copy).then_inc(mix_act, 1)
                    if k == 5:
                        act.wait_ge(mix_mm, MM * it + 4)
                        for c in range(KC):
                            act.activation(mh[:, c, :], ps_m[:, c * RT:(c + 1) * RT], ACT.Gelu, bias=b1[:, c:c + 1]).then_inc(mix_act, 1)
                    if k == 7:
                        act.wait_ge(mix_dve, MD * it + 15)
                        act.activation(dev[:], mv[:, 1:2], ACT.Sqrt, bias=eps[:, 1:2]).then_inc(mix_act, 1)

                for p in range(2):
                    G = it * 2 + p
                    for q in range(NQ):
                        piece(p * NQ + q)
                        for t in range(QT):
                            T = (G * NQ + q) * QT + t
                            if t == 0 and (again or p or q >= 2):
                                act.wait_ge(rows_out[q % 2], 16 * (2 * G + q // 2))
                            act.wait_ge(out_done, T + 1)
                            act.activation(rows[q % 2][:, t, :], ps_o[t][0:RT, 0:D], ACT.Copy).then_inc(row_ready, 1)

            both(act, turn)

        @block.tensor
        def _(pe):
            pe.wait_ge(w_in, W_IN)

            def turn(it, again):
                def piece(k):
                    if k == 0:
                        if again:
                            pe.wait_ge(mix_dve, MD * it)
                        for co in range(KC):
                            for c in range(KC):
                                m = pe.matmul(ps_m[:, co * RT:(co + 1) * RT], K.wqkv_t[:, c, co * P:(co + 1) * P],
                                              K.xt[:, c, bass.ds(it * RT, RT)], start=c == 0, stop=c == KC - 1)
                        m.then_inc(mix_mm, 1)
                    if k == 1:
                        pe.wait_ge(mix_dve, MD * it + 2)
                        for c in range(KC):
                            pe.matmul(ps_m[0:RT, c * P:(c + 1) * P], qe[:, c, :], K.mkv[:, c, :], start=True, stop=True)
                        for c in range(KC):
                            m = pe.matmul(ps_m[0:RT, D:D + H], qe[:, c, :], K.mks[:, c, :], start=c == 0, stop=c == KC - 1)
                        m.then_inc(mix_mm, 1)
                    if k == 4:
                        pe.wait_ge(mix_dve, MD * it + 12)
                        for c in range(KC):
                            m = pe.transpose(ps_m[:, c * RT:(c + 1) * RT], x1[:, c * P:(c + 1) * P], K.ident[0:RT, 0:RT])
                        m.then_inc(mix_mm, 1)
                    if k == 5:
                        pe.wait_ge(mix_act, MA * it + 3)
                        for co in range(KC):
                            for c in range(KC):
                                m = pe.matmul(ps_m[:, co * RT:(co + 1) * RT], K.w1_t[:, c, co * P:(co + 1) * P], x1t[:, c, :],
                                              start=c == 0, stop=c == KC - 1)
                        m.then_inc(mix_mm, 1)
                    if k == 6:
                        pe.wait_ge(mix_act, MA * it + 5)
                        pe.matmul(ps_m[0:RT, 0:D], K.ones[0:1, 0:RT], b2[:], start=True, stop=False)
                        for c in range(KC):
                            m = pe.matmul(ps_m[0:RT, 0:D], mh[:, c, :], K.w2_t[:, c, :], start=False, stop=c == KC - 1)
                        m.then_inc(mix_mm, 1)

                for p in range(2):
                    G = it * 2 + p
                    for q in range(NQ):
                        Q = G * NQ + q
                        piece(p * NQ + q)
                        pe.wait_ge(hot_ready, Q + 1)
                        pe.wait_ge(rows_in[p][q], QT * 16 * (it + 1))
                        for t in range(QT):
                            if again or p or q:
                                pe.wait_ge(row_ready, Q * QT + t - 3)
                            pe.matmul(ps_o[t][0:RT, 0:D], onehot[q % 2][:, t, :], fr[p][:, q * QT + t, :],
                                      start=True, stop=True).then_inc(out_done, 1)

            both(pe, turn)


def join_messages(nc, K, I):
    ctx, sb, ps, sem = stage(nc, "mjoin")
    with ctx:
        w1 = sb("w1", [P, KC, D])
        w2 = sb("w2", [P, KC, D])
        b = sb("b", [1, D])
        edge0 = sb("edge0", [EP, EK, D])
        dsh = sb("dsh", [EP, EK])
        hot = [sb(f"hot{u}", [EP, EK, RT]) for u in range(UN)]
        row = [sb(f"row{u}", [RT, D]) for u in range(UN)]
        idx = sb("idx", [RT, UN], I32)
        hrd = sb("hrd", [RT, NT])
        own = sb("own", [RT, D])
        sums = sb("sums", [RT, D])
        part = sb("part", [RT, D])
        ab = [sb(f"ab{k}", [RT, D]) for k in range(2)]
        abt = sb("abt", [P, 2 * KC, RT])
        emb = sb("emb", [RT, D])
        emb2 = sb("emb2", [RT, D])
        sqr = sb("sqr", [RT, D])
        nn = sb("nn", [RT, 1])
        nrm = sb("nrm", [RT, 1])
        nrc = sb("nrc", [RT, 1])
        rn = sb("rn", [RT, 1])
        psJ = [ps(f"psJ{u}") for u in range(UN)]
        psT = ps("psT")
        psE = ps("psE")
        w_in = sem("w_in")
        idx_ready = sem("idx_ready")
        row_in = [sem(f"row_in{u}", kept=K.kept) for u in range(UN)]
        joined = sem("joined")
        hot_ready = sem("hot_ready")
        ab_ready = sem("ab_ready")
        step = sem("step")
        turned = sem("turned")
        abt_ready = sem("abt_ready")
        emb_done = sem("emb_done")
        hrd_ready = sem("hrd_ready")
        nrm_ready = sem("nrm_ready")
        block = ctx.enter_context(nc.Block())

        @block.sync
        def _(sp):
            load_chunks(sp, w1[:], I["L1_gnn_W1"], w_in)
            load_chunks(sp, w2[:], I["L1_gnn_W2"], w_in)
            sp.dma_start(b[:], I["L1_gnn_b"].rearrange("(o n) -> o n", o=1)).then_inc(w_in, 16)
            sp.dma_start(edge0[:], K.part1_d.rearrange("(p k j) f -> p k j f", p=EP, j=RT)[:, :, 0, :]).then_inc(w_in, 16)

        @block.gpsimd
        def _(pool):
            def body(g, again):
                pool.wait_ge(idx_ready, g + 1)
                for u in range(UN):
                    if again:
                        pool.wait_ge(ab_ready, 5 * ((g - 1) * UN + u + 1))
                    if again or u == 0:
                        pool.nop(nofuse=True)
                    pool.indirect_dma_start(row[u][:], None, K.part1_d, bass.IndirectOffsetOnAxis(ap=idx[:, u:u + 1], axis=0)
                                            ).then_inc(row_in[u], 16)

            turns(pool, body)

        @block.vector
        def _(dve):
            dve.tensor_tensor(hrd[:], K.has[:], K.rdeg[:], ALU.mult).then_inc(hrd_ready, 1)
            dve.wait_ge(hrd_ready, 1)

            def owners(g, i, u, again):
                if again or u:
                    dve.wait_ge(hot_ready, 2 * i)
                dve.tensor_scalar(dsh[:], K.dfirst[:], K.tilebase[0:EP, bass.ds(i, 1)], None, ALU.subtract).then_inc(hot_ready, 1)
                dve.wait_ge(hot_ready, 2 * i + 1)
                if again:
                    dve.wait_ge(joined, i - (UN - 1))
                dve.tensor_tensor(hot[u][:], K.col[0:EP, 0:RT].unsqueeze(1).to_broadcast([EP, EK, RT]),
                                  dsh[:].unsqueeze(2).to_broadcast([EP, EK, RT]), ALU.is_equal).then_inc(hot_ready, 1)

            def operands(g, i, u, again):
                xi = K.xrow[:, bass.ds(i, 1), :].rearrange("p o d -> p (o d)")
                dve.tensor_scalar(own[:], xi, K.has[:, bass.ds(i, 1)], None, ALU.mult).then_inc(ab_ready, 1)
                dve.wait_ge(row_in[u], 16 * (g + 1))
                dve.wait_ge(joined, i + 1)
                dve.tensor_tensor(sums[:], row[u][:], psJ[u][0:RT, 0:D], ALU.add).then_inc(ab_ready, 1)
                dve.wait_ge(ab_ready, 5 * i + 2)
                dve.tensor_scalar(part[:], sums[:], hrd[:, bass.ds(i, 1)], None, ALU.mult).then_inc(ab_ready, 1)
                dve.wait_ge(ab_ready, 5 * i + 3)
                if again or u:
                    dve.wait_ge(turned, i)
                dve.tensor_tensor(ab[0][:], own[:], part[:], ALU.add).then_inc(ab_ready, 1)
                dve.tensor_tensor(ab[1][:], own[:], part[:], ALU.mult).then_inc(ab_ready, 1)

            def embed(g, i, u, again):
                dve.wait_ge(emb_done, i + 1)
                dve.tensor_copy(emb[:], psE[0:RT, 0:D]).then_inc(step, 1)
                dve.wait_ge(step, 5 * i + 1)
                dve.scalar_tensor_tensor(out=emb2[:], in0=emb[:], scalar=0.01, in1=emb[:], op0=ALU.mult, op1=ALU.max
                                         ).then_inc(step, 1)
                dve.wait_ge(nrm_ready, 2 * i + 2)
                dve.tensor_scalar(nrc[:], nrm[:], 1e-12, None, ALU.max).then_inc(step, 1)
                dve.wait_ge(step, 5 * i + 3)
                dve.reciprocal(rn[:], nrc[:]).then_inc(step, 1)
                dve.wait_ge(step, 5 * i + 4)
                xo = K.x[:, bass.ds(i, 1), :].rearrange("p o d -> p (o d)")
                dve.scalar_tensor_tensor(out=xo, in0=emb2[:], scalar=rn[:], in1=xo, op0=ALU.mult, op1=ALU.add).then_inc(step, 1)

            def indices(g, i, u, again):
                if u == 0:
                    if again:
                        for v in range(UN):
                            dve.wait_ge(row_in[v], 16 * g)
                    dve.tensor_copy(idx[:], K.start[:, bass.ds(g * UN, UN)]).then_inc(idx_ready, 1)

            staggered(dve, (indices, 0), (operands, 3), (owners, 0), (embed, 4))

        @block.scalar
        def _(act):
            def body(g, again):
                for u in range(UN):
                    i = g * UN + u
                    act.wait_ge(turned, i + 1)
                    if again or u:
                        act.wait_ge(emb_done, i)
                    act.activation(abt[:], psT[:, 0:2 * KC * RT].rearrange("p (c n) -> p c n", c=2 * KC), ACT.Copy).then_inc(abt_ready, 1)
                    act.wait_ge(step, 5 * i + 2)
                    act.activation(sqr[:], emb2[:], ACT.Square, accum_out=nn[:]).then_inc(nrm_ready, 1)
                    act.wait_ge(nrm_ready, 2 * i + 1)
                    act.activation(nrm[:], nn[:], ACT.Sqrt).then_inc(nrm_ready, 1)

            turns(act, body)

        @block.tensor
        def _(pe):
            pe.wait_ge(w_in, 64)

            def join(g, i, u, again):
                pe.wait_ge(hot_ready, 2 * i + 2)
                if again:
                    pe.wait_ge(ab_ready, 5 * (i - (UN - 1)))
                for k in range(EK):
                    m = pe.matmul(psJ[u][0:RT, 0:D], hot[u][:, k, :], edge0[:, k, :], start=k == 0, stop=k == EK - 1)
                m.then_inc(joined, 1)

            def turn(g, i, u, again):
                pe.wait_ge(ab_ready, 5 * i + 5)
                if again or u:
                    pe.wait_ge(abt_ready, i)
                for k in range(2):
                    for c in range(KC):
                        t = pe.transpose(psT[:, (KC * k + c) * RT:(KC * k + c + 1) * RT], ab[k][:, c * P:(c + 1) * P],
                                         K.ident[0:RT, 0:RT])
                t.then_inc(turned, 1)

            def products(g, i, u, again):
                pe.wait_ge(abt_ready, i + 1)
                if again or u:
                    pe.wait_ge(step, 5 * i - 4)
                pe.matmul(psE[0:RT, 0:D], K.ones[0:1, 0:RT], b[:], start=True, stop=False)
                for k, w in enumerate((w1, w2)):
                    for c in range(KC):
                        m = pe.matmul(psE[0:RT, 0:D], abt[:, KC * k + c, :], w[:, c, :], start=False,
                                      stop=k == 1 and c == KC - 1)
                m.then_inc(emb_done, 1)

            staggered(pe, (turn, 3), (join, 1), (products, 3))


def route_topk(nc, K, I):
    ctx, sb, ps, sem = stage(nc, "topk")
    with ctx:
        wr = sb("wr", [P, KC])
        br = sb("br", [1, 1])
        zero = sb("zero", [TKR, 2 * UT, D])
        xall = sb("xall", [RT, NT, D])
        wall = sb("wall", [RT, N])
        before = sb("before", [RT, RT], BF16)
        junk = sb("junk", [RT, N], BF16)
        part = sb("part", [RT, 3, NT])
        rank = sb("rank", [RT, NT])
        late = sb("late", [RT, NT])
        place = sb("place", [RT, NT], I32)
        psW = [ps(f"psW{b}") for b in range(2)]
        norm = Norm(K, sb, ps, sem)
        w_in = sem("w_in")
        consts = sem("consts")
        kept_rows = sem("kept_rows")
        summed = sem("summed")
        w_done = sem("w_done")
        w_ready = sem("w_ready")
        w_out = sem("w_out")
        wall_in = sem("wall_in")
        counted = sem("counted")
        step = sem("step")
        zeroed = sem("zeroed")
        placed = sem("placed", kept=K.kept)
        block = ctx.enter_context(nc.Block())

        @block.sync
        def _(sp):
            load_cols(sp, wr[:], I["L1_ffn_wr"].rearrange("n o -> (n o)"), w_in)
            sp.dma_start(br[:], I["L1_ffn_br"].rearrange("(o n) -> o n", o=1)).then_inc(w_in, 16)
            sp.wait_ge(consts, 1)
            for h in range(2):
                sp.dma_start(K.tbuf_d[h * 2 * UT * TKR:(h + 1) * 2 * UT * TKR, :].rearrange("(t p) d -> p t d", p=TKR),
                             zero[:]).then_inc(zeroed, 16)
            sp.wait_ge(w_ready, NT)
            for i in range(NT):
                sp.dma_start(K.w_d[i * RT:(i + 1) * RT].rearrange("(p o) -> p o", o=1), K.weight[:, i:i + 1]).then_inc(w_out, 16)
            sp.wait_ge(w_out, 16 * NT)
            sp.dma_start(wall[:], bcast_row(K.w_d, RT)).then_inc(wall_in, 16)

        @block.gpsimd
        def _(pool):
            pool.memset(zero[:], 0.0).then_inc(consts, 1)
            pool.memset(before[:], 0.0).then_inc(consts, 1)
            pool.memset(part[:], 0.0).then_inc(consts, 1)
            pool.wait_ge(consts, 3)
            pool.affine_select(out=before[:], in_=before[:], compare_op=ALU.is_ge, fill=1.0, base=0,
                               pattern=[[1, RT]], channel_multiplier=-1).then_inc(consts, 1)

            def body(g, again):
                for u in range(UN):
                    pool.wait_ge(norm.xn_ready, g * UN + u + 1)
                    pool.tensor_copy(xall[:, bass.ds(g * UN + u, 1), :].rearrange("p o d -> p (o d)"), norm.xn[u][:]
                                     ).then_inc(kept_rows, 1)

            turns(pool, body)
            pool.wait_ge(kept_rows, NT)
            pool.tensor_tensor(K.x[:], K.x[:], xall[:], ALU.add).then_inc(summed, 1)
            pool.wait_ge(zeroed, 32)
            for i in range(NT):
                if i % UN == 0:
                    pool.wait_ge(step, 5 * (i // UN) + 4)
                pool.indirect_dma_start(K.tbuf_d, bass.IndirectOffsetOnAxis(ap=place[:, i:i + 1], axis=0), xall[:, i, :], None,
                                        bounds_check=TOPK - 1, oob_is_err=False).then_inc(placed, 16)
            pool.wait_ge(placed, 16 * NT)

        @block.vector
        def _(dve):
            norm.dve_deviations(dve)

            def normalise(g, i, u, again):
                if again:
                    dve.wait_ge(kept_rows, i - (UN - 1))
                norm.dve_tile(dve, i, u, again)

            def keep_weights(g, i, u, again):
                dve.wait_ge(w_done, i + 1)
                dve.tensor_copy(K.weight[:, bass.ds(i, 1)], psW[u % 2][0:RT, 0:1]).then_inc(w_ready, 1)

            lagged(dve, normalise, keep_weights, 2)
            dve.wait_ge(w_ready, NT)
            dve.wait_ge(wall_in, 16)
            dve.wait_ge(consts, 4)

            n = 0
            for i in range(NT):
                w = K.weight[:, i:i + 1]
                lo, hi = i * RT, (i + 1) * RT
                for k, (a, z, op) in enumerate(((0, lo, ALU.is_ge), (lo, N, ALU.is_gt))):
                    if z > a:
                        if n:
                            dve.wait_ge(counted, n)
                        dve.tensor_scalar(junk[:, 0:z - a], wall[:, a:z], w, 0.0, op, ALU.add,
                                          accum_out=part[:, k, i:i + 1]).then_inc(counted, 1)
                        n += 1
                dve.wait_ge(counted, n)
                dve.scalar_tensor_tensor(out=junk[:, 0:RT], in0=wall[:, lo:hi], scalar=w, in1=before[:],
                                         op0=ALU.is_equal, op1=ALU.mult, accum_out=part[:, 2, i:i + 1]).then_inc(counted, 1)
                n += 1
                if i % UN < UN - 1:
                    continue
                g = i // UN
                own = slice(g * UN, (g + 1) * UN)
                dve.wait_ge(counted, n)
                dve.tensor_reduce(rank[:, own], part[:, :, own].rearrange("p k i -> p i k"), AX_X, ALU.add).then_inc(step, 1)
                dve.wait_ge(step, 5 * g + 1)
                dve.tensor_scalar(late[:, own], rank[:, own], float(TOPK), None, ALU.is_ge).then_inc(step, 1)
                dve.wait_ge(step, 5 * g + 2)
                dve.scalar_tensor_tensor(out=late[:, own], in0=late[:, own], scalar=float(N), in1=rank[:, own],
                                         op0=ALU.mult, op1=ALU.add).then_inc(step, 1)
                dve.wait_ge(step, 5 * g + 3)
                dve.tensor_copy(place[:, own], late[:, own]).then_inc(step, 1)
                dve.tensor_copy(K.slot[:, own], late[:, own]).then_inc(step, 1)

        @block.scalar
        def _(act):
            norm.act_deviations(act)

            def body(g, again):
                for u in range(UN):
                    norm.act_tile(act, g * UN + u, u, again, w_done)

            turns(act, body)

        @block.tensor
        def _(pe):
            pe.wait_ge(w_in, 48)

            def weights(g, i, u, again):
                pe.wait_ge(norm.xt_ready, i + 1)
                if again or u >= 2:
                    pe.wait_ge(w_ready, slot_tiles(i, u))
                W = psW[u % 2][0:RT, 0:1]
                pe.matmul(W, K.ones[0:1, 0:RT], br[:], start=True, stop=False)
                for c in range(KC):
                    m = pe.matmul(W, norm.xt[u][:, c, :], wr[:, c:c + 1], start=False, stop=c == KC - 1)
                m.then_inc(w_done, 1)

            lagged(pe, lambda g, i, u, again: norm.pe_turn(pe, i, u, again), weights, 1)


def take_topk(nc, K, out):
    ctx, sb, ps, sem = stage(nc, "last")
    with ctx:
        row = sb("row", [RT, NT, D])
        cleared = sem("cleared")
        row_in = [sem(f"row_in{g}", kept=K.kept) for g in range(NG)]
        res_ready = sem("res_ready")
        res_out = sem("res_out")
        block = ctx.enter_context(nc.Block())

        @block.gpsimd
        def _(pool):
            for i in range(NT):
                if i % UN == 0:
                    pool.wait_ge(cleared, i // UN + 1)
                pool.indirect_dma_start(row[:, i, :], None, K.ty_d, bass.IndirectOffsetOnAxis(ap=K.slot[:, i:i + 1], axis=0),
                                        bounds_check=TOPK - 1, oob_is_err=False).then_inc(row_in[i // UN], 16)

        @block.vector
        def _(dve):
            for g in range(NG):
                dve.memset(row[:, g * UN:(g + 1) * UN, :], 0.0).then_inc(cleared, 1)
            for i in range(NT):
                if i % UN == 0:
                    dve.wait_ge(row_in[i // UN], 16 * UN)
                dve.scalar_tensor_tensor(out=row[:, i, :], in0=row[:, i, :], scalar=K.weight[:, i:i + 1], in1=K.x[:, i, :],
                                         op0=ALU.mult, op1=ALU.add).then_inc(res_ready, 1)

        @block.sync
        def _(sp):
            for g in range(NG):
                sp.wait_ge(res_ready, UN * (g + 1))
                sp.dma_start(out[g * UN * RT:(g + 1) * UN * RT, :].rearrange("(t p) d -> p t d", p=RT),
                             row[:, g * UN:(g + 1) * UN, :]).then_inc(res_out, 16)
            sp.wait_ge(res_out, 16 * NG)


def layer0_experts(nc, K, I):
    route_experts(nc, K, I)
    networks(nc, K, "ffn0", EXPERTS, RT,
             lambda e: tuple(I[w][bass.ds(e, 1)].rearrange("o a b -> (o a) b") for w in ("L0_ffn_w1", "L0_ffn_w2")),
             I["L0_ffn_b1"].rearrange("e (c p) -> (e c) p", p=P), I["L0_ffn_b2"].rearrange("(o e) d -> o (e d)", o=1),
             ACT.Relu, K.ebuf_d, K.ey_d)
    take_experts(nc, K)


def program(nc, I, out):
    ctx = ExitStack()
    with ctx:
        def sb(name, shape, dt=F32):
            return ctx.enter_context(nc.sbuf_tensor(f"all_{name}", shape, dt))

        def dram(name, shape, dt=F32):
            return nc.dram_tensor(f"scratch_{name}", shape, dt).ap()

        K = Kept(ctx)
        K.x = sb("x", [RT, NT, D])
        K.ident = sb("ident", [P, P])
        K.tri = sb("tri", [P, P])
        K.ones = sb("ones", [P, P])
        K.col = sb("col", [P, P])
        K.colb = sb("colb", [P, P], BF16)
        K.row_i = sb("row_i", [P, 1], I32)
        K.rowf = sb("rowf", [P, 1])
        K.src_t = sb("src_t", [RT, ET + 2 * GT], I32)
        K.dst_t = sb("dst_t", [RT, ET + 2 * GT], I32)
        K.hist = sb("hist", [RT, 2, NT])
        K.mfirst = sb("mfirst", [P, EG])
        K.mlast = sb("mlast", [P, EG])
        K.part_d = dram("part", [E, RW])
        K.ef = I["edge_attr_64"]
        K.has = sb("has", [RT, NT])
        K.start = sb("start", [RT, NT], I32)
        K.rdeg = sb("rdeg", [RT, NT])
        K.join = sb("join", [EP, EK, 2 * H + 1])
        K.tilebase = sb("tilebase", [P, NT])
        K.prob = sb("prob", [RT, NT])
        K.slot = sb("slot", [RT, NT], I32)
        K.ebuf_d = dram("ebuf", [EXPERTS * CAPR, D])
        K.ey_d = dram("ey", [EXPERTS * CAPR, D])
        K.f_d = dram("f", [N, D])
        K.part1_d = dram("part1", [E, D])
        K.tbuf_d = dram("tbuf", [UT * TU * TKR, D])
        K.ty_d = dram("ty", [UT * TU * TKR, D])
        K.w_d = dram("w", [N])
        K.mks = sb("mks", [P, KC, H])
        K.weight = sb("weight", [RT, NT])
        K.mfirst_d = dram("mfirst", [P, EG])
        K.mlast_d = dram("mlast", [P, EG])
        K.seg_t = sb("seg_t", [RT, ET], BF16)
        K.src_hi, K.src_lo, K.dst_hi, K.dst_lo = (sb(n, [RT, ET], BF16) for n in ("shi", "slo", "dhi", "dlo"))
        K.cont = sb("cont", [EP, EK])
        K.single = sb("single", [EP, EK])
        K.dfirst = sb("dfirst", [EP, EK])
        K.xt = sb("xt", [P, KC, N])
        K.mkv = sb("mkv", [P, KC, P])
        K.kv_d = dram("kv", [N, 2 * D])
        K.q_d = dram("q", [N, D])
        K.neg_d = dram("neg", [ET, RT + 1])
        K.cont_d = dram("cont", [ET])
        K.single_d = dram("single", [ET])
        prepare(nc, K, I)
        node_tables(nc, K, I)
        edge_attention(nc, K, I)
        run_starts(nc, K)
        run_scales(nc, K)
        join_attention(nc, K, I)
        layer0_experts(nc, K, I)
        K.wqkv_t = sb("wqkv_t", [P, KC, 3 * D])
        K.w1_t = sb("w1_t", [P, KC, D])
        K.w2_t = sb("w2_t", [P, KC, D])
        K.xrow = sb("xrow", [RT, NT, D])
        turn_weights(nc, K, I)
        message_tables(nc, K, I)
        edge_messages(nc, K, I)
        join_messages(nc, K, I)
        route_topk(nc, K, I)
        networks(nc, K, "ffn1", TU, TKR, (I["L1_ffn_w1"], I["L1_ffn_w2"]),
                 I["L1_ffn_b1"].rearrange("(c p) -> c p", p=P), I["L1_ffn_b2"].rearrange("(o d) -> o d", o=1),
                 ACT.Gelu_apprx_tanh, K.tbuf_d, K.ty_d)
        take_topk(nc, K, out)


_OUT = ((N, D), "float32")
_INS = ["x", "src", "dst", "edge_attr_64", "L0_gnn_Wq", "L0_gnn_Wk", "L0_gnn_Wv", "L0_gnn_W1", "L0_gnn_b1", "L0_gnn_W2",
        "L0_gnn_b2", "L0_gnn_Wo", "L0_gnn_bo", "L0_mix_w_qkv", "L0_mix_b_qkv", "L0_mix_kln_g", "L0_mix_kln_b",
        "L0_mix_vln_g", "L0_mix_vln_b", "L0_mix_w1", "L0_mix_b1", "L0_mix_w2", "L0_mix_b2", "L0_ffn_gate_w",
        "L0_ffn_gate_b", "L0_ffn_w1", "L0_ffn_b1", "L0_ffn_w2", "L0_ffn_b2", "L1_gnn_W1", "L1_gnn_W2", "L1_gnn_b",
        "L1_mix_Wqkv", "L1_mix_ln1_g", "L1_mix_ln1_b", "L1_mix_W1", "L1_mix_b1", "L1_mix_W2", "L1_mix_b2",
        "L1_mix_ln2_g", "L1_mix_ln2_b", "L1_ffn_wr", "L1_ffn_br", "L1_ffn_w1", "L1_ffn_b1", "L1_ffn_w2", "L1_ffn_b2"]


def kernel(**inputs):
    import numpy as _np
    import concourse.bacc as _bacc
    from concourse import mybir as _mybir
    from concourse.bass_utils import run_bass_kernel_spmd as _run

    nc = _bacc.Bacc("TRN2", target_bir_lowering=False, num_devices=1)
    arrays, args = {}, {}
    for name in _INS:
        a = _np.ascontiguousarray(inputs[name])
        arrays[f"in_{name}_dram"] = a
        args[name] = nc.dram_tensor(f"in_{name}_dram", a.shape, _mybir.dt.from_np(a.dtype), kind="ExternalInput").ap()
    shape, dtype = _OUT
    out = nc.dram_tensor("out_0_dram", shape, _mybir.dt.from_np(_np.dtype(dtype)), kind="ExternalOutput").ap()
    program(nc, args, out)
    r = _run(nc, [arrays], core_ids=[0])
    return r.results[0]["out_0_dram"]
```
